# Optimizing a Trainium2 kernel written in Bass

```python
import numpy as np
import jax
import jax.numpy as jnp

def _softmax(x, axis=-1):
    return jax.nn.softmax(x, axis=axis)

def _gelu(x):
    return jax.nn.gelu(x, approximate=True)

def _silu(x):
    return jax.nn.silu(x)

def _sigmoid(x):
    return jax.nn.sigmoid(x)

def _layernorm(x, axis=-1, eps=1e-05):
    m = jnp.mean(x, axis=axis, keepdims=True)
    v = jnp.var(x, axis=axis, keepdims=True)
    return (x - m) / jnp.sqrt(v + eps)

def _scatter_add(tgt, idx, src, axis=0):
    return tgt.at[idx].add(src)

def _segment_sum(src, seg, n):
    return jax.ops.segment_sum(src, seg, n)
kernel_name = 'mk_prb_d4_jaxref_r8_532a94'

def setup_inputs(seed: int=0):
    np.random.seed(seed)
    _w = jnp.asarray

    def _L0_attn_setup():
        import jax, jax.numpy as jnp
        import numpy as np
        D_MODEL = 128
        NUM_HEADS = 16
        D_K = D_MODEL // NUM_HEADS
        key = jax.random.key(seed)
        k1, k2, k3, k4, k5 = jax.random.split(key, 5)
        scale = 1.0 / np.sqrt(D_MODEL)
        x = jax.random.normal(k1, (2, 1024, D_MODEL), dtype=jnp.float32)
        W_qkv = jax.random.normal(k2, (D_MODEL, 3 * D_MODEL), dtype=jnp.float32) * scale
        b_qkv = jax.random.normal(k3, (3 * D_MODEL,), dtype=jnp.float32) * 0.01
        W_out = jax.random.normal(k4, (D_MODEL, D_MODEL), dtype=jnp.float32) * scale
        b_out = jax.random.normal(k5, (D_MODEL,), dtype=jnp.float32) * 0.01
        return {'x': x, 'W_qkv': W_qkv, 'b_qkv': b_qkv, 'W_out': W_out, 'b_out': b_out}
    _L0_attn_in = _L0_attn_setup()

    def _L0_ffn_setup():
        import jax, jax.numpy as jnp
        import numpy as np
        DIM = 128
        DEPTH = 2
        HEADS = 8
        DIM_HEAD = 64
        WINDOW = 64
        INNER = HEADS * DIM_HEAD
        HID = int(DIM * 4 * 2 / 3)
        B, N = (2, 1024)
        QK_SCALE = 8.0

        def shift_token(t):
            t1, t2 = jnp.split(t, 2, axis=-1)
            t2 = jnp.pad(t2, ((0, 0), (1, 0), (0, 0)))[:, :-1]
            return jnp.concatenate([t1, t2], axis=-1)

        def l2norm(t):
            return t / jnp.clip(jnp.linalg.norm(t, axis=-1, keepdims=True), 1e-12)

        def rotate_half(x):
            x1, x2 = jnp.split(x, 2, axis=-1)
            return jnp.concatenate([-x2, x1], axis=-1)

        def rotary_xpos(q, k):
            n = q.shape[-2]
            half_idx = jnp.arange(0, DIM_HEAD, 2, dtype=jnp.float32)
            inv_freq = 1.0 / 10000.0 ** (half_idx / DIM_HEAD)
            t = jnp.arange(n, dtype=jnp.float32)
            freqs = t[:, None] * inv_freq[None, :]
            freqs = jnp.concatenate([freqs, freqs], axis=-1)
            base = (half_idx + 0.4 * DIM_HEAD) / (1.4 * DIM_HEAD)
            power = (t - n // 2) / float(WINDOW // 2)
            scale = base[None, :] ** power[:, None]
            scale = jnp.concatenate([scale, scale], axis=-1)
            cos, sin = (jnp.cos(freqs), jnp.sin(freqs))
            q = q * cos * scale + rotate_half(q) * sin * scale
            k = k * cos / scale + rotate_half(k) * sin / scale
            return (q, k)

        def local_attention(q, k, v):
            b, h, n, d = q.shape
            w = n // WINDOW
            bq = q.reshape(b, h, w, WINDOW, d) * QK_SCALE
            bk = k.reshape(b, h, w, WINDOW, d)
            bv = v.reshape(b, h, w, WINDOW, d)

            def look_around(t):
                p = jnp.pad(t, ((0, 0), (0, 0), (1, 0), (0, 0), (0, 0)))
                return jnp.concatenate([p[:, :, :w], p[:, :, 1:]], axis=3)
            bk, bv = (look_around(bk), look_around(bv))
            bt = jnp.arange(n).reshape(w, WINDOW)
            btp = jnp.pad(bt, ((1, 0), (0, 0)), constant_values=-1)
            btk = jnp.concatenate([btp[:w], btp[1:]], axis=1)
            sim = jnp.einsum('bhwid,bhwjd->bhwij', bq, bk)
            i = bt[:, :, None]
            j = btk[:, None, :]
            mask = (i < j) | (i > j + WINDOW) | (j == -1)
            sim = jnp.where(mask, -jnp.finfo(sim.dtype).max, sim)
            attn = jax.nn.softmax(sim, axis=-1)
            out = jnp.einsum('bhwij,bhwjd->bhwid', attn, bv)
            return out.reshape(b, h, n, d)

        def _layer(x, wqkv, qs, ksc, wo, lg, lb, w1, b1, w2, b2):
            b, n, _ = x.shape
            h = shift_token(x)
            qkv = h @ wqkv
            q, k, v = jnp.split(qkv, 3, axis=-1)
            to_heads = lambda t: t.reshape(b, n, HEADS, DIM_HEAD).transpose(0, 2, 1, 3)
            q, k, v = (to_heads(q), to_heads(k), to_heads(v))
            q = l2norm(q) * qs
            k = l2norm(k) * ksc
            q, k = rotary_xpos(q, k)
            o = local_attention(q, k, v)
            o = o.transpose(0, 2, 1, 3).reshape(b, n, INNER)
            x = x + o @ wo
            h = shift_token(x)
            mu = h.mean(-1, keepdims=True)
            var = h.var(-1, keepdims=True)
            h = (h - mu) / jnp.sqrt(var + 1e-05) * lg + lb
            h = h @ w1 + b1
            a, g = jnp.split(h, 2, axis=-1)
            h = a * jax.nn.gelu(g, approximate=False)
            x = x + h @ w2 + b2
            return x
        key = jax.random.key(seed)
        ks = jax.random.split(key, 6)
        return {'x': jax.random.normal(ks[0], (B, N, DIM), jnp.float32), 'wqkv': jax.random.normal(ks[1], (DEPTH, DIM, 3 * INNER), jnp.float32) * 0.02, 'q_scale': jnp.ones((DEPTH, DIM_HEAD), jnp.float32), 'k_scale': jnp.ones((DEPTH, DIM_HEAD), jnp.float32), 'wo': jax.random.normal(ks[2], (DEPTH, INNER, DIM), jnp.float32) * 0.02, 'ln_g': jnp.ones((DEPTH, DIM), jnp.float32), 'ln_b': jnp.zeros((DEPTH, DIM), jnp.float32), 'w1': jax.random.normal(ks[3], (DEPTH, DIM, 2 * HID), jnp.float32) * 0.02, 'b1': jnp.zeros((DEPTH, 2 * HID), jnp.float32), 'w2': jax.random.normal(ks[4], (DEPTH, HID, DIM), jnp.float32) * 0.02, 'b2': jnp.zeros((DEPTH, DIM), jnp.float32)}
    _L0_ffn_in = _L0_ffn_setup()

    def _L1_attn_setup():
        import jax, jax.numpy as jnp
        import numpy as np
        EMB = 128
        HEADS = 16
        ATT = EMB // HEADS
        key = jax.random.key(seed)
        ks = jax.random.split(key, 5)
        s = 1.0 / np.sqrt(EMB)
        return {'x': jax.random.normal(ks[0], (4, 256, EMB), dtype=jnp.float32), 'Wq': jax.random.uniform(ks[1], (EMB, HEADS * ATT), jnp.float32, -s, s), 'Wk': jax.random.uniform(ks[2], (EMB, HEADS * ATT), jnp.float32, -s, s), 'Wv': jax.random.uniform(ks[3], (EMB, HEADS * ATT), jnp.float32, -s, s), 'Wo': jax.random.uniform(ks[4], (HEADS * ATT, EMB), jnp.float32, -s, s)}
    _L1_attn_in = _L1_attn_setup()

    def _L1_ffn_setup():
        import jax, jax.numpy as jnp
        import numpy as np
        E, K, D, H = (8, 2, 128, 256)
        B, S = (1, 128)

        def _grouped_swiglu(x_sorted, counts, w1, w2, w3):
            if hasattr(jax.lax, 'ragged_dot'):
                gs = counts.astype(jnp.int32)
                h = jax.nn.silu(jax.lax.ragged_dot(x_sorted, w1, gs)) * jax.lax.ragged_dot(x_sorted, w3, gs)
                return jax.lax.ragged_dot(h, w2, gs)
            pos = jnp.arange(x_sorted.shape[0])
            eid = jnp.searchsorted(jnp.cumsum(counts), pos, side='right')
            out = jnp.zeros((x_sorted.shape[0], w2.shape[-1]), x_sorted.dtype)
            for e in range(w1.shape[0]):
                xm = jnp.where((eid == e)[:, None], x_sorted, 0.0)
                he = jax.nn.silu(xm @ w1[e]) * (xm @ w3[e])
                out = out + he @ w2[e]
            return out
        key = jax.random.key(seed)
        k0, k1, k2, k3, k4 = jax.random.split(key, 5)
        sD = 1.0 / np.sqrt(D)
        sH = 1.0 / np.sqrt(H)
        return {'hidden_states': jax.random.normal(k0, (B, S, D), jnp.float32), 'gate_w': jax.random.normal(k1, (E, D), jnp.float32) * sD, 'w1': jax.random.normal(k2, (E, D, H), jnp.float32) * sD, 'w2': jax.random.normal(k3, (E, H, D), jnp.float32) * sH, 'w3': jax.random.normal(k4, (E, D, H), jnp.float32) * sD}
    _L1_ffn_in = _L1_ffn_setup()

    def _L2_attn_setup():
        import jax, jax.numpy as jnp
        import numpy as np
        B, T, C = (2, 256, 128)
        NHEADS = 16
        HEAD_DIM = C // NHEADS
        THETA = 10000.0
        SCALE_BASE = 512.0
        GN_EPS = 1e-05

        def _rotate_half(x):
            x1 = x[..., 0::2]
            x2 = x[..., 1::2]
            return jnp.stack([-x2, x1], axis=-1).reshape(x.shape)

        def _rope_xpos(q, k, T):
            d = q.shape[-1]
            half = jnp.arange(0, d, 2, dtype=jnp.float32)
            inv_freq = 1.0 / THETA ** (half / d)
            t = jnp.arange(T, dtype=jnp.float32)
            freqs = t[:, None] * inv_freq[None, :]
            freqs = jnp.repeat(freqs, 2, axis=-1)
            scale_vec = (half + 0.4 * d) / (1.4 * d)
            power = (t - T // 2) / SCALE_BASE
            scale = scale_vec[None, :] ** power[:, None]
            scale = jnp.repeat(scale, 2, axis=-1)
            cos, sin = (jnp.cos(freqs), jnp.sin(freqs))
            q = q * (cos * scale) + _rotate_half(q) * (sin * scale)
            k = k * (cos / scale) + _rotate_half(k) * (sin / scale)
            return (q, k)

        def _decay_mask(T):
            gamma = 1.0 - 2.0 ** (-5.0 - jnp.arange(NHEADS, dtype=jnp.float32))
            idx = jnp.arange(T)
            diff = idx[:, None] - idx[None, :]
            causal = diff >= 0
            expn = jnp.where(causal, diff, 0).astype(jnp.float32)
            return jnp.where(causal[None], gamma[:, None, None] ** expn[None], 0.0)
        key = jax.random.key(seed)
        ks = jax.random.split(key, 4)
        s = 0.02
        return {'x': jax.random.normal(ks[0], (B, T, C), jnp.float32), 'w_qkv': jax.random.normal(ks[1], (3 * C, C), jnp.float32) * s, 'w_gated': jax.random.normal(ks[2], (C, C), jnp.float32) * s, 'w_proj': jax.random.normal(ks[3], (C, C), jnp.float32) * s, 'gn_weight': jnp.ones((C,), jnp.float32), 'gn_bias': jnp.zeros((C,), jnp.float32)}
    _L2_attn_in = _L2_attn_setup()

    def _L2_ffn_setup():
        import jax, jax.numpy as jnp
        import numpy as np
        D_MODEL, D_FF, N_EXPERTS, TOP_K = (128, 256, 8, 2)
        B, S = (2, 256)
        key = jax.random.key(seed)
        ks = jax.random.split(key, 6)
        sd = 1.0 / np.sqrt(D_MODEL)
        sf = 1.0 / np.sqrt(D_FF)
        return {'x': jax.random.normal(ks[0], (B, S, D_MODEL), jnp.float32), 'router_w': jax.random.normal(ks[1], (N_EXPERTS, D_MODEL), jnp.float32) * sd, 'gate_w': jax.random.normal(ks[2], (N_EXPERTS, D_MODEL, D_FF), jnp.float32) * sd, 'gate_b': jnp.zeros((N_EXPERTS, D_FF), jnp.float32), 'up_w': jax.random.normal(ks[3], (N_EXPERTS, D_MODEL, D_FF), jnp.float32) * sd, 'up_b': jnp.zeros((N_EXPERTS, D_FF), jnp.float32), 'down_w': jax.random.normal(ks[4], (N_EXPERTS, D_FF, D_MODEL), jnp.float32) * sf, 'down_b': jnp.zeros((N_EXPERTS, D_MODEL), jnp.float32)}
    _L2_ffn_in = _L2_ffn_setup()

    def _L3_attn_setup():
        import jax, jax.numpy as jnp
        import numpy as np
        D_MODEL = 128
        N_HEADS = 16
        D_LATENT = 32
        HEAD_DIM = D_MODEL // N_HEADS

        def apply_rope(x):
            B, T, H, D = x.shape
            inv_freq = 1.0 / 10000.0 ** (jnp.arange(0, D, 2, dtype=jnp.float32) / D)
            t = jnp.arange(T, dtype=jnp.float32)
            freqs = t[:, None] * inv_freq[None, :]
            sin_f = jnp.sin(freqs)[None, :, None, :]
            cos_f = jnp.cos(freqs)[None, :, None, :]
            x1, x2 = jnp.split(x, 2, axis=-1)
            return jnp.concatenate([x1 * cos_f - x2 * sin_f, x1 * sin_f + x2 * cos_f], axis=-1)
        key = jax.random.key(seed)
        ks = jax.random.split(key, 10)
        B, T = (4, 512)
        s = lambda fan_in: 1.0 / np.sqrt(fan_in)
        return {'x': jax.random.normal(ks[0], (B, T, D_MODEL), dtype=jnp.float32), 'Wq': jax.random.normal(ks[1], (D_MODEL, D_MODEL), dtype=jnp.float32) * s(D_MODEL), 'bq': jnp.zeros((D_MODEL,), jnp.float32), 'Wdown': jax.random.normal(ks[2], (D_MODEL, D_LATENT), dtype=jnp.float32) * s(D_MODEL), 'bdown': jnp.zeros((D_LATENT,), jnp.float32), 'Wup': jax.random.normal(ks[3], (D_LATENT, 2 * D_MODEL), dtype=jnp.float32) * s(D_LATENT), 'bup': jnp.zeros((2 * D_MODEL,), jnp.float32), 'Wout': jax.random.normal(ks[4], (D_MODEL, D_MODEL), dtype=jnp.float32) * s(D_MODEL), 'bout': jnp.zeros((D_MODEL,), jnp.float32)}
    _L3_attn_in = _L3_attn_setup()

    def _L3_ffn_setup():
        import jax, jax.numpy as jnp
        import numpy as np
        B, S, D = (4, 256, 128)
        E = 8
        CF = 1
        key = jax.random.key(seed)
        k_x, k_g, k_w, k_b = jax.random.split(key, 4)
        x = jax.random.normal(k_x, (B, S, D), dtype=jnp.float32)
        Wg = jax.random.normal(k_g, (D, E), dtype=jnp.float32) * (1.0 / np.sqrt(D))
        We = jax.random.normal(k_w, (D, D), dtype=jnp.float32) * (1.0 / np.sqrt(D))
        be = jax.random.normal(k_b, (D,), dtype=jnp.float32) * 0.01
        return {'x': x, 'Wg': Wg, 'We': We, 'be': be}
    _L3_ffn_in = _L3_ffn_setup()
    _d = {'L0_attn_x': _L0_attn_in['x'], 'L0_attn_W_qkv': _L0_attn_in['W_qkv'], 'L0_attn_b_qkv': _L0_attn_in['b_qkv'], 'L0_attn_W_out': _L0_attn_in['W_out'], 'L0_attn_b_out': _L0_attn_in['b_out'], 'L0_ffn_wqkv': _L0_ffn_in['wqkv'], 'L0_ffn_q_scale': _L0_ffn_in['q_scale'], 'L0_ffn_k_scale': _L0_ffn_in['k_scale'], 'L0_ffn_wo': _L0_ffn_in['wo'], 'L0_ffn_ln_g': _L0_ffn_in['ln_g'], 'L0_ffn_ln_b': _L0_ffn_in['ln_b'], 'L0_ffn_w1': _L0_ffn_in['w1'], 'L0_ffn_b1': _L0_ffn_in['b1'], 'L0_ffn_w2': _L0_ffn_in['w2'], 'L0_ffn_b2': _L0_ffn_in['b2'], 'L1_attn_Wq': _L1_attn_in['Wq'], 'L1_attn_Wk': _L1_attn_in['Wk'], 'L1_attn_Wv': _L1_attn_in['Wv'], 'L1_attn_Wo': _L1_attn_in['Wo'], 'L1_ffn_gate_w': _L1_ffn_in['gate_w'], 'L1_ffn_w1': _L1_ffn_in['w1'], 'L1_ffn_w2': _L1_ffn_in['w2'], 'L1_ffn_w3': _L1_ffn_in['w3'], 'L2_attn_w_qkv': _L2_attn_in['w_qkv'], 'L2_attn_w_gated': _L2_attn_in['w_gated'], 'L2_attn_w_proj': _L2_attn_in['w_proj'], 'L2_attn_gn_weight': _L2_attn_in['gn_weight'], 'L2_attn_gn_bias': _L2_attn_in['gn_bias'], 'L2_ffn_router_w': _L2_ffn_in['router_w'], 'L2_ffn_gate_w': _L2_ffn_in['gate_w'], 'L2_ffn_gate_b': _L2_ffn_in['gate_b'], 'L2_ffn_up_w': _L2_ffn_in['up_w'], 'L2_ffn_up_b': _L2_ffn_in['up_b'], 'L2_ffn_down_w': _L2_ffn_in['down_w'], 'L2_ffn_down_b': _L2_ffn_in['down_b'], 'L3_attn_Wq': _L3_attn_in['Wq'], 'L3_attn_bq': _L3_attn_in['bq'], 'L3_attn_Wdown': _L3_attn_in['Wdown'], 'L3_attn_bdown': _L3_attn_in['bdown'], 'L3_attn_Wup': _L3_attn_in['Wup'], 'L3_attn_bup': _L3_attn_in['bup'], 'L3_attn_Wout': _L3_attn_in['Wout'], 'L3_attn_bout': _L3_attn_in['bout'], 'L3_ffn_Wg': _L3_ffn_in['Wg'], 'L3_ffn_We': _L3_ffn_in['We'], 'L3_ffn_be': _L3_ffn_in['be']}
    _x0 = _d['L0_attn_x']
    _d['L0_attn_x'] = jax.random.normal(jax.random.fold_in(jax.random.key(seed), 1), (4, 1024, 128), dtype=_x0.dtype)
    del _x0
    return _d

def reference(L0_attn_x, L0_attn_W_qkv, L0_attn_b_qkv, L0_attn_W_out, L0_attn_b_out, L0_ffn_wqkv, L0_ffn_q_scale, L0_ffn_k_scale, L0_ffn_wo, L0_ffn_ln_g, L0_ffn_ln_b, L0_ffn_w1, L0_ffn_b1, L0_ffn_w2, L0_ffn_b2, L1_attn_Wq, L1_attn_Wk, L1_attn_Wv, L1_attn_Wo, L1_ffn_gate_w, L1_ffn_w1, L1_ffn_w2, L1_ffn_w3, L2_attn_w_qkv, L2_attn_w_gated, L2_attn_w_proj, L2_attn_gn_weight, L2_attn_gn_bias, L2_ffn_router_w, L2_ffn_gate_w, L2_ffn_gate_b, L2_ffn_up_w, L2_ffn_up_b, L2_ffn_down_w, L2_ffn_down_b, L3_attn_Wq, L3_attn_bq, L3_attn_Wdown, L3_attn_bdown, L3_attn_Wup, L3_attn_bup, L3_attn_Wout, L3_attn_bout, L3_ffn_Wg, L3_ffn_We, L3_ffn_be):

    def _L0_attn_ref(x, W_qkv, b_qkv, W_out, b_out):
        import jax, jax.numpy as jnp
        import numpy as np
        D_MODEL = 128
        NUM_HEADS = 16
        D_K = D_MODEL // NUM_HEADS
        B, S, _ = x.shape
        qkv = (jnp.einsum('bsd,de->bse', x, W_qkv) + b_qkv).reshape(B, S, NUM_HEADS, 3 * D_K)
        q, k, v = (qkv[..., :D_K], qkv[..., D_K:2 * D_K], qkv[..., 2 * D_K:])
        scores = jnp.einsum('bshd,bsgd->bshg', q, k) / np.sqrt(D_K)
        attn = jax.nn.softmax(scores, axis=-1)
        context = jnp.einsum('bshg,bsgd->bshd', attn, v).reshape(B, S, NUM_HEADS * D_K)
        return jnp.einsum('bsd,de->bse', context, W_out) + b_out

    def _L0_ffn_ref(x, wqkv, q_scale, k_scale, wo, ln_g, ln_b, w1, b1, w2, b2):
        import jax, jax.numpy as jnp
        import numpy as np
        DIM = 128
        DEPTH = 2
        HEADS = 8
        DIM_HEAD = 64
        WINDOW = 64
        INNER = HEADS * DIM_HEAD
        HID = int(DIM * 4 * 2 / 3)
        B, N = (2, 1024)
        QK_SCALE = 8.0

        def shift_token(t):
            t1, t2 = jnp.split(t, 2, axis=-1)
            t2 = jnp.pad(t2, ((0, 0), (1, 0), (0, 0)))[:, :-1]
            return jnp.concatenate([t1, t2], axis=-1)

        def l2norm(t):
            return t / jnp.clip(jnp.linalg.norm(t, axis=-1, keepdims=True), 1e-12)

        def rotate_half(x):
            x1, x2 = jnp.split(x, 2, axis=-1)
            return jnp.concatenate([-x2, x1], axis=-1)

        def rotary_xpos(q, k):
            n = q.shape[-2]
            half_idx = jnp.arange(0, DIM_HEAD, 2, dtype=jnp.float32)
            inv_freq = 1.0 / 10000.0 ** (half_idx / DIM_HEAD)
            t = jnp.arange(n, dtype=jnp.float32)
            freqs = t[:, None] * inv_freq[None, :]
            freqs = jnp.concatenate([freqs, freqs], axis=-1)
            base = (half_idx + 0.4 * DIM_HEAD) / (1.4 * DIM_HEAD)
            power = (t - n // 2) / float(WINDOW // 2)
            scale = base[None, :] ** power[:, None]
            scale = jnp.concatenate([scale, scale], axis=-1)
            cos, sin = (jnp.cos(freqs), jnp.sin(freqs))
            q = q * cos * scale + rotate_half(q) * sin * scale
            k = k * cos / scale + rotate_half(k) * sin / scale
            return (q, k)

        def local_attention(q, k, v):
            b, h, n, d = q.shape
            w = n // WINDOW
            bq = q.reshape(b, h, w, WINDOW, d) * QK_SCALE
            bk = k.reshape(b, h, w, WINDOW, d)
            bv = v.reshape(b, h, w, WINDOW, d)

            def look_around(t):
                p = jnp.pad(t, ((0, 0), (0, 0), (1, 0), (0, 0), (0, 0)))
                return jnp.concatenate([p[:, :, :w], p[:, :, 1:]], axis=3)
            bk, bv = (look_around(bk), look_around(bv))
            bt = jnp.arange(n).reshape(w, WINDOW)
            btp = jnp.pad(bt, ((1, 0), (0, 0)), constant_values=-1)
            btk = jnp.concatenate([btp[:w], btp[1:]], axis=1)
            sim = jnp.einsum('bhwid,bhwjd->bhwij', bq, bk)
            i = bt[:, :, None]
            j = btk[:, None, :]
            mask = (i < j) | (i > j + WINDOW) | (j == -1)
            sim = jnp.where(mask, -jnp.finfo(sim.dtype).max, sim)
            attn = jax.nn.softmax(sim, axis=-1)
            out = jnp.einsum('bhwij,bhwjd->bhwid', attn, bv)
            return out.reshape(b, h, n, d)

        def _layer(x, wqkv, qs, ksc, wo, lg, lb, w1, b1, w2, b2):
            b, n, _ = x.shape
            h = shift_token(x)
            qkv = h @ wqkv
            q, k, v = jnp.split(qkv, 3, axis=-1)
            to_heads = lambda t: t.reshape(b, n, HEADS, DIM_HEAD).transpose(0, 2, 1, 3)
            q, k, v = (to_heads(q), to_heads(k), to_heads(v))
            q = l2norm(q) * qs
            k = l2norm(k) * ksc
            q, k = rotary_xpos(q, k)
            o = local_attention(q, k, v)
            o = o.transpose(0, 2, 1, 3).reshape(b, n, INNER)
            x = x + o @ wo
            h = shift_token(x)
            mu = h.mean(-1, keepdims=True)
            var = h.var(-1, keepdims=True)
            h = (h - mu) / jnp.sqrt(var + 1e-05) * lg + lb
            h = h @ w1 + b1
            a, g = jnp.split(h, 2, axis=-1)
            h = a * jax.nn.gelu(g, approximate=False)
            x = x + h @ w2 + b2
            return x
        for l in range(DEPTH):
            x = _layer(x, wqkv[l], q_scale[l], k_scale[l], wo[l], ln_g[l], ln_b[l], w1[l], b1[l], w2[l], b2[l])
        return x

    def _L1_attn_ref(x, Wq, Wk, Wv, Wo):
        import jax, jax.numpy as jnp
        import numpy as np
        EMB = 128
        HEADS = 16
        ATT = EMB // HEADS
        b, t, _ = x.shape
        h, d = (HEADS, ATT)
        scale = d ** (-0.25)
        q = (x @ Wq).reshape(b, t, h, d) * scale
        k = (x @ Wk).reshape(b, t, h, d) * scale
        v = (x @ Wv).reshape(b, t, h, d)
        dot = jnp.einsum('bqhd,bkhd->bhqk', q, k)
        causal = jnp.tril(jnp.ones((t, t), dtype=bool))
        dot = jnp.where(causal[None, None], dot, -jnp.inf)
        attn = jax.nn.softmax(dot, axis=-1)
        out = jnp.einsum('bhqk,bkhd->bqhd', attn, v).reshape(b, t, h * d)
        return out @ Wo

    def _L1_ffn_ref(hidden_states, gate_w, w1, w2, w3):
        import jax, jax.numpy as jnp
        import numpy as np
        E, K, D, H = (8, 2, 128, 256)
        B, S = (1, 128)

        def _grouped_swiglu(x_sorted, counts, w1, w2, w3):
            if hasattr(jax.lax, 'ragged_dot'):
                gs = counts.astype(jnp.int32)
                h = jax.nn.silu(jax.lax.ragged_dot(x_sorted, w1, gs)) * jax.lax.ragged_dot(x_sorted, w3, gs)
                return jax.lax.ragged_dot(h, w2, gs)
            pos = jnp.arange(x_sorted.shape[0])
            eid = jnp.searchsorted(jnp.cumsum(counts), pos, side='right')
            out = jnp.zeros((x_sorted.shape[0], w2.shape[-1]), x_sorted.dtype)
            for e in range(w1.shape[0]):
                xm = jnp.where((eid == e)[:, None], x_sorted, 0.0)
                he = jax.nn.silu(xm @ w1[e]) * (xm @ w3[e])
                out = out + he @ w2[e]
            return out
        x = hidden_states.reshape(-1, D)
        N = x.shape[0]
        scores = jax.nn.softmax(x @ gate_w.T, axis=-1)
        top_scores, sel = jax.lax.top_k(scores, K)
        sel_flat = sel.T.reshape(-1)
        scores_flat = top_scores.T.reshape(-1)
        order = jnp.argsort(sel_flat, stable=True)
        tok_sorted = order % N
        scores_sorted = scores_flat[order]
        counts = jnp.bincount(sel_flat, length=E)
        x_sorted = x[tok_sorted]
        y = _grouped_swiglu(x_sorted, counts, w1, w2, w3)
        weighted = y * scores_sorted[:, None]
        out = jnp.zeros((N, D), x.dtype).at[tok_sorted].add(weighted)
        return out.reshape(hidden_states.shape)

    def _L2_attn_ref(x, w_qkv, w_gated, w_proj, gn_weight, gn_bias):
        import jax, jax.numpy as jnp
        import numpy as np
        B, T, C = (2, 256, 128)
        NHEADS = 16
        HEAD_DIM = C // NHEADS
        THETA = 10000.0
        SCALE_BASE = 512.0
        GN_EPS = 1e-05

        def _rotate_half(x):
            x1 = x[..., 0::2]
            x2 = x[..., 1::2]
            return jnp.stack([-x2, x1], axis=-1).reshape(x.shape)

        def _rope_xpos(q, k, T):
            d = q.shape[-1]
            half = jnp.arange(0, d, 2, dtype=jnp.float32)
            inv_freq = 1.0 / THETA ** (half / d)
            t = jnp.arange(T, dtype=jnp.float32)
            freqs = t[:, None] * inv_freq[None, :]
            freqs = jnp.repeat(freqs, 2, axis=-1)
            scale_vec = (half + 0.4 * d) / (1.4 * d)
            power = (t - T // 2) / SCALE_BASE
            scale = scale_vec[None, :] ** power[:, None]
            scale = jnp.repeat(scale, 2, axis=-1)
            cos, sin = (jnp.cos(freqs), jnp.sin(freqs))
            q = q * (cos * scale) + _rotate_half(q) * (sin * scale)
            k = k * (cos / scale) + _rotate_half(k) * (sin / scale)
            return (q, k)

        def _decay_mask(T):
            gamma = 1.0 - 2.0 ** (-5.0 - jnp.arange(NHEADS, dtype=jnp.float32))
            idx = jnp.arange(T)
            diff = idx[:, None] - idx[None, :]
            causal = diff >= 0
            expn = jnp.where(causal, diff, 0).astype(jnp.float32)
            return jnp.where(causal[None], gamma[:, None, None] ** expn[None], 0.0)
        Bx, Tx, Cx = x.shape
        qkv = x @ w_qkv.T
        q, k, v = jnp.split(qkv, 3, axis=-1)

        def to_heads(u):
            return u.reshape(Bx, Tx, NHEADS, HEAD_DIM).transpose(0, 2, 1, 3)
        q, k, v = (to_heads(q), to_heads(k), to_heads(v))
        q, k = _rope_xpos(q, k, Tx)
        mask = _decay_mask(Tx)
        scores = jnp.einsum('bhtd,bhsd->bhts', q, k) * HEAD_DIM ** (-0.5)
        scores = scores * mask[None]
        y = jnp.einsum('bhts,bhsd->bhtd', scores, v)
        y = y.transpose(0, 2, 1, 3).reshape(Bx, Tx, Cx)
        yt = y.transpose(0, 2, 1).reshape(Bx, NHEADS, HEAD_DIM, Tx)
        mean = yt.mean(axis=(2, 3), keepdims=True)
        var = yt.var(axis=(2, 3), keepdims=True)
        yn = (yt - mean) / jnp.sqrt(var + GN_EPS)
        yn = yn.reshape(Bx, Cx, Tx)
        yn = yn * gn_weight[None, :, None] + gn_bias[None, :, None]
        yn = yn.transpose(0, 2, 1)
        out = jax.nn.silu(x @ w_gated.T) * yn
        return out @ w_proj.T

    def _L2_ffn_ref(x, router_w, gate_w, gate_b, up_w, up_b, down_w, down_b):
        import jax, jax.numpy as jnp
        import numpy as np
        D_MODEL, D_FF, N_EXPERTS, TOP_K = (128, 256, 8, 2)
        B, S = (2, 256)
        b, s, d = x.shape
        xf = x.reshape(b * s, d)
        n = xf.shape[0]
        router_logits = xf @ router_w.T
        probs = jax.nn.softmax(router_logits, axis=-1)
        topv, topi = jax.lax.top_k(probs, TOP_K)
        mask = jnp.zeros_like(probs).at[jnp.arange(n)[:, None], topi].set(1.0)
        probs = probs * mask
        probs = probs / (probs.sum(axis=-1, keepdims=True) + 1e-09)
        g = jnp.einsum('nd,edf->nef', xf, gate_w) + gate_b
        u = jnp.einsum('nd,edf->nef', xf, up_w) + up_b
        h = jax.nn.silu(g) * u
        expert_out = jnp.einsum('nef,efd->ned', h, down_w) + down_b
        y = jnp.einsum('ne,ned->nd', probs, expert_out)
        return y.reshape(b, s, d)

    def _L3_attn_ref(x, Wq, bq, Wdown, bdown, Wup, bup, Wout, bout):
        import jax, jax.numpy as jnp
        import numpy as np
        D_MODEL = 128
        N_HEADS = 16
        D_LATENT = 32
        HEAD_DIM = D_MODEL // N_HEADS

        def apply_rope(x):
            B, T, H, D = x.shape
            inv_freq = 1.0 / 10000.0 ** (jnp.arange(0, D, 2, dtype=jnp.float32) / D)
            t = jnp.arange(T, dtype=jnp.float32)
            freqs = t[:, None] * inv_freq[None, :]
            sin_f = jnp.sin(freqs)[None, :, None, :]
            cos_f = jnp.cos(freqs)[None, :, None, :]
            x1, x2 = jnp.split(x, 2, axis=-1)
            return jnp.concatenate([x1 * cos_f - x2 * sin_f, x1 * sin_f + x2 * cos_f], axis=-1)
        B, T, D = x.shape
        H, Dh = (N_HEADS, HEAD_DIM)
        q = x @ Wq + bq
        kv_latent = x @ Wdown + bdown
        kv = kv_latent @ Wup + bup
        q = q.reshape(B, T, H, Dh)
        kv = kv.reshape(B, T, H, 2 * Dh)
        k, v = jnp.split(kv, 2, axis=-1)
        q = apply_rope(q)
        k = apply_rope(k)
        att = jnp.einsum('bthd,btgd->bthg', q, k) / jnp.sqrt(jnp.float32(Dh))
        att = jax.nn.softmax(att, axis=-1)
        out = jnp.einsum('bthg,btgd->bthd', att, v)
        out = out.reshape(B, T, D)
        return out @ Wout + bout

    def _L3_ffn_ref(x, Wg, We, be):
        import jax, jax.numpy as jnp
        import numpy as np
        B, S, D = (4, 256, 128)
        E = 8
        CF = 1
        b, s, d = x.shape
        n = b * s
        cap = n // E * CF
        h = x.reshape(n, d)
        router_logits = h @ Wg
        probs = jax.nn.softmax(router_logits, axis=1)
        best = jnp.argmax(probs, axis=1)
        mask = jax.nn.one_hot(best, E, dtype=probs.dtype)
        gate = jnp.sum(probs * mask, axis=1)
        locations = jnp.cumsum(mask, axis=0) - 1.0
        mask = mask * (locations < cap).astype(mask.dtype)
        loc_idx = jnp.sum(locations * mask, axis=1).astype(jnp.int32)
        new_gate = gate[:, None] * mask
        loc_oh = jax.nn.one_hot(loc_idx, cap, dtype=new_gate.dtype)
        combine = new_gate[:, :, None] * loc_oh[:, None, :]
        dispatch = (combine != 0).astype(h.dtype)
        dispatched = jnp.einsum('nec,nd->ecd', dispatch, h).reshape(E * cap, d)
        expert_out = dispatched @ We + be
        out = combine.reshape(n, E * cap) @ expert_out
        return out.reshape(b, s, d)
    x = L0_attn_x
    xn = _layernorm(x, axis=-1)
    x = x + _L0_attn_ref(xn, L0_attn_W_qkv, L0_attn_b_qkv, L0_attn_W_out, L0_attn_b_out) + _L0_ffn_ref(xn, L0_ffn_wqkv, L0_ffn_q_scale, L0_ffn_k_scale, L0_ffn_wo, L0_ffn_ln_g, L0_ffn_ln_b, L0_ffn_w1, L0_ffn_b1, L0_ffn_w2, L0_ffn_b2)
    xn = _layernorm(x, axis=-1)
    x = x + _L1_attn_ref(xn, L1_attn_Wq, L1_attn_Wk, L1_attn_Wv, L1_attn_Wo) + _L1_ffn_ref(xn, L1_ffn_gate_w, L1_ffn_w1, L1_ffn_w2, L1_ffn_w3)
    xn = _layernorm(x, axis=-1)
    x = x + _L2_attn_ref(xn, L2_attn_w_qkv, L2_attn_w_gated, L2_attn_w_proj, L2_attn_gn_weight, L2_attn_gn_bias) + _L2_ffn_ref(xn, L2_ffn_router_w, L2_ffn_gate_w, L2_ffn_gate_b, L2_ffn_up_w, L2_ffn_up_b, L2_ffn_down_w, L2_ffn_down_b)
    xn = _layernorm(x, axis=-1)
    x = x + _L3_attn_ref(xn, L3_attn_Wq, L3_attn_bq, L3_attn_Wdown, L3_attn_bdown, L3_attn_Wup, L3_attn_bup, L3_attn_Wout, L3_attn_bout) + _L3_ffn_ref(xn, L3_ffn_Wg, L3_ffn_We, L3_ffn_be)
    return x

_drawn_inputs = setup_inputs


def setup_inputs(seed=0):
    import zlib

    import numpy as np

    out = dict(_drawn_inputs(seed))
    spreads = {'L0_ffn_q_scale': (1.0, 0.6),
     'L0_ffn_k_scale': (1.0, 0.6),
     'L0_ffn_ln_g': (1.0, 0.6),
     'L0_ffn_ln_b': (0.0, 0.8),
     'L0_ffn_b1': (0.0, 0.444),
     'L0_ffn_b2': (0.0, 0.1),
     'L2_attn_gn_weight': (1.0, 0.6),
     'L2_attn_gn_bias': (0.0, 0.8),
     'L2_ffn_gate_b': (0.0, 0.307),
     'L2_ffn_up_b': (0.0, 0.289),
     'L2_ffn_down_b': (0.0, 0.1),
     'L3_attn_bq': (0.0, 0.532),
     'L3_attn_bdown': (0.0, 0.343),
     'L3_attn_bup': (0.0, 0.397),
     'L3_attn_bout': (0.0, 0.1)}
    factors = {'L0_attn_b_qkv': 5.777,
     'L0_attn_b_out': 3.524,
     'L1_attn_Wq': 3.983,
     'L1_attn_Wk': 3.677,
     'L2_attn_w_qkv': 3.613,
     'L2_attn_w_gated': 3.344,
     'L2_attn_w_proj': 3.443,
     'L3_ffn_be': 33.301}
    for name, (base, spread) in spreads.items():
        noise = np.random.default_rng([zlib.crc32(name.encode()), seed]).standard_normal(out[name].shape)
        drawn = base * np.exp(spread * noise) if base else spread * noise
        out[name] = jnp.asarray(drawn.astype(out[name].dtype))
    for name, factor in factors.items():
        out[name] = (out[name] * factor).astype(out[name].dtype)
    return out
```

```python
from contextlib import ExitStack

import numpy as np

import concourse.bass as bass
from concourse import mybir

ALU = mybir.AluOpType
ACT = mybir.ActivationFunctionType
AX = mybir.AxisListType
F32 = mybir.dt.float32
BF16 = mybir.dt.bfloat16
ds = bass.ds

P = 128
D = 128
BATCH, SEQ = 4, 1024
TOK = BATCH * SEQ
CH = 512
NCH = TOK // CH
TPB = SEQ // P
EPS = 1e-5

HEADS, HD = 16, 8
QUADS = 4
SCALE8 = float(1.0 / np.sqrt(8.0))
Q_PART = [0, 0, 1, 1, 0, 2]
K_PART = [0, 1, 0, 1, 2, 0]
M_ROW = 8 * len(Q_PART)


class Scope:

    def __init__(self, nc, ctx, name):
        self.nc, self.ctx, self.name = nc, ctx, name
        self.sems = []
        ctx.callback(self.release)

    def release(self):
        if self.sems:
            self.nc.clear_and_free_semaphores(self.sems)
            self.nc.all_engine_barrier()

    def sb(self, name, shape, dt=F32):
        return self.ctx.enter_context(self.nc.sbuf_tensor(f"{self.name}_{name}", shape, dt))

    def ps(self, name, shape, dt=F32):
        return self.ctx.enter_context(self.nc.psum_tensor(f"{self.name}_{name}", shape, dt))

    def sem(self, name):
        self.sems.append(self.nc.alloc_semaphore(f"{self.name}_{name}"))
        return self.sems[-1]


def load_phase(nc, name, loads):
    with ExitStack() as ctx:
        landed = Scope(nc, ctx, name).sem("landed")
        with nc.Block() as block:
            @block.sync
            def _(sp):
                for dst, src in loads:
                    sp.dma_start(dst, src).then_inc(landed, 16)
                sp.wait_ge(landed, 16 * len(loads))


def layernorm(nc, name, src, dst, mean_w, eps_col, gain=None, shift=None):
    with ExitStack() as ctx:
        s = Scope(nc, ctx, name)
        cen = s.sb("cen", [P, 2, CH])
        sq = s.sb("sq", [P, 2, CH])
        std = s.sb("std", [P, 2, CH])
        rstd = s.sb("rstd", [P, 2, CH])
        mean_ps = s.ps("mean_ps", [P, 2, CH])
        var_ps = s.ps("var_ps", [P, 2, CH])
        mean_ready, centred = s.sem("mean_ready"), s.sem("centred")
        squared, var_ready = s.sem("squared"), s.sem("var_ready")
        rooted, inverted, scaled = s.sem("rooted"), s.sem("inverted"), s.sem("scaled")
        affine = s.sem("affine")
        with nc.Block() as block:
            @block.tensor
            def _(pe):
                with nc.tensor.Fori(0, NCH // 2) as n:
                    for i in range(2):
                        pe.wait_ge(centred, n * 2 + i + 1)
                        nc.tensor.matmul(mean_ps[:, i], mean_w[:], src[:, ds(n * 2 * CH + i * CH, CH)],
                                         start=True, stop=True).then_inc(mean_ready, 1)
                    for i in range(2):
                        pe.wait_ge(squared, n * 2 + i + 1)
                        pe.wait_ge(rooted, n * 2 + i + 1)
                        nc.tensor.matmul(var_ps[:, i], mean_w[:], sq[:, i], start=True,
                                         stop=True).then_inc(var_ready, 1)

            @block.scalar
            def _(act):
                act.sem_inc(rooted, 2)
                with nc.scalar.Fori(0, NCH // 2) as n:
                    for i in range(2):
                        act.wait_ge(centred, n * 2 + i + 3)
                        nc.scalar.activation(sq[:, i], cen[:, i], ACT.Square).then_inc(squared, 1)
                    for i in range(2):
                        act.wait_ge(var_ready, n * 2 + i + 1)
                        act.wait_ge(inverted, n * 2 + i + 1)
                        nc.scalar.activation(std[:, i], var_ps[:, i], ACT.Sqrt,
                                             bias=eps_col[:]).then_inc(rooted, 1)

            @block.vector
            def _(dve):
                dve.sem_inc(centred, 2)
                dve.sem_inc(inverted, 2)
                dve.sem_inc(scaled, 2)
                with nc.vector.Fori(0, NCH // 2) as n:
                    for i in range(2):
                        dve.wait_ge(mean_ready, n * 2 + i + 1)
                        dve.wait_ge(scaled, n * 2 + i + 1)
                        nc.vector.tensor_tensor(cen[:, i], src[:, ds(n * 2 * CH + i * CH, CH)], mean_ps[:, i],
                                                ALU.subtract).then_inc(centred, 1)
                    for i in range(2):
                        dve.wait_ge(rooted, n * 2 + i + 3)
                        nc.vector.reciprocal(rstd[:, i], std[:, i]).then_inc(inverted, 1)
                        dve.wait_ge(inverted, n * 2 + i + 3)
                        nc.vector.tensor_tensor(dst[:, ds(n * 2 * CH + i * CH, CH)], cen[:, i], rstd[:, i],
                                                ALU.mult).then_inc(scaled, 1)
                        if gain is not None:
                            dve.wait_ge(scaled, n * 2 + i + 3)
                            nc.vector.tensor_scalar(dst[:, ds(n * 2 * CH + i * CH, CH)],
                                                    dst[:, ds(n * 2 * CH + i * CH, CH)],
                                                    gain, shift, ALU.mult, ALU.add).then_inc(affine, 1)


def narrow_attention(nc, name, w, c, xn, res, causal=False, latent=False):
    NHALF = 2
    RING = 4
    with ExitStack() as ctx:
        s = Scope(nc, ctx, name)
        kin = 32 if latent else P
        wq, wk = s.sb("wq", [P, D]), s.sb("wk", [kin, D])
        wv, bv = s.sb("wv", [kin, QUADS * P]), s.sb("bv", [1, QUADS * P])
        wo = s.sb("wo", [P, QUADS, D])
        bqk = s.sb("bqk", [P, 4])
        selq = s.sb("selq", [P, QUADS * 2 * 3 * P], BF16)
        selk = s.sb("selk", [P, QUADS * 2 * 3 * P], BF16)
        sumbc = s.sb("sumbc", [P, P])
        kone = s.sb("kone", [P, 1])
        identb = s.sb("identb", [P, P], BF16)
        ones1 = s.sb("ones1", [1, P])
        loads = [(wq[:], w["wq"]), (wk[:], w["wk"]), (wv[:], w["wv"]), (bv[:], w["bv"]),
                 (wo[:], w["wo"].rearrange("q p n -> p q n")), (bqk[:], w["bqk"]),
                 (selq[:], c["selq"]), (selk[:], c["selk"]), (sumbc[:], c["sumbc"]), (kone[:], c["kone"]),
                 (identb[:], c["identb"]), (ones1[:], c["ones1"])]
        if latent:
            wqr, wkr = s.sb("wqr", [P, D]), s.sb("wkr", [kin, D])
            wdown, bdown = s.sb("wdown", [P, kin]), s.sb("bdown", [kin, 1])
            cos, sin = s.sb("cos", [P, SEQ]), s.sb("sin", [P, SEQ])
            lat = s.sb("lat", [kin, SEQ])
            qkr = s.sb("qkr", [P, 2, SEQ])
            loads += [(wqr[:], w["wqr"]), (wkr[:], w["wkr"]), (wdown[:], w["wdown"]), (bdown[:], w["bdown"]),
                      (cos[:], c["cos8"]), (sin[:], c["sin8"])]
        if causal:
            mask_qk, mask_kq = s.sb("mask_qk", [P, P], BF16), s.sb("mask_kq", [P, P], BF16)
            loads += [(mask_qk[:], c["mask_qk"]), (mask_kq[:], c["mask_kq"])]
        load_phase(nc, name + "_load", loads)

        xb = s.sb("xb", [P, SEQ])
        qk = s.sb("qk", [P, 2, SEQ])
        part = s.sb("part", [P, 2, 3, SEQ], BF16)
        rest = s.sb("rest", [P, 2, SEQ])
        kx = s.sb("kx", [P, 2, SEQ], BF16)
        qx = s.sb("qx", [P, 2, SEQ], BF16)
        qxm = s.sb("qxm", [P, 2, SEQ], BF16)
        vq = s.sb("vq", [P, TPB, P])
        halfmax = s.sb("halfmax", [P, TPB, 4, NHALF])
        negmax = s.sb("negmax", [P, TPB, 4])
        negrest = s.sb("negrest", [P, TPB, 4])
        mst = s.sb("mst", [P, TPB, 2, P], BF16)
        pr = s.sb("pr", [P, RING, 2, CH])
        osum = s.sb("osum", [P, CH])
        rsum = s.sb("rsum", [P, CH])
        ctxt = s.sb("ctxt", [P, QUADS, SEQ])
        ab = s.ps("ab", [P, 2, CH])
        st = s.ps("st", [P, 2, 2, CH])
        ob = s.ps("ob", [P, CH])
        mb = s.ps("mb", [P, CH])

        xb_ready, qk_raw, qk_ready = s.sem("xb_ready"), s.sem("qk_raw"), s.sem("qk_ready")
        part_high, rest_ready, part_mid, split_done = (s.sem("part_high"), s.sem("rest_ready"), s.sem("part_mid"),
                                                       s.sem("split_done"))
        ab_full, ab_done = s.sem("ab_full"), s.sem("ab_done")
        max_step, max_ready = s.sem("max_step"), s.sem("max_ready")
        st_full, exp_done, pv_done = s.sem("st_full"), s.sem("exp_done"), s.sem("pv_done")
        o_copied, sum_ready, r_ready, ctx_ready = (s.sem("o_copied"), s.sem("sum_ready"), s.sem("r_ready"),
                                                   s.sem("ctx_ready"))
        zeroed = s.sem("zeroed")

        halves = [(qb, h) for qb in range(TPB) for h in range(NHALF) if not causal or h * CH < (qb + 1) * P]
        PREP = 10 if latent else 4
        QJOBS = 10 + 4 * len(halves) + 4
        BJOBS = PREP + QUADS * QJOBS + 2
        steps = [(ch, kb, g) for ch in range(2) for kb in range(4 * ch + 4 if causal else TPB) for g in range(2)]
        NST = len(steps)
        assert NST % RING == 0
        MSTEPS = 5

        def width(qb, h):
            return min(CH, (qb + 1) * P - h * CH) if causal else CH

        def first_col(ch, kb):
            return max(0, kb - 4 * ch) * P if causal else 0

        with nc.Block() as block:
            @block.gpsimd
            def _(pool):
                nc.gpsimd.memset(mst[:], 0.0).then_inc(zeroed, 1)
                nc.gpsimd.memset(halfmax[:], -3.0e38).then_inc(zeroed, 1)
                with nc.gpsimd.Fori(0, BATCH) as b:
                    for i in range(2):
                        if latent:
                            pool.wait_ge(qk_raw, b * 2 + i + 1)
                            nc.gpsimd.tensor_tensor(qk[:, i], qk[:, i], qkr[:, i], ALU.add).then_inc(qk_ready, 1)
                        pool.wait_ge(part_high, b * 2 + i + 1)
                        nc.gpsimd.tensor_tensor(rest[:, i], qk[:, i], part[:, i, 0],
                                                ALU.subtract).then_inc(rest_ready, 1)
                        pool.wait_ge(part_mid, b * 2 + i + 1)
                        nc.gpsimd.tensor_tensor(part[:, i, 2], rest[:, i], part[:, i, 1],
                                                ALU.subtract).then_inc(split_done, 1)

            @block.tensor
            def _(pe):
                def job(base, k, products):
                    pe.wait_ge(ab_done, base + k + 1)
                    for i, (at, n, lhsT, rhs) in enumerate(products):
                        last = nc.tensor.matmul(ab[:, k % 2, at:at + n] if lhsT.shape[-1] == P else
                                                ab[0:lhsT.shape[-1], k % 2, at:at + n], lhsT, rhs,
                                                start=i == 0, stop=i == len(products) - 1, skip_group_check=True)
                    last.then_inc(ab_full, 1)

                pe.wait_ge(zeroed, 2)
                with nc.tensor.Fori(0, BATCH) as b:
                    pe.wait_ge(xb_ready, b + 1)
                    base = b * BJOBS
                    k = 0
                    if latent:
                        for ch in range(2):
                            job(base, k, [(0, CH, wdown[:], xb[:, ch * CH:ch * CH + CH])])
                            k += 1
                    for wt in ((wq, wqr) if latent else (wq,)):
                        for ch in range(2):
                            job(base, k, [(0, CH, wt[:], xb[:, ch * CH:ch * CH + CH])])
                            k += 1
                    kv_in = lat if latent else xb
                    if latent:
                        pe.wait_ge(ab_done, base + 2 + 2)
                    for wt in ((wk, wkr) if latent else (wk,)):
                        for ch in range(2):
                            job(base, k, [(0, CH, wt[:], kv_in[:, ch * CH:ch * CH + CH])])
                            k += 1
                    assert k == PREP
                    with nc.tensor.Fori(0, QUADS) as q:
                        qbase = b * BJOBS + PREP + q * QJOBS
                        k = 0
                        pe.wait_ge(split_done, b * 2 + 2)
                        for i, sel in ((1, selk), (0, selq)):
                            for g in range(2):
                                for ch in range(2):
                                    job(qbase, k, [(0, CH, sel[:, ds(q * 6 * P + (g * 3 + l) * P, P)],
                                                    part[:, i, l, ch * CH:ch * CH + CH]) for l in range(3)])
                                    k += 1
                        for half in range(2):
                            mm = []
                            for j in range(4):
                                kb = half * 4 + j
                                mm.append((j * P, P, kv_in[:, kb * P:kb * P + P], wv[:, ds(q * P, P)]))
                                mm.append((j * P, P, ones1[:], bv[:, ds(q * P, P)]))
                            pe.wait_ge(ab_done, qbase + k + 1)
                            for i, (at, n, lhsT, rhs) in enumerate(mm):
                                last = nc.tensor.matmul(ab[:, k % 2, at:at + n], lhsT, rhs, start=i % 2 == 0,
                                                        stop=i % 2 == 1, skip_group_check=True)
                            last.then_inc(ab_full, 1)
                            k += 1
                        pe.wait_ge(ab_done, qbase + 8 + 2)
                        for qb, half in halves:
                            for h in range(4):
                                g, r = h // 2, 64 * (h % 2)
                                n = width(qb, half)
                                diag = causal and qb // 4 == half
                                pe.wait_ge(ab_done, qbase + k + 1)
                                last = nc.tensor.matmul(ab[:, k % 2, 0:n], qx[r:r + 64, g, qb * P:qb * P + P],
                                                        kx[r:r + 64, g, half * CH:half * CH + n],
                                                        start=True, stop=not diag, skip_group_check=True)
                                if diag:
                                    last = nc.tensor.matmul(ab[:, k % 2, n - P:n], identb[:], mask_qk[:],
                                                            start=False, stop=True, skip_group_check=True)
                                last.then_inc(ab_full, 1)
                                k += 1
                        pe.wait_ge(max_ready, b * QUADS + q + 1)
                        for g in range(2):
                            for ch in range(2):
                                job(qbase, k, [(0, CH, selq[:, ds(q * 6 * P + (g * 3 + l) * P, P)],
                                                part[:, 0, l, ch * CH:ch * CH + CH]) for l in range(3)]
                                    + [(j * P, P, mst[:, ch * 4 + j, g], identb[:]) for j in range(4)])
                                k += 1
                        assert k == QJOBS
                        pe.wait_ge(ab_done, qbase + k + 2)
                        sbase = (b * QUADS + q) * NST
                        cbase = (b * QUADS + q) * 2

                        def pv(t):
                            ch, kb, g = steps[t]
                            at = first_col(ch, kb)
                            last_kb = 4 * ch + 3 if causal else TPB - 1
                            pe.wait_ge(exp_done, sbase + t + 3)
                            if kb == 0 and g == 0:
                                pe.wait_ge(o_copied, cbase + ch + 1)
                            for jj in range(2):
                                h = 2 * g + jj
                                mm = nc.tensor.matmul(ob[32 * h:32 * h + 32, at:CH], vq[:, kb, 32 * h:32 * h + 32],
                                                      pr[:, t % RING, jj, at:CH], start=kb == 0, stop=kb == last_kb,
                                                      skip_group_check=True)
                            mm.then_inc(pv_done, 1)

                        def sums(ch):
                            pe.wait_ge(o_copied, cbase + ch + 2)
                            nc.tensor.matmul(mb[:], sumbc[:], osum[:], start=True, stop=True).then_inc(sum_ready, 1)

                        for t, (ch, kb, g) in enumerate(steps):
                            at = first_col(ch, kb)
                            diag = causal and kb >= 4 * ch
                            pe.wait_ge(exp_done, sbase + t + 1)
                            for jj in range(2):
                                r = 64 * jj
                                mm = nc.tensor.matmul(st[:, g, jj, at:CH], kx[r:r + 64, g, kb * P:kb * P + P],
                                                      qxm[r:r + 64, g, ch * CH + at:ch * CH + CH],
                                                      start=True, stop=not diag, skip_group_check=True)
                                if diag:
                                    mm = nc.tensor.matmul(st[:, g, jj, at:at + P], identb[:], mask_kq[:],
                                                          start=False, stop=True, skip_group_check=True)
                            mm.then_inc(st_full, 1)
                            if t >= 2:
                                pv(t - 2)
                                if t < NST - 2 and steps[t - 1][0] != steps[t - 2][0]:
                                    sums(0)
                        pv(NST - 2)
                        pv(NST - 1)
                        sums(1)
                    pe.wait_ge(ctx_ready, b * 2 * QUADS + 2 * QUADS + 1)
                    for ch in range(2):
                        job(base, BJOBS - 2 + ch, [(0, CH, wo[:, i], ctxt[:, i, ch * CH:ch * CH + CH])
                                                   for i in range(QUADS)])

            @block.scalar
            def _(act):
                act.sem_inc(exp_done, 2)
                with nc.scalar.Fori(0, BATCH) as b:
                    for i in range(2):
                        act.wait_ge(qk_ready, b * 2 + i + 1)
                        nc.scalar.activation(part[:, i, 0], qk[:, i], ACT.Copy).then_inc(part_high, 1)
                        act.wait_ge(rest_ready, b * 2 + i + 1)
                        nc.scalar.activation(part[:, i, 1], rest[:, i], ACT.Copy).then_inc(part_mid, 1)
                    with nc.scalar.Fori(0, QUADS) as q:
                        sbase = (b * QUADS + q) * NST
                        for t, (ch, kb, g) in enumerate(steps):
                            at = first_col(ch, kb)
                            act.wait_ge(st_full, sbase + t + 1)
                            act.wait_ge(pv_done, sbase + t + 1)
                            nc.scalar.activation(pr[:, t % RING, :, at:CH], st[:, g, :, at:CH], ACT.Exp,
                                                 scale=SCALE8).then_inc(exp_done, 1)

            @block.vector
            def _(dve):
                dve.sem_inc(ab_done, 2)
                dve.sem_inc(pv_done, RING)
                dve.sem_inc(o_copied, 1)
                dve.sem_inc(ctx_ready, 1)
                dve.wait_ge(zeroed, 2)
                with nc.vector.Fori(0, BATCH) as b:
                    base = b * BJOBS
                    k = 0
                    nc.vector.tensor_scalar(xb[:], xn[:, ds(b * SEQ, SEQ)], 1.0, None, ALU.mult).then_inc(xb_ready, 1)
                    if latent:
                        for ch in range(2):
                            dve.wait_ge(ab_full, base + k + 1)
                            nc.vector.tensor_scalar(lat[:, ch * CH:ch * CH + CH], ab[0:kin, k % 2], bdown[:], None,
                                                    ALU.add).then_inc(ab_done, 1)
                            k += 1
                    for i in range(2):
                        for rot in range(2 if latent else 1):
                            for ch in range(2):
                                dve.wait_ge(ab_full, base + k + 1)
                                bias = bqk[:, 2 * rot + i:2 * rot + i + 1]
                                cols = slice(ch * CH, ch * CH + CH)
                                if latent:
                                    nc.vector.scalar_tensor_tensor(
                                        out=(qkr if rot else qk)[:, i, cols], in0=ab[:, k % 2], scalar=bias,
                                        in1=(sin if rot else cos)[:, cols], op0=ALU.add,
                                        op1=ALU.mult).then_inc(ab_done, 1)
                                else:
                                    nc.vector.tensor_scalar(qk[:, i, cols], ab[:, k % 2], bias, None,
                                                            ALU.add).then_inc(ab_done, 1)
                                k += 1
                        dve.wait_ge(ab_done, base + k + 2)
                        dve.sem_inc(qk_raw if latent else qk_ready, 1)
                    with nc.vector.Fori(0, QUADS) as q:
                        qbase = b * BJOBS + PREP + q * QJOBS
                        unit = b * QUADS + q
                        k = 0
                        for dst, one in ((kx, True), (qx, False)):
                            for g in range(2):
                                for ch in range(2):
                                    dve.wait_ge(ab_full, qbase + k + 1)
                                    cols = slice(ch * CH, ch * CH + CH)
                                    if one:
                                        nc.vector.tensor_scalar(dst[:, g, cols], ab[:, k % 2], kone[:], None,
                                                                ALU.add).then_inc(ab_done, 1)
                                    else:
                                        nc.vector.tensor_copy(dst[:, g, cols], ab[:, k % 2]).then_inc(ab_done, 1)
                                    k += 1
                        for half in range(2):
                            dve.wait_ge(ab_full, qbase + k + 1)
                            nc.vector.tensor_copy(vq[:, half * 4:half * 4 + 4].rearrange("p a b -> p (a b)"),
                                                  ab[:, k % 2]).then_inc(ab_done, 1)
                            k += 1
                        for qb, half in halves:
                            for h in range(4):
                                dve.wait_ge(ab_full, qbase + k + 1)
                                nc.vector.tensor_reduce(halfmax[:, qb, h, half:half + 1],
                                                        ab[:, k % 2, 0:width(qb, half)], AX.X,
                                                        ALU.max).then_inc(ab_done, 1)
                                k += 1
                        dve.wait_ge(ab_done, qbase + k + 2)
                        nc.vector.tensor_reduce(negmax[:], halfmax[:], AX.X, ALU.max,
                                                negate=True).then_inc(max_step, 1)
                        cols = [mst[:].rearrange("p t g (j r) -> p t (g j) r", j=2)[:, :, :, M_ROW + l] for l in range(3)]
                        dve.wait_ge(max_step, unit * MSTEPS + 1)
                        nc.vector.tensor_copy(cols[0], negmax[:]).then_inc(max_step, 1)
                        dve.wait_ge(max_step, unit * MSTEPS + 2)
                        nc.vector.tensor_tensor(negrest[:], negmax[:], cols[0], ALU.subtract).then_inc(max_step, 1)
                        dve.wait_ge(max_step, unit * MSTEPS + 3)
                        nc.vector.tensor_copy(cols[1], negrest[:]).then_inc(max_step, 1)
                        dve.wait_ge(max_step, unit * MSTEPS + 4)
                        nc.vector.tensor_tensor(cols[2], negrest[:], cols[1], ALU.subtract).then_inc(max_step, 1)
                        dve.wait_ge(max_step, unit * MSTEPS + 5)
                        dve.sem_inc(max_ready, 1)
                        for g in range(2):
                            for ch in range(2):
                                dve.wait_ge(ab_full, qbase + k + 1)
                                nc.vector.tensor_copy(qxm[:, g, ch * CH:ch * CH + CH], ab[:, k % 2]).then_inc(ab_done, 1)
                                k += 1
                        for ch in range(2):
                            nst = sum(1 for x in steps if x[0] <= ch)
                            dve.wait_ge(pv_done, unit * NST + nst + RING)
                            nc.vector.tensor_copy(osum[:], ob[:]).then_inc(o_copied, 1)
                            dve.wait_ge(sum_ready, unit * 2 + ch + 1)
                            nc.vector.reciprocal(rsum[:], mb[:]).then_inc(r_ready, 1)
                            dve.wait_ge(r_ready, unit * 2 + ch + 1)
                            nc.vector.tensor_tensor(ctxt[:, ds(q, 1), ch * CH:ch * CH + CH].rearrange("p a n -> p (a n)"),
                                                    osum[:], rsum[:], ALU.mult).then_inc(ctx_ready, 1)
                            dve.wait_ge(ctx_ready, unit * 2 + ch + 2)
                    for ch in range(2):
                        k = BJOBS - 2 + ch
                        dve.wait_ge(ab_full, base + k + 1)
                        cols = ds(b * SEQ + ch * CH, CH)
                        nc.vector.tensor_tensor(res[:, cols], res[:, cols], ab[:, k % 2], ALU.add).then_inc(ab_done, 1)


def headwise_attention(nc, name, w, c, xn, res, latent=False):
    NB = TOK // P
    HH = HEADS * HEADS
    with ExitStack() as ctx:
        s = Scope(nc, ctx, name)
        wqkv = s.sb("wqkv", [P, D if latent else 3 * D])
        bqkv = s.sb("bqkv", [P, 3 * D])
        wo, bo = s.sb("wo", [P, D]), s.sb("bo", [P, 1])
        ident = s.sb("ident", [P, P])
        loads = [(wqkv[:], w["wqkv"]), (bqkv[:], w["bqkv"].broadcast_to([P, 3 * D])), (wo[:], w["wo"]),
                 (bo[:], w["bo"]), (ident[:], c["ident"])]
        if latent:
            RANK = w["wdown"].shape[1]
            wdown, bdown, wup = s.sb("wdown", [P, RANK]), s.sb("bdown", [RANK, 1]), s.sb("wup", [RANK, 2 * D])
            cos, sin = s.sb("cos", [P, TPB, HD]), s.sb("sin", [P, TPB, HD])
            loads += [(wdown[:], w["wdown"]), (bdown[:], w["bdown"]), (wup[:], w["wup"]),
                      (cos[:], c["cos8"]), (sin[:], c["sin8"])]
            latb = s.sb("latb", [RANK, 2, P])
            cosqk, sinqk = s.sb("cosqk", [P, 2, 2 * D]), s.sb("sinqk", [P, 2, 2 * D])
            roped = s.sb("roped", [P, 2, 2 * D])
            lat_ps = s.ps("lat_ps", [RANK, 2, CH])
        load_phase(nc, name + "_load", loads)

        xblk = s.sb("xblk", [P, 2, P])
        qkv = s.sb("qkv", [P, 2, 3 * D])
        prod = s.sb("prod", [P, 2, HEADS, HEADS, HD])
        score = s.sb("score", [P, 2, HEADS, HEADS])
        top = s.sb("top", [P, 2, HEADS])
        less = s.sb("less", [P, 2, HEADS, HEADS])
        ex = s.sb("ex", [P, 2, HEADS, HEADS])
        total = s.sb("total", [P, 2, HEADS])
        inv = s.sb("inv", [P, 2, HEADS])
        prob = s.sb("prob", [P, 2, HEADS, HEADS])
        pv = s.sb("pv", [P, 2, HEADS, HEADS, HD])
        ct = s.sb("ct", [P, 2, P])
        qkv_ps = s.ps("qkv_ps", [P, 2, CH])
        ct_ps = s.ps("ct_ps", [P, CH])
        out_ps = s.ps("out_ps", [P, CH])

        x_copied, qkv_full, qkv_read = s.sem("x_copied"), s.sem("qkv_full"), s.sem("qkv_read")
        prod_ready, scored, topped = s.sem("prod_ready"), s.sem("scored"), s.sem("topped")
        less_ready, ex_ready, summed, inverted = (s.sem("less_ready"), s.sem("ex_ready"), s.sem("summed"),
                                                  s.sem("inverted"))
        prob_ready, pv_ready = s.sem("prob_ready"), s.sem("pv_ready")
        ct_full, ct_copied, out_full, out_added = (s.sem("ct_full"), s.sem("ct_copied"), s.sem("out_full"),
                                                   s.sem("out_added"))
        if latent:
            lat_full, lat_ready, rope_part, rope_done = (s.sem("lat_full"), s.sem("lat_ready"),
                                                         s.sem("rope_part"), s.sem("rope_done"))

        def q_of(i):
            return roped[:, i % 2, 0:D] if latent else qkv[:, i % 2, 0:D]

        def k_of(i):
            return roped[:, i % 2, D:2 * D] if latent else qkv[:, i % 2, D:2 * D]

        def blocks(engine, body):
            body(0, 0, 2)
            body(1, 1, 2)
            with engine.Fori(1, (NB - 2) // 2) as n:
                body(n * 2, 0, 2)
                body(n * 2 + 1, 1, 2)
            body(NB - 2, 0, 1)
            body(NB - 1, 1, 0)

        with nc.Block() as block:
            @block.tensor
            def _(pe):
                def project(i, sl):
                    pe.wait_ge(x_copied, i + 1)
                    pe.wait_ge(qkv_read, i + 1)
                    if latent:
                        nc.tensor.matmul(lat_ps[:, sl, 0:P], wdown[:], xblk[:, sl], start=True,
                                         stop=True).then_inc(lat_full, 1)
                    mm = nc.tensor.matmul(qkv_ps[:, sl, 0:wqkv.shape[1]], xblk[:, sl], wqkv[:], start=True,
                                          stop=True)
                    if not latent:
                        mm.then_inc(qkv_full, 1)

                def project_up(i, sl):
                    if latent:
                        pe.wait_ge(lat_ready, i + 1)
                        nc.tensor.matmul(qkv_ps[:, sl, D:3 * D], latb[:, sl], wup[:], start=True,
                                         stop=True).then_inc(qkv_full, 1)

                for i in range(2):
                    project(i, i)
                    project_up(i, i)

                def body(i, sl, left):
                    if left == 2:
                        project(i + 2, sl)
                    pe.wait_ge(pv_ready, i + 1)
                    pe.wait_ge(ct_copied, i + 1)
                    for g in range(HEADS):
                        mm = nc.tensor.matmul(ct_ps[:, 0:P], pv[:, sl, g].rearrange("p h d -> p (h d)"), ident[:],
                                              start=g == 0, stop=g == HEADS - 1)
                    mm.then_inc(ct_full, 1)
                    if left == 2:
                        project_up(i + 2, sl)
                    pe.wait_ge(ct_copied, i + 2)
                    pe.wait_ge(out_added, i + 1)
                    nc.tensor.matmul(out_ps[:, 0:P], wo[:], ct[:, sl], start=True, stop=True).then_inc(out_full, 1)

                blocks(nc.tensor, body)

            @block.scalar
            def _(act):
                act.sem_inc(ct_copied, 1)

                def latent_copy(i, sl):
                    if latent:
                        act.wait_ge(lat_full, i + 1)
                        nc.scalar.activation(latb[:, sl], lat_ps[:, sl, 0:P], ACT.Identity,
                                             bias=bdown[:]).then_inc(lat_ready, 1)

                for i in range(2):
                    latent_copy(i, i)

                def body(i, sl, left):
                    act.wait_ge(less_ready, i + 1)
                    nc.scalar.activation(ex[:, sl], less[:, sl], ACT.Exp, scale=SCALE8).then_inc(ex_ready, 1)
                    if left == 2:
                        latent_copy(i + 2, sl)
                    act.wait_ge(ct_full, i + 1)
                    nc.scalar.activation(ct[:, sl], ct_ps[:, 0:P], ACT.Copy).then_inc(ct_copied, 1)

                blocks(nc.scalar, body)

            @block.gpsimd
            def _(pool):
                def products(i, sl):
                    pool.wait_ge(qkv_read, i + 3)
                    if latent:
                        v4 = qkv[:, sl, 0:2 * D].rearrange("p (n a b) -> p n a b", a=2, b=HD // 2)
                        s4 = sinqk[:, sl].rearrange("p (n a b) -> p n a b", a=2, b=HD // 2)
                        n_heads = 2 * HEADS
                        half = HD // 2
                        pool.wait_ge(scored, i + 1)
                        tab = lambda t, lo, hi: (t[:, ds(i % TPB, 1) if not isinstance(i, int)
                                                   else slice(i % TPB, i % TPB + 1), lo:hi]
                                                 .broadcast_to([P, n_heads, hi - lo]))
                        nc.gpsimd.tensor_tensor(cosqk[:, sl].rearrange("p (n b) -> p n b", b=HD),
                                                qkv[:, sl, 0:2 * D].rearrange("p (n b) -> p n b", b=HD),
                                                tab(cos, 0, HD), ALU.mult).then_inc(rope_part, 1)
                        nc.gpsimd.tensor_tensor(s4[:, :, 0], v4[:, :, 1], tab(sin, 0, half),
                                                ALU.mult).then_inc(rope_part, 1)
                        nc.gpsimd.tensor_tensor(s4[:, :, 1], v4[:, :, 0], tab(sin, half, HD),
                                                ALU.mult).then_inc(rope_part, 1)
                        pool.wait_ge(rope_part, i * 3 + 3)
                        nc.gpsimd.tensor_tensor(roped[:, sl], cosqk[:, sl], sinqk[:, sl],
                                                ALU.add).then_inc(rope_done, 1)
                        pool.wait_ge(rope_done, i + 1)
                    q3 = q_of(sl).rearrange("p (h a d) -> p h a d", a=1, d=HD).broadcast_to([P, HEADS, HEADS, HD])
                    k3 = k_of(sl).rearrange("p (a g d) -> p a g d", a=1, d=HD).broadcast_to([P, HEADS, HEADS, HD])
                    nc.gpsimd.tensor_tensor(prod[:, sl], q3, k3, ALU.mult).then_inc(prod_ready, 1)

                products(0, 0)

                def body(i, sl, left):
                    pool.wait_ge(topped, i + 1)
                    nc.gpsimd.tensor_tensor(less[:, sl], score[:, sl],
                                            top[:, sl].rearrange("p (h a) -> p h a", a=1)
                                            .broadcast_to([P, HEADS, HEADS]), ALU.subtract).then_inc(less_ready, 1)
                    if left:
                        products(i + 1, 1 - sl)

                blocks(nc.gpsimd, body)

            @block.vector
            def _(dve):
                dve.sem_inc(qkv_read, 2)
                dve.sem_inc(scored, 2)
                dve.sem_inc(out_added, 1)

                def bring(i, sl):
                    nc.vector.tensor_scalar(xblk[:, sl], xn[:, ds(i * P, P)], 1.0, None,
                                            ALU.mult).then_inc(x_copied, 1)

                def evacuate(i, sl):
                    dve.wait_ge(qkv_full, i + 1)
                    nc.vector.tensor_tensor(qkv[:, sl], qkv_ps[:, sl, 0:3 * D], bqkv[:], ALU.add).then_inc(qkv_read, 1)

                def store(i):
                    dve.wait_ge(out_full, i + 1)
                    cols = ds(i * P, P)
                    nc.vector.scalar_tensor_tensor(out=res[:, cols], in0=out_ps[:, 0:P], scalar=bo[:],
                                                   in1=res[:, cols], op0=ALU.add, op1=ALU.add).then_inc(out_added, 1)

                bring(0, 0)
                bring(1, 1)
                evacuate(0, 0)

                def body(i, sl, left):
                    dve.wait_ge(prod_ready, i + 1)
                    nc.vector.tensor_reduce(score[:, sl], prod[:, sl], AX.X, ALU.add).then_inc(scored, 1)
                    dve.wait_ge(scored, i + 3)
                    nc.vector.tensor_reduce(top[:, sl], score[:, sl], AX.X, ALU.max).then_inc(topped, 1)
                    if left:
                        evacuate(i + 1, 1 - sl)
                    if left == 2:
                        bring(i + 2, sl)
                    if not (isinstance(i, int) and i == 0):
                        store(i - 1)
                    dve.wait_ge(ex_ready, i + 1)
                    nc.vector.tensor_reduce(total[:, sl], ex[:, sl], AX.X, ALU.add).then_inc(summed, 1)
                    dve.wait_ge(summed, i + 1)
                    nc.vector.reciprocal(inv[:, sl], total[:, sl]).then_inc(inverted, 1)
                    dve.wait_ge(inverted, i + 1)
                    nc.vector.tensor_tensor(prob[:, sl], ex[:, sl],
                                            inv[:, sl].rearrange("p (h a) -> p h a", a=1)
                                            .broadcast_to([P, HEADS, HEADS]), ALU.mult).then_inc(prob_ready, 1)
                    dve.wait_ge(prob_ready, i + 1)
                    pgh = (prob[:, sl].rearrange("p h (g a) -> p g h a", a=1)
                           .broadcast_to([P, HEADS, HEADS, HD]))
                    vgd = (qkv[:, sl, 2 * D:3 * D].rearrange("p (g a d) -> p g a d", a=1, d=HD)
                           .broadcast_to([P, HEADS, HEADS, HD]))
                    nc.vector.tensor_tensor(pv[:, sl], pgh, vgd, ALU.mult).then_inc(pv_ready, 1)

                blocks(nc.vector, body)
                store(NB - 1)


EXPERTS, HID = 8, 256
NBLK = TOK // P


def route(nc, name, wg, c, xn, kind, rows, rows_f=None):
    CAP = TOK // EXPERTS
    wide = 1 if kind == "switch" else EXPERTS
    with ExitStack() as ctx:
        s = Scope(nc, ctx, name)
        gate = s.sb("gate", [P, EXPERTS])
        rev = s.sb("rev", [P, 1, EXPERTS])
        identb = s.sb("identb", [P, P], BF16)
        loads = [(gate[:], wg), (rev[:], c["rev"]), (identb[:], c["identb"])]
        if kind == "switch":
            tri, onesb = s.sb("tri", [P, P], BF16), s.sb("onesb", [P, P], BF16)
            loads += [(tri[:], c["tri"]), (onesb[:], c["onesb"])]
        load_phase(nc, name + "_load", loads)

        def field(n, dt=F32):
            return s.sb(n, [P, NBLK, EXPERTS], dt)

        prob, less, a, b2, hot1, hot2 = (field("prob"), field("less"), field("a"), field("b2"), field("hot1"),
                                         field("hot2"))
        hotb = field("hotb", BF16)
        top, inv = s.sb("top", [P, NBLK]), s.sb("inv", [P, NBLK])
        wt = s.sb("wt", [P, NBLK, wide])
        rest = s.sb("rest", [P, NBLK, wide])
        parts = s.sb("parts", [P, NBLK, 3, wide], BF16)
        logit_ps = s.ps("logit_ps", [P, NBLK, EXPERTS])
        count_ps = s.ps("count_ps", [P, NBLK, EXPERTS])
        row_ps = s.ps("row_ps", [3 * wide, 2, CH])
        logits, less_ready, exped, step = s.sem("logits"), s.sem("less_ready"), s.sem("exped"), s.sem("step")
        hot_ready, counted, parted = s.sem("hot_ready"), s.sem("counted"), s.sem("parted")
        row_full, row_copied = s.sem("row_full"), s.sem("row_copied")
        rev_b = rev[:].broadcast_to([P, NBLK, EXPERTS])

        def over(t):
            return t[:].rearrange("p (n a) -> p n a", a=1).broadcast_to([P, NBLK, EXPERTS])

        with nc.Block() as block:
            @block.tensor
            def _(pe):
                for i in range(NBLK):
                    mm = nc.tensor.matmul(logit_ps[:, i], xn[:, i * P:i * P + P], gate[:], start=True, stop=True)
                mm.then_inc(logits, 1)
                if kind == "switch":
                    pe.wait_ge(hot_ready, 1)
                    nc.tensor.matmul(count_ps[:].rearrange("p n e -> p (n e)"), tri[:],
                                     hotb[:].rearrange("p n e -> p (n e)"), start=True, stop=False,
                                     skip_group_check=True)
                    for i in range(NBLK - 1):
                        mm = nc.tensor.matmul(count_ps[:, i + 1:], onesb[:],
                                              hotb[:, i:i + 1].broadcast_to([P, NBLK - 1 - i, EXPERTS]),
                                              start=False, stop=i == NBLK - 2, skip_group_check=True)
                    mm.then_inc(counted, 1)
                pe.wait_ge(parted, 1)
                for n in range(NCH):
                    if n >= 2:
                        pe.wait_ge(row_copied, n - 1)
                    for j in range(4):
                        mm = nc.tensor.matmul(row_ps[:, n % 2, j * P:j * P + P],
                                              parts[:, n * 4 + j].rearrange("p l e -> p (l e)"), identb[:],
                                              start=True, stop=True)
                    mm.then_inc(row_full, 1)

            @block.scalar
            def _(act):
                act.wait_ge(less_ready, 1)
                nc.scalar.activation(a[:], less[:], ACT.Exp).then_inc(exped, 1)
                for n in range(NCH):
                    act.wait_ge(row_full, n + 1)
                    if rows_f is not None:
                        nc.scalar.activation(rows_f[:, n * CH:n * CH + CH], row_ps[:, n % 2], ACT.Copy)
                    nc.scalar.activation(rows[:, n * CH:n * CH + CH], row_ps[:, n % 2],
                                         ACT.Copy).then_inc(row_copied, 1)

            @block.vector
            def _(dve):
                k = 0

                def chained(instruction):
                    nonlocal k
                    k += 1
                    instruction.then_inc(step, 1)
                    dve.wait_ge(step, k)

                dve.wait_ge(logits, 1)
                chained(nc.vector.tensor_reduce(top[:], logit_ps[:], AX.X, ALU.max))
                nc.vector.tensor_tensor(less[:], logit_ps[:], over(top), ALU.subtract).then_inc(less_ready, 1)
                dve.wait_ge(exped, 1)
                chained(nc.vector.tensor_reduce(top[:], a[:], AX.X, ALU.add))
                chained(nc.vector.reciprocal(inv[:], top[:]))
                chained(nc.vector.tensor_tensor(prob[:], a[:], over(inv), ALU.mult))

                def first_max(src, hot):
                    chained(nc.vector.tensor_reduce(top[:], src[:], AX.X, ALU.max))
                    chained(nc.vector.tensor_tensor(b2[:], src[:], over(top), ALU.is_equal))
                    chained(nc.vector.tensor_tensor(b2[:], b2[:], rev_b, ALU.mult))
                    chained(nc.vector.tensor_reduce(top[:], b2[:], AX.X, ALU.max))
                    chained(nc.vector.tensor_tensor(hot[:], b2[:], over(top), ALU.is_equal))

                first_max(prob, hot1)
                if kind == "switch":
                    nc.vector.tensor_copy(hotb[:], hot1[:]).then_inc(hot_ready, 1)
                    dve.wait_ge(counted, 1)
                    chained(nc.vector.scalar_tensor_tensor(out=hot2[:], in0=count_ps[:], scalar=float(CAP),
                                                           in1=hot1[:], op0=ALU.is_le, op1=ALU.mult))
                    chained(nc.vector.tensor_tensor(less[:], prob[:], hot2[:], ALU.mult))
                    chained(nc.vector.tensor_reduce(wt[:].rearrange("p n e -> p (n e)"), less[:], AX.X, ALU.add))
                else:
                    chained(nc.vector.scalar_tensor_tensor(out=less[:], in0=hot1[:], scalar=-2.0, in1=prob[:],
                                                           op0=ALU.mult, op1=ALU.add))
                    first_max(less, hot2)
                    chained(nc.vector.tensor_tensor(hot1[:], hot1[:], hot2[:], ALU.add))
                    chained(nc.vector.tensor_tensor(wt[:], prob[:], hot1[:], ALU.mult))
                    if kind == "two_normed":
                        chained(nc.vector.tensor_reduce(top[:], wt[:], AX.X, ALU.add))
                        chained(nc.vector.tensor_scalar(top[:], top[:], 1e-9, None, ALU.add))
                        chained(nc.vector.reciprocal(inv[:], top[:]))
                        chained(nc.vector.tensor_tensor(wt[:], wt[:], over(inv), ALU.mult))
                chained(nc.vector.tensor_copy(parts[:, :, 0], wt[:]))
                chained(nc.vector.tensor_tensor(rest[:], wt[:], parts[:, :, 0], ALU.subtract))
                chained(nc.vector.tensor_copy(parts[:, :, 1], rest[:]))
                nc.vector.tensor_tensor(parts[:, :, 2], rest[:], parts[:, :, 1], ALU.subtract).then_inc(parted, 1)


def experts(nc, name, w, c, xn, res, biased):
    KR = 3 * EXPERTS
    with ExitStack() as ctx:
        s = Scope(nc, ctx, name)
        rows = s.sb("rows", [KR, TOK], BF16)
        rows_f = s.sb("rows_f", [KR, TOK]) if biased else None
        w1, w3 = s.sb("w1", [P, EXPERTS, HID]), s.sb("w3", [P, EXPERTS, HID])
        w2 = s.sb("w2", [P, EXPERTS, 2, D])
        spread = s.sb("spread", [KR, EXPERTS, P], BF16)
        loads = [(w1[:], w["w1"].rearrange("e d h -> d e h")), (w3[:], w["w3"].rearrange("e d h -> d e h")),
                 (w2[:], w["w2"].rearrange("e (f p) d -> p e f d", p=P)), (spread[:], c["spread"])]
        if biased:
            b13, b2 = s.sb("b13", [P, 2, EXPERTS, 2]), s.sb("b2", [KR, D])
            loads += [(b13[:], w["b13"]), (b2[:], w["b2"])]
        load_phase(nc, name + "_load", loads)
        route(nc, name + "r", w["gate"], c, xn, "two_normed" if biased else "two", rows, rows_f)

        act1 = s.sb("act1", [P, 2, CH])
        mixed = s.sb("mixed", [P, 2, CH])
        weighed = s.sb("weighed", [P, 2, CH])
        wb = s.sb("wb", [P, 2, CH])
        h1, h3 = s.ps("h1", [P, 2, CH]), s.ps("h3", [P, 2, CH])
        wb_ps, y_ps = s.ps("wb_ps", [P, 2, CH]), s.ps("y_ps", [P, CH])
        h_full, act_done, mixed_done, weighed_done = (s.sem("h_full"), s.sem("act_done"), s.sem("mixed_done"),
                                                      s.sem("weighed_done"))
        wb_full, wb_copied, used, y_full, y_added = (s.sem("wb_full"), s.sem("wb_copied"), s.sem("used"),
                                                     s.sem("y_full"), s.sem("y_added"))
        J = 2 * EXPERTS

        with nc.Block() as block:
            @block.tensor
            def _(pe):
                with nc.tensor.Fori(0, NCH) as n:
                    cols = ds(n * CH, CH)

                    def down(j):
                        e, f = j // 2, j % 2
                        pe.wait_ge(weighed_done, n * J + j + 3)
                        if j == 0:
                            pe.wait_ge(y_added, n + 1)
                        nc.tensor.matmul(y_ps[:], w2[:, e, f], weighed[:, f], start=j == 0,
                                         stop=j == J - 1).then_inc(used, 1)
                        if j == 0 and biased:
                            nc.tensor.matmul(y_ps[:], b2[:], rows_f[:, cols], start=False, stop=False)

                    for j in range(J):
                        e, f = j // 2, j % 2
                        if f == 0:
                            pe.wait_ge(wb_copied, n * EXPERTS + e + 1)
                        pe.wait_ge(mixed_done, n * J + j + 1)
                        nc.tensor.matmul(h1[:, f], w1[:, e, f * P:f * P + P], xn[:, cols], start=True, stop=True)
                        nc.tensor.matmul(h3[:, f], w3[:, e, f * P:f * P + P], xn[:, cols], start=True,
                                         stop=True).then_inc(h_full, 1)
                        if f == 0:
                            nc.tensor.matmul(wb_ps[:, e % 2], spread[:, e], rows[:, cols], start=True,
                                             stop=True).then_inc(wb_full, 1)
                        if j >= 2:
                            down(j - 2)
                    down(J - 2)
                    down(J - 1)
                    pe.wait_ge(used, n * J + J + 2)
                    pe.sem_inc(y_full, 1)

            @block.scalar
            def _(act):
                act.sem_inc(wb_copied, 2)
                with nc.scalar.Fori(0, NCH) as n:
                    for j in range(J):
                        e, f = j // 2, j % 2
                        act.wait_ge(h_full, n * J + j + 1)
                        act.wait_ge(mixed_done, n * J + j + 1)
                        bias = dict(bias=b13[:, 0, e, f:f + 1]) if biased else {}
                        nc.scalar.activation(act1[:, f], h1[:, f], ACT.Silu, **bias).then_inc(act_done, 1)
                        if f == 0:
                            act.wait_ge(wb_full, n * EXPERTS + e + 1)
                            act.wait_ge(weighed_done, n * J + j + 1)
                            nc.scalar.activation(wb[:, e % 2], wb_ps[:, e % 2], ACT.Copy).then_inc(wb_copied, 1)

            @block.vector
            def _(dve):
                dve.sem_inc(mixed_done, 2)
                dve.sem_inc(y_added, 1)
                dve.sem_inc(used, 2)
                with nc.vector.Fori(0, NCH) as n:
                    for j in range(J):
                        e, f = j // 2, j % 2
                        dve.wait_ge(act_done, n * J + j + 1)
                        dve.wait_ge(weighed_done, n * J + j + 1)
                        if biased:
                            nc.vector.scalar_tensor_tensor(out=mixed[:, f], in0=h3[:, f],
                                                           scalar=b13[:, 1, e, f:f + 1], in1=act1[:, f],
                                                           op0=ALU.add, op1=ALU.mult).then_inc(mixed_done, 1)
                        else:
                            nc.vector.tensor_tensor(mixed[:, f], h3[:, f], act1[:, f],
                                                    ALU.mult).then_inc(mixed_done, 1)
                    dve.wait_ge(y_full, n + 1)
                    cols = ds(n * CH, CH)
                    nc.vector.tensor_tensor(res[:, cols], res[:, cols], y_ps[:], ALU.add).then_inc(y_added, 1)

            @block.gpsimd
            def _(pool):
                pool.sem_inc(weighed_done, 2)
                with nc.gpsimd.Fori(0, NCH) as n:
                    for j in range(J):
                        e, f = j // 2, j % 2
                        pool.wait_ge(wb_copied, n * EXPERTS + e + 3)
                        pool.wait_ge(mixed_done, n * J + j + 3)
                        pool.wait_ge(used, n * J + j + 1)
                        nc.gpsimd.tensor_tensor(weighed[:, f], mixed[:, f], wb[:, e % 2],
                                                ALU.mult).then_inc(weighed_done, 1)


def switch_ffn(nc, name, w, c, xn, res):
    with ExitStack() as ctx:
        s = Scope(nc, ctx, name)
        rows = s.sb("rows", [3, TOK], BF16)
        we, be, ones3 = s.sb("we", [P, D]), s.sb("be", [P, 1]), s.sb("ones3", [3, P], BF16)
        load_phase(nc, name + "_load", [(we[:], w["we"]), (be[:], w["be"]), (ones3[:], c["onesb"][0:3])])
        route(nc, name + "r", w["wg"], c, xn, "switch", rows)
        y = s.sb("y", [P, 2, CH])
        gated = s.sb("gated", [P, 2, CH])
        y_ps, g_ps = s.ps("y_ps", [P, 2, CH]), s.ps("g_ps", [P, 2, CH])
        full, y_ready, gated_done, added = s.sem("full"), s.sem("y_ready"), s.sem("gated_done"), s.sem("added")
        with nc.Block() as block:
            @block.tensor
            def _(pe):
                with nc.tensor.Fori(0, NCH // 2) as n:
                    for i in range(2):
                        cols = ds(n * 2 * CH + i * CH, CH)
                        pe.wait_ge(gated_done, n * 2 + i + 1)
                        nc.tensor.matmul(y_ps[:, i], we[:], xn[:, cols], start=True, stop=True)
                        nc.tensor.matmul(g_ps[:, i], ones3[:], rows[:, cols], start=True, stop=True).then_inc(full, 1)

            @block.scalar
            def _(act):
                with nc.scalar.Fori(0, NCH // 2) as n:
                    for i in range(2):
                        act.wait_ge(full, n * 2 + i + 1)
                        act.wait_ge(gated_done, n * 2 + i + 1)
                        nc.scalar.activation(y[:, i], y_ps[:, i], ACT.Identity, bias=be[:]).then_inc(y_ready, 1)

            @block.vector
            def _(dve):
                dve.sem_inc(gated_done, 2)
                with nc.vector.Fori(0, NCH // 2) as n:
                    for i in range(2):
                        cols = ds(n * 2 * CH + i * CH, CH)
                        dve.wait_ge(y_ready, n * 2 + i + 1)
                        nc.vector.tensor_tensor(gated[:, i], y[:, i], g_ps[:, i], ALU.mult).then_inc(gated_done, 1)
                        dve.wait_ge(gated_done, n * 2 + i + 3)
                        nc.vector.tensor_tensor(res[:, cols], res[:, cols], gated[:, i], ALU.add).then_inc(added, 1)
                        dve.wait_ge(added, n * 2 + i + 1)


def constants_experts(c):
    bf = np.dtype("bfloat16")
    c["rev"] = np.tile(np.arange(EXPERTS, 0, -1, dtype=np.float32), (P, 1)).reshape(P, 1, EXPERTS)
    i, j = np.arange(P)[:, None], np.arange(P)[None, :]
    c["tri"] = (i <= j).astype(bf)
    c["onesb"] = np.ones((P, P), bf)
    spread = np.zeros((3, EXPERTS, EXPERTS, P), np.float32)
    for e in range(EXPERTS):
        spread[:, e, e] = 1
    c["spread"] = spread.reshape(3 * EXPERTS, EXPERTS, P).astype(bf)


def layout_experts(I, t):
    t["f1_gate"] = I["L1_ffn_gate_w"].T
    t["f1_w1"], t["f1_w3"], t["f1_w2"] = I["L1_ffn_w1"], I["L1_ffn_w3"], I["L1_ffn_w2"]
    t["f2_gate"] = I["L2_ffn_router_w"].T
    t["f2_w1"], t["f2_w3"], t["f2_w2"] = I["L2_ffn_gate_w"], I["L2_ffn_up_w"], I["L2_ffn_down_w"]
    b13 = np.stack([I["L2_ffn_gate_b"], I["L2_ffn_up_b"]]).reshape(2, EXPERTS, 2, P)
    t["f2_b13"] = b13.transpose(3, 0, 1, 2)
    t["f2_b2"] = np.concatenate([I["L2_ffn_down_b"]] * 3)


def retention(nc, name, w, c, xn, res, eps_col):
    with ExitStack() as ctx:
        s = Scope(nc, ctx, name)
        wqk = s.sb("wqk", [P, 4, D])
        wv, wgate, wproj = s.sb("wv", [P, D]), s.sb("wgate", [P, D]), s.sb("wproj", [P, D])
        gn = s.sb("gn", [P, 2])
        rope = s.sb("rope", [P, 4, SEQ])
        decay = s.sb("decay", [P, HEADS, P])
        dq, dk = s.sb("dq", [P, 1, P]), s.sb("dk", [P, 1, P])
        dchunk = s.sb("dchunk", [P, 1])
        headmask = s.sb("headmask", [P, HEADS])
        blockmask = s.sb("blockmask", [P, 1, P])
        headmean = s.sb("headmean", [P, P])
        ident = s.sb("ident", [P, P])
        load_phase(nc, name + "_load", [
            (wqk[:], w["wqk"]), (wv[:], w["wv"]), (wgate[:], w["wgate"]), (wproj[:], w["wproj"]), (gn[:], w["gn"]),
            (rope[:], c["ret_rope"]), (decay[:], c["ret_decay"]), (dq[:], c["ret_dq"]), (dk[:], c["ret_dk"]),
            (dchunk[:], c["ret_dchunk"]), (headmask[:], c["headmask"]), (blockmask[:], c["blockmask"]),
            (headmean[:], c["headmean"]), (ident[:], c["ident"])])

        xb = s.sb("xb", [P, SEQ])
        qk = s.sb("qk", [P, 4, SEQ])
        qr, kr = s.sb("qr", [P, SEQ]), s.sb("kr", [P, SEQ])
        qdec, kdec = s.sb("qdec", [P, TPB, P]), s.sb("kdec", [P, TPB, P])
        kt = s.sb("kt", [P, TPB, P])
        v = s.sb("v", [P, TPB, P])
        kv = s.sb("kv", [P, TPB - 1, P])
        state = s.sb("state", [P, TPB, P])
        km = s.sb("km", [P, 2, SEQ])
        sd = s.sb("sd", [P, 2, TPB, P])
        gate = s.sb("gate", [P, SEQ])
        yt = s.sb("yt", [P, TPB, P])
        yf, cen, z, zg = s.sb("yf", [P, SEQ]), s.sb("cen", [P, SEQ]), s.sb("z", [P, SEQ]), s.sb("zg", [P, SEQ])
        sq = s.sb("sq", [P, SEQ])
        stat = s.sb("stat", [P, 6])
        ab = s.ps("ab", [P, 2, CH])
        st = s.ps("st", [P, 2, TPB, P])
        y_ps = s.ps("y_ps", [P, TPB, P])

        copied, ab_full, ab_done = s.sem("copied"), s.sem("ab_full"), s.sem("ab_done")
        roped, decayed = s.sem("roped"), s.sem("decayed")
        gate_full, gate_done = s.sem("gate_full"), s.sem("gate_done")
        kt_full, kt_copied, kv_full, kv_copied, state_step = (s.sem("kt_full"), s.sem("kt_copied"), s.sem("kv_full"),
                                                              s.sem("kv_copied"), s.sem("state_step"))
        km_ready, st_full, sd_ready, y_step, y_full, y_copied = (s.sem("km_ready"), s.sem("st_full"),
                                                                 s.sem("sd_ready"), s.sem("y_step"),
                                                                 s.sem("y_full"), s.sem("y_copied"))
        stat_step, squared, rooted, z_ready, zg_ready, added = (s.sem("stat_step"), s.sem("squared"), s.sem("rooted"),
                                                                s.sem("z_ready"), s.sem("zg_ready"), s.sem("added"))
        zeroed = s.sem("zeroed")
        JOBS = 16
        V_JOB, YT_JOB, MEAN_JOB, VAR_JOB, OUT_JOB = 8, 10, 12, 13, 14
        STATS = 7

        with nc.Block() as block:
            @block.tensor
            def _(pe):
                with nc.tensor.Fori(0, BATCH) as b:
                    base = b * JOBS

                    def take(k):
                        pe.wait_ge(ab_done, base + k + 1)
                        return k % 2

                    pe.wait_ge(copied, b + 1)
                    for i in range(4):
                        for ch in range(2):
                            sl = take(2 * i + ch)
                            nc.tensor.matmul(ab[:, sl], wqk[:, i], xb[:, ch * CH:ch * CH + CH], start=True,
                                             stop=True).then_inc(ab_full, 1)
                    for half in range(2):
                        sl = take(V_JOB + half)
                        for j in range(4):
                            t = half * 4 + j
                            mm = nc.tensor.matmul(ab[:, sl, j * P:j * P + P], xb[:, t * P:t * P + P], wv[:],
                                                  start=True, stop=True)
                        mm.then_inc(ab_full, 1)
                    pe.wait_ge(y_copied, b + 1)
                    for ch in range(2):
                        mm = nc.tensor.matmul(y_ps[:, 4 * ch:4 * ch + 4].rearrange("p a b -> p (a b)"), wgate[:],
                                              xb[:, ch * CH:ch * CH + CH], start=True, stop=True)
                    mm.then_inc(gate_full, 1)
                    pe.wait_ge(decayed, b * 2 + 2)
                    for t in range(TPB):
                        mm = nc.tensor.matmul(st[:, 0, t], kdec[:, t], ident[:], start=True, stop=True)
                    mm.then_inc(kt_full, 1)
                    pe.wait_ge(kt_copied, b + 1)
                    pe.wait_ge(ab_done, base + V_JOB + 2 + 2)
                    for t in range(TPB - 1):
                        mm = nc.tensor.matmul(st[:, 1, t], kt[:, t], v[:, t], start=True, stop=True)
                    mm.then_inc(kv_full, 1)
                    pe.wait_ge(state_step, b * (TPB - 1) + TPB - 1)
                    pe.wait_ge(gate_done, b + 1)
                    for t in range(TPB):
                        nc.tensor.matmul(y_ps[:, t], qdec[:, t], state[:, t], start=t % 4 == 0, stop=False,
                                         skip_group_check=True)

                    def within(h):
                        pe.wait_ge(sd_ready, b * HEADS + h + 3)
                        for t in range(TPB):
                            mm = nc.tensor.matmul(y_ps[:, t, h * HD:h * HD + HD], sd[:, h % 2, t],
                                                  v[:, t, h * HD:h * HD + HD], start=False, stop=h == HEADS - 1,
                                                  skip_group_check=True)
                        mm.then_inc(y_step, 1)

                    for h in range(HEADS):
                        pe.wait_ge(km_ready, b * HEADS + h + 1)
                        pe.wait_ge(sd_ready, b * HEADS + h + 1)
                        for t in range(TPB):
                            mm = nc.tensor.matmul(st[:, h % 2, t], km[:, h % 2, t * P:t * P + P],
                                                  qr[:, t * P:t * P + P], start=True, stop=True)
                        mm.then_inc(st_full, 1)
                        if h:
                            within(h - 1)
                    within(HEADS - 1)
                    pe.wait_ge(y_copied, b + 2)
                    for half in range(2):
                        sl = take(YT_JOB + half)
                        for j in range(4):
                            mm = nc.tensor.matmul(ab[:, sl, j * P:j * P + P], yt[:, half * 4 + j], ident[:],
                                                  start=True, stop=True)
                        mm.then_inc(ab_full, 1)
                    pe.wait_ge(stat_step, b * STATS + 1)
                    nc.tensor.matmul(ab[:, take(MEAN_JOB), 0:1], headmean[:], stat[:, 0:1], start=True,
                                     stop=True).then_inc(ab_full, 1)
                    pe.wait_ge(squared, b + 1)
                    nc.tensor.matmul(ab[:, take(VAR_JOB), 0:1], headmean[:], stat[:, 1:2], start=True,
                                     stop=True).then_inc(ab_full, 1)
                    pe.wait_ge(zg_ready, b + 1)
                    for ch in range(2):
                        sl = take(OUT_JOB + ch)
                        nc.tensor.matmul(ab[:, sl], wproj[:], zg[:, ch * CH:ch * CH + CH], start=True,
                                         stop=True).then_inc(ab_full, 1)

            @block.scalar
            def _(act):
                act.sem_inc(y_copied, 1)
                with nc.scalar.Fori(0, BATCH) as b:
                    act.wait_ge(gate_full, b + 1)
                    nc.scalar.activation(gate[:], y_ps[:].rearrange("p a b -> p (a b)"), ACT.Silu).then_inc(gate_done, 1)
                    act.wait_ge(kt_full, b + 1)
                    nc.scalar.activation(kt[:], st[:, 0], ACT.Copy).then_inc(kt_copied, 1)
                    act.wait_ge(y_step, b * HEADS + HEADS + 2)
                    nc.scalar.activation(yt[:], y_ps[:], ACT.Copy).then_inc(y_copied, 1)
                    act.wait_ge(stat_step, b * STATS + 2)
                    nc.scalar.activation(sq[:], cen[:], ACT.Square, accum_out=stat[:, 1:2]).then_inc(squared, 1)
                    act.wait_ge(stat_step, b * STATS + 3)
                    nc.scalar.activation(stat[:, 3:4], stat[:, 2:3], ACT.Sqrt).then_inc(rooted, 1)

            @block.gpsimd
            def _(pool):
                nc.gpsimd.memset(state[:], 0.0).then_inc(zeroed, 1)
                with nc.gpsimd.Fori(0, BATCH) as b:
                    pool.wait_ge(ab_done, b * JOBS + 4 + 2)
                    nc.gpsimd.tensor_tensor(qr[:], qk[:, 0], qk[:, 1], ALU.add).then_inc(roped, 1)
                    pool.wait_ge(ab_done, b * JOBS + 8 + 2)
                    nc.gpsimd.tensor_tensor(kr[:], qk[:, 2], qk[:, 3], ALU.add).then_inc(roped, 1)
                    pool.wait_ge(roped, b * 2 + 2)
                    nc.gpsimd.tensor_tensor(kdec[:], kr[:].rearrange("p (t n) -> p t n", n=P),
                                            dk[:].broadcast_to([P, TPB, P]), ALU.mult).then_inc(decayed, 1)
                    nc.gpsimd.tensor_tensor(qdec[:], qr[:].rearrange("p (t n) -> p t n", n=P),
                                            dq[:].broadcast_to([P, TPB, P]), ALU.mult).then_inc(decayed, 1)
                    pool.wait_ge(z_ready, b + 1)
                    nc.gpsimd.tensor_tensor(zg[:], z[:], gate[:], ALU.mult).then_inc(zg_ready, 1)

            @block.vector
            def _(dve):
                dve.sem_inc(ab_done, 2)
                dve.sem_inc(sd_ready, 2)
                dve.sem_inc(y_step, 2)
                dve.wait_ge(zeroed, 1)
                with nc.vector.Fori(0, BATCH) as b:
                    base = b * JOBS
                    nc.vector.tensor_scalar(xb[:], xn[:, ds(b * SEQ, SEQ)], 1.0, None, ALU.mult).then_inc(copied, 1)
                    for i in range(4):
                        for ch in range(2):
                            k = 2 * i + ch
                            cols = slice(ch * CH, ch * CH + CH)
                            dve.wait_ge(ab_full, base + k + 1)
                            nc.vector.tensor_tensor(qk[:, i, cols], ab[:, k % 2], rope[:, i, cols],
                                                    ALU.mult).then_inc(ab_done, 1)
                    for half in range(2):
                        k = V_JOB + half
                        dve.wait_ge(ab_full, base + k + 1)
                        nc.vector.tensor_copy(v[:, 4 * half:4 * half + 4].rearrange("p a b -> p (a b)"),
                                              ab[:, k % 2]).then_inc(ab_done, 1)
                    dve.wait_ge(kv_full, b + 1)
                    nc.vector.tensor_tensor(kv[:], st[:, 1, 0:TPB - 1], blockmask[:].broadcast_to([P, TPB - 1, P]),
                                            ALU.mult).then_inc(kv_copied, 1)
                    dve.wait_ge(kv_copied, b + 1)
                    for t in range(TPB - 1):
                        nc.vector.scalar_tensor_tensor(out=state[:, t + 1], in0=state[:, t], scalar=dchunk[:],
                                                       in1=kv[:, t], op0=ALU.mult, op1=ALU.add).then_inc(state_step, 1)
                        dve.wait_ge(state_step, b * (TPB - 1) + t + 1)

                    def mask_k(h):
                        dve.wait_ge(roped, b * 2 + 2)
                        nc.vector.tensor_scalar(km[:, h % 2], kr[:], headmask[:, h:h + 1], None,
                                                ALU.mult).then_inc(km_ready, 1)

                    mask_k(0)
                    mask_k(1)
                    for h in range(HEADS):
                        dve.wait_ge(st_full, b * HEADS + h + 1)
                        dve.wait_ge(y_step, b * HEADS + h + 1)
                        nc.vector.tensor_tensor(sd[:, h % 2], st[:, h % 2],
                                                decay[:, h:h + 1].broadcast_to([P, TPB, P]),
                                                ALU.mult).then_inc(sd_ready, 1)
                        if h + 2 < HEADS:
                            mask_k(h + 2)
                    for half in range(2):
                        k = YT_JOB + half
                        dve.wait_ge(ab_full, base + k + 1)
                        nc.vector.tensor_copy(yf[:, half * CH:half * CH + CH], ab[:, k % 2]).then_inc(ab_done, 1)
                    dve.wait_ge(ab_done, base + YT_JOB + 2 + 2)
                    nc.vector.tensor_reduce(stat[:, 0:1], yf[:], AX.X, ALU.add).then_inc(stat_step, 1)
                    dve.wait_ge(ab_full, base + MEAN_JOB + 1)
                    nc.vector.tensor_scalar(cen[:], yf[:], ab[:, MEAN_JOB % 2, 0:1], None,
                                            ALU.subtract).then_inc(stat_step, 1)
                    dve.wait_ge(stat_step, b * STATS + 2)
                    dve.sem_inc(ab_done, 1)
                    dve.wait_ge(ab_full, base + VAR_JOB + 1)
                    nc.vector.tensor_scalar(stat[:, 2:3], ab[:, VAR_JOB % 2, 0:1], EPS, None,
                                            ALU.add).then_inc(stat_step, 1)
                    dve.wait_ge(stat_step, b * STATS + 3)
                    dve.sem_inc(ab_done, 1)
                    dve.wait_ge(rooted, b + 1)
                    nc.vector.reciprocal(stat[:, 4:5], stat[:, 3:4]).then_inc(stat_step, 1)
                    dve.wait_ge(stat_step, b * STATS + 4)
                    nc.vector.tensor_tensor(stat[:, 5:6], stat[:, 4:5], gn[:, 0:1], ALU.mult).then_inc(stat_step, 1)
                    dve.wait_ge(stat_step, b * STATS + 5)
                    nc.vector.tensor_scalar(z[:], cen[:], stat[:, 5:6], gn[:, 1:2], ALU.mult,
                                            ALU.add).then_inc(z_ready, 1)
                    dve.sem_inc(stat_step, 2)
                    for ch in range(2):
                        k = OUT_JOB + ch
                        dve.wait_ge(ab_full, base + k + 1)
                        cols = ds(b * SEQ + ch * CH, CH)
                        nc.vector.tensor_tensor(res[:, cols], res[:, cols], ab[:, k % 2], ALU.add).then_inc(ab_done, 1)


def constants_retention(c):
    f = np.float32
    half = np.arange(0, HD, 2, dtype=f)
    inv = (1.0 / f(10000.0) ** (half / f(HD))).astype(f)
    t = np.arange(SEQ, dtype=f)
    ang = np.repeat((t[:, None] * inv[None, :]).astype(f), 2, axis=-1)
    vec = ((half + f(0.4 * HD)) / f(1.4 * HD)).astype(f)
    power = ((t - SEQ // 2) / f(512.0)).astype(f)
    scale = np.repeat((vec[None, :] ** power[:, None]).astype(f), 2, axis=-1)
    cos, sin = np.cos(ang), np.sin(ang) * np.tile(np.array([-1, 1], f), HD // 2)
    four = [cos * scale, sin * scale, cos / scale, sin / scale]
    c["ret_rope"] = np.stack([np.tile(a.T, (HEADS, 1)) for a in four], axis=1).astype(f)
    gamma = 1.0 - 2.0 ** (-5.0 - np.arange(HEADS, dtype=np.float64))
    d = np.arange(P)[None, :] - np.arange(P)[:, None]
    dec = np.where(d[:, None, :] >= 0, gamma[None, :, None] ** np.maximum(d, 0)[:, None, :], 0.0)
    c["ret_decay"] = (dec * HD ** -0.5).astype(f)
    rows = np.repeat(gamma, HD)[:, None]
    c["ret_dq"] = (rows ** (np.arange(P)[None, :] + 1) * HD ** -0.5).astype(f).reshape(P, 1, P)
    c["ret_dk"] = (rows ** (P - 1 - np.arange(P)[None, :])).astype(f).reshape(P, 1, P)
    c["ret_dchunk"] = (rows ** P).astype(f)
    head = np.arange(P) // HD
    c["headmask"] = (head[:, None] == np.arange(HEADS)[None, :]).astype(f)
    same = (head[:, None] == head[None, :]).astype(f)
    c["blockmask"] = same.reshape(P, 1, P)
    c["headmean"] = same * f(1.0 / (HD * SEQ))


def layout_retention(I, t):
    q, k, v = (I["L2_attn_w_qkv"][i * D:i * D + D].T for i in range(3))
    partner = np.arange(D) ^ 1
    t["a2_wqk"] = np.stack([q, q[:, partner], k, k[:, partner]], axis=1)
    t["a2_wv"], t["a2_wgate"], t["a2_wproj"] = v, I["L2_attn_w_gated"].T, I["L2_attn_w_proj"].T
    t["a2_gn"] = columns(I["L2_attn_gn_weight"], I["L2_attn_gn_bias"])


WH, WD, WINDOW, DEPTH = 8, 64, 64, 2
INNER = WH * WD
SPAN = WINDOW + P
FF = int(D * 4 * 2 / 3)


def shift_tokens(nc, name, src, dst):
    HALF = D // 2
    with ExitStack() as ctx:
        s = Scope(nc, ctx, name)
        moved = s.sem("moved")
        seqs = lambda t, lo, hi: t[lo:hi].rearrange("p (b n) -> p b n", b=BATCH)
        with nc.Block() as block:
            @block.vector
            def _(dve):
                nc.vector.tensor_copy(dst[0:HALF], src[0:HALF]).then_inc(moved, 1)

            @block.scalar
            def _(act):
                nc.scalar.activation(seqs(dst, HALF, D)[:, :, 1:], seqs(src, HALF, D)[:, :, :SEQ - 1],
                                     ACT.Copy).then_inc(moved, 1)

            @block.gpsimd
            def _(pool):
                nc.gpsimd.memset(seqs(dst, HALF, D)[:, :, 0:1], 0.0).then_inc(moved, 1)


def window_attention(nc, name, w, c, ht, src, dst):
    NB = TOK // P
    PAIRS = INNER // P
    SLOT_HEAD = [2 * ((bank % 2) * 2 + col) + bank // 2 for bank in range(4) for col in range(2)]
    WS = float(8.0)
    VW = WD + 1
    with ExitStack() as ctx:
        s = Scope(nc, ctx, name)
        wqkv, wo = s.sb("wqkv", [P, 3, INNER]), s.sb("wo", [P, PAIRS, D])
        table = s.sb("table", [P, TPB, 4, WD])
        gains = s.sb("gains", [P, 1, 4, WD])
        mask = s.sb("mask", [P, TPB, SPAN], BF16)
        ident, identb = s.sb("ident", [P, P]), s.sb("identb", [P, P], BF16)
        load_phase(nc, name + "_load", [
            (wqkv[:], w["wqkv"].rearrange("d (a n) -> d a n", a=3)), (wo[:], w["wo"].rearrange("(j p) d -> p j d", p=P)),
            (table[:], c["win_rope"]), (gains[:], w["gains"].broadcast_to([P, 4 * WD]).rearrange(
                "p (a f d) -> p a f d", a=1, f=4)), (mask[:], c["win_mask"]), (ident[:], c["ident"]),
            (identb[:], c["identb"])])
        hb = s.sb("hb", [P, 2, P])
        squares = s.sb("squares", [P, 2, 2 * WH, WD])
        norm2, clipped, rnorm = s.sb("norm2", [P, 2, 2 * WH]), s.sb("clipped", [P, 2, 2 * WH]), s.sb(
            "rnorm", [P, 2, 2 * WH])
        minus_half = s.sb("minus_half", [P, 2 * WH])
        rot_a, rot_b = s.sb("rot_a", [P, 2, 2, INNER]), s.sb("rot_b", [P, 2, 2, INNER])
        rot = s.sb("rot", [P, 2, 2, INNER])
        qk = s.sb("qk", [P, 2, 2, INNER])
        qt, kt = s.sb("qt", [P, 2, PAIRS, P]), s.sb("kt", [P, 2, PAIRS, SPAN])
        v, vprev = s.sb("v", [P, 2, WH, VW]), s.sb("vprev", [WINDOW, 2, WH, VW])
        top = s.sb("top", [P, 2, WH])
        less, ex = s.sb("less", [P, 2, WH, SPAN]), s.sb("ex", [P, 2, WH, SPAN])
        pt, ptprev = s.sb("pt", [P, WH, P]), s.sb("ptprev", [WINDOW, WH, P])
        inv = s.sb("inv", [P, 2, WH])
        o, ot = s.sb("o", [P, 2, INNER]), s.sb("ot", [P, 2, PAIRS, P])
        sets = s.ps("sets", [P, 2, 4, CH])

        ready = s.sem("ready")
        hb_ready, qk_full, v_full, squared, v_copied = (s.sem("hb_ready"), s.sem("qk_full"), s.sem("v_full"),
                                                        s.sem("squared"), s.sem("v_copied"))
        rotated, norm_step, norm_ready, rnorm_ready, qk_ready = (s.sem("rotated"), s.sem("norm_step"),
                                                               s.sem("norm_ready"), s.sem("rnorm_ready"),
                                                               s.sem("qk_ready"))
        t_full, qkt_copied, s_full, topped, less_ready, ex_ready = (
            s.sem("t_full"), s.sem("qkt_copied"), s.sem("s_full"), s.sem("topped"), s.sem("less_ready"),
            s.sem("ex_ready"))
        pt_full, pt_copied, o_full, inverted, o_ready, vprev_copied = (
            s.sem("pt_full"), s.sem("pt_copied"), s.sem("o_full"), s.sem("inverted"), s.sem("o_ready"),
            s.sem("vprev_copied"))
        ot_full, ot_copied, out_full, added = s.sem("ot_full"), s.sem("ot_copied"), s.sem("out_full"), s.sem("added")

        def of_block(i):
            return slice(i % TPB, i % TPB + 1) if isinstance(i, int) else ds(i % TPB, 1)

        def blocks(engine, first, body):
            first(0, 0)
            body(0, 0, 2)
            body(1, 1, 2)
            with engine.Fori(1, (NB - 2) // 2) as n:
                body(n * 2, 0, 2)
                body(n * 2 + 1, 1, 2)
            body(NB - 2, 0, 1)
            body(NB - 1, 1, 0)

        with nc.Block() as block:
            @block.gpsimd
            def _(pool):
                nc.gpsimd.memset(v[:], 1.0).then_inc(ready, 1)
                nc.gpsimd.memset(vprev[:], 0.0).then_inc(ready, 1)
                nc.gpsimd.memset(kt[:], 0.0).then_inc(ready, 1)
                nc.gpsimd.memset(minus_half[:], -0.5).then_inc(ready, 1)

            @block.vector
            def _(dve):
                nc.vector.tensor_tensor(table[:], table[:], gains[:].broadcast_to([P, TPB, 4, WD]),
                                        ALU.mult).then_inc(ready, 1)

        with nc.Block() as block:
            @block.tensor
            def _(pe):
                def project_qk(i, sl):
                    pe.wait_ge(hb_ready, i + 1)
                    for j in range(2):
                        mm = nc.tensor.matmul(sets[:, sl, j], hb[:, sl], wqkv[:, j], start=True, stop=True)
                    mm.then_inc(qk_full, 1)

                def project_v(i, sl):
                    nc.tensor.matmul(sets[:, sl, 2], hb[:, sl], wqkv[:, 2], start=True, stop=True).then_inc(v_full, 1)

                def turn_qk(i, sl):
                    pe.wait_ge(qk_ready, i + 1)
                    for a in range(2):
                        for j in range(PAIRS):
                            mm = nc.tensor.transpose(sets[:, sl, a, j * P:j * P + P], qk[:, sl, a, j * P:j * P + P],
                                                     ident[:])
                    mm.then_inc(t_full, 1)

                def scores(i, sl):
                    pe.wait_ge(qkt_copied, i * 3 + 3)
                    pe.wait_ge(v_copied, i + 1)
                    pe.wait_ge(added, i + 1)
                    for bank in range(4):
                        nc.tensor.matmul(sets[:, sl, bank, 0:2 * SPAN].rearrange("p (a n) -> p a n", a=2), identb[:],
                                         mask[:, of_block(i)].broadcast_to([P, 2, SPAN]), start=True, stop=False,
                                         skip_group_check=True)
                    for u in (0, 4, 1, 5, 2, 6, 3, 7):
                        h = SLOT_HEAD[u]
                        r = WD * (h % 2)
                        mm = nc.tensor.matmul(sets[:, sl, u // 2, u % 2 * SPAN:u % 2 * SPAN + SPAN],
                                              qt[r:r + WD, sl, h // 2], kt[r:r + WD, sl, h // 2], start=False,
                                              stop=True, skip_group_check=True)
                    mm.then_inc(s_full, 1)

                def turn_p(i, sl):
                    pe.wait_ge(ex_ready, i + 1)
                    for u in range(WH):
                        nc.tensor.transpose(sets[:, sl, u // 4, u % 4 * P:u % 4 * P + P], ex[:, sl, u, WINDOW:SPAN],
                                            ident[:])
                    for u in range(WH):
                        mm = nc.tensor.transpose(sets[:, sl, 2 + u // 4, u % 4 * P:u % 4 * P + P], ex[:, sl, u, 0:P],
                                                 ident[:])
                    mm.then_inc(pt_full, 1)

                def values(i, sl):
                    pe.wait_ge(pt_copied, i * 2 + 2)
                    pe.wait_ge(vprev_copied, i + 1)
                    for u in range(WH):
                        h = SLOT_HEAD[u]
                        out = sets[:, sl, h // 4, h % 4 * VW:h % 4 * VW + VW]
                        nc.tensor.matmul(out, pt[:, u], v[:, sl, h], start=True, stop=False, skip_group_check=True)
                        mm = nc.tensor.matmul(out, ptprev[:, u], vprev[:, sl, h], start=False, stop=True,
                                              skip_group_check=True)
                    mm.then_inc(o_full, 1)

                def turn_o(i, sl):
                    pe.wait_ge(o_ready, i + 1)
                    for j in range(PAIRS):
                        mm = nc.tensor.transpose(sets[:, sl, 2, j * P:j * P + P], o[:, sl, j * P:j * P + P], ident[:])
                    mm.then_inc(ot_full, 1)

                def output(i, sl):
                    pe.wait_ge(ot_copied, i + 1)
                    for j in range(PAIRS):
                        mm = nc.tensor.matmul(sets[:, sl, 3, 0:P], wo[:, j], ot[:, sl, j], start=j == 0,
                                              stop=j == PAIRS - 1)
                    mm.then_inc(out_full, 1)

                def first(i, sl):
                    project_qk(i, sl)
                    project_v(i, sl)
                    turn_qk(i, sl)
                    scores(i, sl)

                def body(i, sl, left):
                    if left:
                        project_qk(i + 1, 1 - sl)
                    if not (isinstance(i, int) and i == 0):
                        output(i - 1, 1 - sl)
                    turn_p(i, sl)
                    if left:
                        project_v(i + 1, 1 - sl)
                    values(i, sl)
                    if left:
                        turn_qk(i + 1, 1 - sl)
                    turn_o(i, sl)
                    if left:
                        scores(i + 1, 1 - sl)
                    else:
                        output(i, sl)

                blocks(nc.tensor, first, body)

            @block.scalar
            def _(act):
                act.sem_inc(vprev_copied, 2)

                def square(i, sl):
                    act.wait_ge(qk_full, i + 1)
                    nc.scalar.activation(squares[:, sl].rearrange("p h d -> p (h d)"),
                                         sets[:, sl, 0:2].rearrange("p a n -> p (a n)"), ACT.Square).then_inc(squared, 1)

                def copy_v(i, sl):
                    act.wait_ge(v_full, i + 1)
                    nc.scalar.activation(v[:, sl, :, 0:WD], sets[:, sl, 2].rearrange("p (h d) -> p h d", h=WH),
                                         ACT.Copy).then_inc(v_copied, 1)

                def copy_qkt(i, sl):
                    act.wait_ge(t_full, i + 1)
                    nc.scalar.activation(qt[:, sl].rearrange("p j n -> p (j n)"), sets[:, sl, 0],
                                         ACT.Copy).then_inc(qkt_copied, 1)
                    keys = sets[:, sl, 1].rearrange("p (j n) -> p j n", j=PAIRS)
                    nc.scalar.activation(kt[:, sl, :, WINDOW:SPAN], keys, ACT.Copy).then_inc(qkt_copied, 1)
                    nc.scalar.activation(kt[:, 1 - sl, :, 0:WINDOW], keys[:, :, P - WINDOW:P],
                                         ACT.Copy).then_inc(qkt_copied, 1)

                def exponentials(i, sl):
                    act.wait_ge(less_ready, i + 1)
                    nc.scalar.activation(ex[:, sl], less[:, sl], ACT.Exp, scale=WS).then_inc(ex_ready, 1)

                def copy_pt(i, sl):
                    act.wait_ge(pt_full, i + 1)
                    nc.scalar.activation(pt[:].rearrange("p u n -> p (u n)"),
                                         sets[:, sl, 0:2].rearrange("p a n -> p (a n)"), ACT.Copy).then_inc(pt_copied, 1)
                    nc.scalar.activation(ptprev[:].rearrange("p u n -> p (u n)"),
                                         sets[0:WINDOW, sl, 2:4].rearrange("p a n -> p (a n)"),
                                         ACT.Copy).then_inc(pt_copied, 1)

                def copy_vprev(i, sl):
                    act.wait_ge(o_full, i + 1)
                    act.wait_ge(v_copied, i + 2)
                    nc.scalar.activation(vprev[:, sl], v[P - WINDOW:P, 1 - sl], ACT.Copy).then_inc(vprev_copied, 1)

                def copy_ot(i, sl):
                    act.wait_ge(ot_full, i + 1)
                    nc.scalar.activation(ot[:, sl].rearrange("p j n -> p (j n)"), sets[:, sl, 2],
                                         ACT.Copy).then_inc(ot_copied, 1)

                def first(i, sl):
                    square(i, sl)
                    copy_v(i, sl)
                    copy_qkt(i, sl)
                    exponentials(i, sl)
                    act.wait_ge(v_copied, 1)
                    nc.scalar.activation(vprev[:, 1], v[P - WINDOW:P, 0], ACT.Copy).then_inc(vprev_copied, 1)

                def body(i, sl, left):
                    if left:
                        square(i + 1, 1 - sl)
                    copy_pt(i, sl)
                    if left:
                        copy_v(i + 1, 1 - sl)
                        copy_qkt(i + 1, 1 - sl)
                    copy_ot(i, sl)
                    if left == 2:
                        copy_vprev(i, sl)
                    if left:
                        exponentials(i + 1, 1 - sl)

                blocks(nc.scalar, first, body)

            @block.gpsimd
            def _(pool):
                def inverse_norm(i, sl):
                    pool.wait_ge(norm_ready, i + 1)
                    nc.gpsimd.tensor_tensor(rnorm[:, sl], clipped[:, sl], minus_half[:], ALU.pow).then_inc(rnorm_ready, 1)

                def body(i, sl, left):
                    if left:
                        inverse_norm(i + 1, 1 - sl)

                blocks(nc.gpsimd, inverse_norm, body)

            @block.vector
            def _(dve):
                dve.sem_inc(added, 2)

                def bring(i, sl):
                    nc.vector.tensor_scalar(hb[:, sl], ht[:, ds(i * P, P)], 1.0, None, ALU.mult).then_inc(hb_ready, 1)

                def rotate(i, sl):
                    dve.wait_ge(squared, i + 1)
                    nc.vector.tensor_reduce(norm2[:, sl], squares[:, sl], AX.X, ALU.add).then_inc(norm_step, 1)
                    dve.wait_ge(norm_step, i + 1)
                    nc.vector.tensor_scalar(clipped[:, sl], norm2[:, sl], 1e-24, None, ALU.max).then_inc(norm_ready, 1)
                    proj = sets[:, sl, 0:2].rearrange("p a (h d) -> p a h d", d=WD)
                    half = WD // 2

                    def factor(f, lo, hi):
                        t4 = table[:, of_block(i), f:f + 2, lo:hi].rearrange("p t f (a d) -> p (t f) a d", a=1)
                        return t4.broadcast_to([P, 2, WH, hi - lo])

                    nc.vector.tensor_tensor(rot_a[:, sl].rearrange("p a (h d) -> p a h d", d=WD), proj,
                                            factor(0, 0, WD), ALU.mult).then_inc(rotated, 1)
                    part = rot_b[:, sl].rearrange("p a (h d) -> p a h d", d=WD)
                    nc.vector.tensor_tensor(part[:, :, :, 0:half], proj[:, :, :, half:WD], factor(2, 0, half),
                                            ALU.mult).then_inc(rotated, 1)
                    nc.vector.tensor_tensor(part[:, :, :, half:WD], proj[:, :, :, 0:half], factor(2, half, WD),
                                            ALU.mult).then_inc(rotated, 1)
                    dve.wait_ge(rotated, i * 4 + 3)
                    nc.vector.tensor_tensor(rot[:, sl], rot_a[:, sl], rot_b[:, sl], ALU.add).then_inc(rotated, 1)
                    dve.wait_ge(rotated, i * 4 + 4)
                    dve.wait_ge(rnorm_ready, i + 1)
                    nc.vector.tensor_tensor(qk[:, sl].rearrange("p a (h d) -> p (a h) d", d=WD),
                                            rot[:, sl].rearrange("p a (h d) -> p (a h) d", d=WD),
                                            rnorm[:, sl].rearrange("p (h a) -> p h a", a=1)
                                            .broadcast_to([P, 2 * WH, WD]), ALU.mult).then_inc(qk_ready, 1)

                def softmax_arguments(i, sl):
                    dve.wait_ge(s_full, i + 1)
                    got = sets[:, sl, :, 0:2 * SPAN].rearrange("p b (c n) -> p b c n", c=2)
                    nc.vector.tensor_reduce(top[:, sl].rearrange("p (b c) -> p b c", c=2), got, AX.X,
                                            ALU.max).then_inc(topped, 1)
                    dve.wait_ge(topped, i + 1)
                    nc.vector.tensor_tensor(less[:, sl].rearrange("p (b c) n -> p b c n", c=2), got,
                                            top[:, sl].rearrange("p (b c a) -> p b c a", c=2, a=1)
                                            .broadcast_to([P, 4, 2, SPAN]), ALU.subtract).then_inc(less_ready, 1)

                def normalise(i, sl):
                    dve.wait_ge(o_full, i + 1)
                    got = sets[:, sl, 0:2, 0:4 * VW].rearrange("p b (c n) -> p b c n", n=VW)
                    nc.vector.reciprocal(inv[:, sl].rearrange("p (b c a) -> p b c a", b=2, a=1),
                                         got[:, :, :, WD:VW]).then_inc(inverted, 1)
                    dve.wait_ge(inverted, i + 1)
                    nc.vector.tensor_tensor(o[:, sl].rearrange("p (b c n) -> p b c n", b=2, n=WD), got[:, :, :, 0:WD],
                                            inv[:, sl].rearrange("p (b c a) -> p b c a", b=2, a=1)
                                            .broadcast_to([P, 2, 4, WD]), ALU.mult).then_inc(o_ready, 1)

                def store(i, sl):
                    dve.wait_ge(out_full, i + 1)
                    cols = ds(i * P, P)
                    nc.vector.tensor_tensor(dst[:, cols], src[:, cols], sets[:, sl, 3, 0:P], ALU.add).then_inc(added, 1)

                def first(i, sl):
                    bring(0, 0)
                    bring(1, 1)
                    rotate(i, sl)
                    softmax_arguments(i, sl)

                def body(i, sl, left):
                    if left:
                        rotate(i + 1, 1 - sl)
                    if not (isinstance(i, int) and i == 0):
                        store(i - 1, 1 - sl)
                    if left == 2:
                        bring(i + 2, sl)
                    normalise(i, sl)
                    if left:
                        softmax_arguments(i + 1, 1 - sl)
                    else:
                        store(i, sl)

                blocks(nc.vector, first, body)


def geglu(nc, name, w, hn, xf, total=None):
    parts = [(j * P, min(P, FF - j * P)) for j in range((FF + P - 1) // P)]
    J = len(parts)
    with ExitStack() as ctx:
        s = Scope(nc, ctx, name)
        w1, w2 = s.sb("w1", [P, 2 * FF]), s.sb("w2", [P, J, D])
        b1, b2 = s.sb("b1", [P, 2 * J]), s.sb("b2", [P, 1])
        load_phase(nc, name + "_load", [(w1[:], w["w1"]), (w2[:], w["w2"].rearrange("(j p) d -> p j d", p=P)),
                                        (b1[:], w["b1"]), (b2[:], w["b2"])])
        g_act, u = s.sb("g_act", [P, 2, CH]), s.sb("u", [P, 2, CH])
        a_ps, g_ps, y_ps = s.ps("a_ps", [P, 2, CH]), s.ps("g_ps", [P, 2, CH]), s.ps("y_ps", [P, 2, CH])
        full, act_done, u_ready, used, y_full, y_added, total_added = (
            s.sem("full"), s.sem("act_done"), s.sem("u_ready"), s.sem("used"), s.sem("y_full"), s.sem("y_added"),
            s.sem("total_added"))
        jobs = [(i, j, (i * J + j) % 2, lo, n) for i in range(2) for j, (lo, n) in enumerate(parts)]
        NJ = len(jobs)
        with nc.Block() as block:
            @block.tensor
            def _(pe):
                with nc.tensor.Fori(0, NCH // 2) as n:
                    def down(k):
                        i, j, sl, lo, m = jobs[k]
                        pe.wait_ge(u_ready, n * NJ + k + 3)
                        if j == 0:
                            pe.wait_ge(y_added, n * 2 + i + 1)
                        mm = nc.tensor.matmul(y_ps[:, i], w2[0:m, j], u[0:m, sl], start=j == 0, stop=j == J - 1)
                        mm.then_inc(used, 1)

                    for k, (i, j, sl, lo, m) in enumerate(jobs):
                        cols = ds(n * 2 * CH + i * CH, CH)
                        pe.wait_ge(u_ready, n * NJ + k + 1)
                        nc.tensor.matmul(a_ps[0:m, sl], w1[:, lo:lo + m], hn[:, cols], start=True, stop=True)
                        nc.tensor.matmul(g_ps[0:m, sl], w1[:, FF + lo:FF + lo + m], hn[:, cols], start=True,
                                         stop=True).then_inc(full, 1)
                        if k:
                            down(k - 1)
                    down(NJ - 1)

            @block.scalar
            def _(act):
                with nc.scalar.Fori(0, NCH // 2) as n:
                    for k, (i, j, sl, lo, m) in enumerate(jobs):
                        act.wait_ge(full, n * NJ + k + 1)
                        act.wait_ge(u_ready, n * NJ + k + 1)
                        nc.scalar.activation(g_act[0:m, sl], g_ps[0:m, sl], ACT.Gelu,
                                             bias=b1[0:m, J + j:J + j + 1]).then_inc(act_done, 1)

            @block.vector
            def _(dve):
                dve.sem_inc(u_ready, 2)
                dve.sem_inc(used, 2)
                dve.sem_inc(y_added, 2)
                with nc.vector.Fori(0, NCH // 2) as n:
                    for k, (i, j, sl, lo, m) in enumerate(jobs):
                        dve.wait_ge(act_done, n * NJ + k + 1)
                        dve.wait_ge(used, n * NJ + k + 1)
                        nc.vector.scalar_tensor_tensor(out=u[0:m, sl], in0=a_ps[0:m, sl], scalar=b1[0:m, j:j + 1],
                                                       in1=g_act[0:m, sl], op0=ALU.add,
                                                       op1=ALU.mult).then_inc(u_ready, 1)
                        if j == J - 1:
                            cols = ds(n * 2 * CH + i * CH, CH)
                            dve.wait_ge(used, n * NJ + k + 3)
                            nc.vector.scalar_tensor_tensor(out=xf[:, cols], in0=y_ps[:, i], scalar=b2[:],
                                                           in1=xf[:, cols], op0=ALU.add,
                                                           op1=ALU.add).then_inc(y_added, 1)
                            if total is not None:
                                dve.wait_ge(y_added, n * 2 + i + 3)
                                nc.vector.tensor_tensor(total[:, cols], total[:, cols], xf[:, cols],
                                                        ALU.add).then_inc(total_added, 1)


def local_transformer(nc, name, w, c, xn, res, mean_w, eps_col):
    with ExitStack() as ctx:
        s = Scope(nc, ctx, name)
        xf, ht = s.sb("xf", [P, TOK]), s.sb("ht", [P, TOK])
        ln = s.sb("ln", [P, 2 * DEPTH])
        load_phase(nc, name + "_load", [(ln[:], w["ln"])])
        for l in range(DEPTH):
            wl = {k[1:]: v for k, v in w.items() if k[0] == str(l)}
            src = xf if l else xn
            shift_tokens(nc, f"{name}s{l}", src, ht)
            window_attention(nc, f"{name}w{l}", wl, c, ht, src, xf)
            shift_tokens(nc, f"{name}t{l}", xf, ht)
            layernorm(nc, f"{name}n{l}", ht, ht, mean_w, eps_col, gain=ln[:, 2 * l:2 * l + 1],
                      shift=ln[:, 2 * l + 1:2 * l + 2])
            geglu(nc, f"{name}g{l}", wl, ht, xf, res if l == DEPTH - 1 else None)


def constants_local(c):
    f = np.float32
    half = np.arange(0, WD, 2, dtype=f)
    inv = (1.0 / f(10000.0) ** (half / f(WD))).astype(f)
    t = np.arange(SEQ, dtype=f)
    ang = (t[:, None] * inv[None, :]).astype(f)
    ang = np.concatenate([ang, ang], axis=-1)
    base = ((half + f(0.4 * WD)) / f(1.4 * WD)).astype(f)
    power = ((t - SEQ // 2) / f(WINDOW // 2)).astype(f)
    scale = (base[None, :].astype(np.float64) ** power[:, None]).astype(f)
    scale = np.concatenate([scale, scale], axis=-1)
    cos = np.cos(ang)
    sin = np.sin(ang) * np.concatenate([-np.ones(WD // 2, f), np.ones(WD // 2, f)])
    four = [cos * scale, cos / scale, sin * scale, sin / scale]
    c["win_rope"] = np.stack([a.reshape(TPB, P, WD).transpose(1, 0, 2) for a in four], axis=2).astype(f)
    q, k = np.arange(P)[:, None], np.arange(SPAN)[None, :] - WINDOW
    seen = (k <= q) & (k >= q - WINDOW)
    mask = np.where(seen, 0.0, -1e30)[:, None, :].repeat(TPB, axis=1)
    mask[:, 0, :WINDOW] = -1e30
    c["win_mask"] = mask.astype(np.dtype("bfloat16"))


def layout_local(I, t):
    partner = (np.arange(WD) + WD // 2) % WD
    J = (FF + P - 1) // P
    t["f0_ln"] = columns(*[I[k][l] for l in range(DEPTH) for k in ("L0_ffn_ln_g", "L0_ffn_ln_b")])
    for l in range(DEPTH):
        qs, ks = I["L0_ffn_q_scale"][l], I["L0_ffn_k_scale"][l]
        t[f"f0_{l}wqkv"], t[f"f0_{l}wo"] = I["L0_ffn_wqkv"][l], I["L0_ffn_wo"][l]
        t[f"f0_{l}gains"] = np.concatenate([qs, ks, qs[partner], ks[partner]]).reshape(1, 4 * WD)
        t[f"f0_{l}w1"] = I["L0_ffn_w1"][l]
        w2 = np.zeros((J * P, D), np.float32)
        w2[:FF] = I["L0_ffn_w2"][l]
        t[f"f0_{l}w2"] = w2
        b1 = np.zeros((2, J * P), np.float32)
        b1[:, :FF] = I["L0_ffn_b1"][l].reshape(2, FF)
        t[f"f0_{l}b1"] = b1.reshape(2 * J, P).T
        t[f"f0_{l}b2"] = I["L0_ffn_b2"][l].reshape(D, 1)


ONLY = 0


def build_program(nc, t, out):
    with ExitStack() as ctx:
        s = Scope(nc, ctx, "all")
        x = s.sb("x", [P, TOK])
        xn = s.sb("xn", [P, TOK])
        mean_w, eps_col = s.sb("mean_w", [P, P]), s.sb("eps_col", [P, 1])
        load_phase(nc, "load_x", [(x[:], t["xT"]), (mean_w[:], t["mean_w"]), (eps_col[:], t["eps_col"])])

        def part(prefix):
            return {k[len(prefix):]: v for k, v in t.items() if k.startswith(prefix)}

        phases = [
            lambda: headwise_attention(nc, "a0", part("a0_"), t, xn, x),
            lambda: local_transformer(nc, "f0", part("f0_"), t, xn, x, mean_w, eps_col),
            lambda: narrow_attention(nc, "a1", part("a1_"), t, xn, x, causal=True),
            lambda: experts(nc, "f1", part("f1_"), t, xn, x, biased=False),
            lambda: retention(nc, "a2", part("a2_"), t, xn, x, eps_col),
            lambda: experts(nc, "f2", part("f2_"), t, xn, x, biased=True),
            lambda: headwise_attention(nc, "a3", part("a3_"), t, xn, x, latent=True),
            lambda: switch_ffn(nc, "f3", part("f3_"), t, xn, x),
        ]
        for n, phase in enumerate(phases):
            if n % 2 == 0 and not ONLY:
                layernorm(nc, f"ln{n // 2}", x, xn, mean_w, eps_col)
            if ONLY and ONLY == n + 1:
                layernorm(nc, f"ln{n // 2}", x, xn, mean_w, eps_col)
            if not ONLY or ONLY == n + 1:
                phase()
        stored = s.sem("stored")
        with nc.Block() as block:
            @block.sync
            def _(sp):
                sp.dma_start(out, x[:]).then_inc(stored, 16)
                sp.wait_ge(stored, 16)


def constants():
    bf = np.dtype("bfloat16")
    f = np.float32
    c = {}
    c["mean_w"] = np.full((P, P), 1.0 / P, f)
    c["eps_col"] = np.full((P, 1), EPS, f)
    c["ident"] = np.eye(P, dtype=f)
    c["identb"] = np.eye(P).astype(bf)
    c["ones1"] = np.ones((1, P), f)
    for key, parts in (("selq", Q_PART), ("selk", K_PART)):
        sel = np.zeros((P, QUADS, 2, 3, P), f)
        for q in range(QUADS):
            for g in range(2):
                for jj in range(2):
                    head = 4 * q + 2 * g + jj
                    for slot, l in enumerate(parts):
                        for d in range(HD):
                            sel[head * HD + d, q, g, l, 64 * jj + 8 * slot + d] = 1
        c[key] = sel.reshape(P, -1).astype(bf)
    kone = np.zeros((P, 1), f)
    for jj in range(2):
        kone[64 * jj + M_ROW:64 * jj + M_ROW + 3] = 1
    c["kone"] = kone
    sumbc = np.zeros((P, P), f)
    for j in range(4):
        sumbc[32 * j + HD, 32 * j:32 * j + 32] = 1
    c["sumbc"] = sumbc
    i, j = np.arange(P)[:, None], np.arange(P)[None, :]
    c["mask_qk"] = np.where(j > i, -1e30, 0).astype(bf)
    c["mask_kq"] = np.where(i > j, -1e30, 0).astype(bf)
    inv = (1.0 / f(10000.0) ** (np.arange(0, HD, 2, dtype=f) / f(HD))).astype(f)
    ang = (np.arange(SEQ, dtype=f)[:, None] * inv[None, :]).astype(f)
    cos, sin = np.cos(ang), np.sin(ang)
    by_block = lambda a: a.reshape(TPB, P, HD).transpose(1, 0, 2)
    c["cos8"] = by_block(np.concatenate([cos, cos], 1)).astype(f)
    c["sin8"] = by_block(np.concatenate([-sin, sin], 1)).astype(f)
    constants_experts(c)
    constants_local(c)
    constants_retention(c)
    return c


def quad_columns(wv, bias):
    k = wv.shape[0]
    out = np.zeros((k, HEADS, 32), np.float32)
    out[:, :, :HD] = wv.reshape(k, HEADS, HD)
    row = np.zeros((1, HEADS, 32), np.float32)
    if bias is not None:
        row[0, :, :HD] = bias.reshape(HEADS, HD)
    row[0, :, HD] = 1
    return out.reshape(k, -1), row.reshape(1, -1)


def quad_rows(wo, bias):
    out = np.zeros((HEADS, 32, D), np.float32)
    out[:, :HD] = wo.reshape(HEADS, HD, D)
    if bias is not None:
        out[0, HD] = bias
    return out.reshape(QUADS, P, D)


def columns(*vectors):
    out = np.zeros((P, len(vectors)), np.float32)
    for i, v in enumerate(vectors):
        if v is not None:
            out[:, i] = v
    return out


def layout(I):
    t = {"xT": I["L0_attn_x"].reshape(TOK, D).T}
    wqkv = I["L0_attn_W_qkv"].reshape(D, HEADS, 3, HD)
    bqkv = I["L0_attn_b_qkv"].reshape(HEADS, 3, HD)
    t["a0_wqkv"] = wqkv.transpose(0, 2, 1, 3).reshape(D, 3 * D)
    t["a0_bqkv"] = bqkv.transpose(1, 0, 2).reshape(1, 3 * D)
    t["a0_wo"], t["a0_bo"] = I["L0_attn_W_out"], I["L0_attn_b_out"].reshape(D, 1)

    t["a1_wq"], t["a1_wk"] = I["L1_attn_Wq"], I["L1_attn_Wk"]
    t["a1_bqk"] = columns(None, None, None, None)
    t["a1_wv"], t["a1_bv"] = quad_columns(I["L1_attn_Wv"], None)
    t["a1_wo"] = quad_rows(I["L1_attn_Wo"], None)

    wup, bup = I["L3_attn_Wup"].reshape(-1, HEADS, 2, HD), I["L3_attn_bup"].reshape(HEADS, 2, HD)
    t["a3_wqkv"] = I["L3_attn_Wq"]
    t["a3_bqkv"] = np.concatenate([I["L3_attn_bq"], bup[:, 0].reshape(-1), bup[:, 1].reshape(-1)]).reshape(1, 3 * D)
    t["a3_wdown"], t["a3_bdown"] = I["L3_attn_Wdown"], I["L3_attn_bdown"].reshape(-1, 1)
    t["a3_wup"] = wup.transpose(0, 2, 1, 3).reshape(-1, 2 * D)
    t["a3_wo"], t["a3_bo"] = I["L3_attn_Wout"], I["L3_attn_bout"].reshape(D, 1)
    layout_local(I, t)
    layout_experts(I, t)
    layout_retention(I, t)
    t["f3_wg"], t["f3_we"], t["f3_be"] = I["L3_ffn_Wg"], I["L3_ffn_We"], I["L3_ffn_be"].reshape(-1, 1)
    return t


def kernel(**inputs):
    import concourse.bacc as bacc
    from concourse.bass_utils import run_bass_kernel_spmd as run

    nc = bacc.Bacc("TRN2", target_bir_lowering=False, num_devices=1)
    arrays, views = {}, {}
    for key, a in {**constants(), **layout({k: np.asarray(v) for k, v in inputs.items()})}.items():
        a = np.ascontiguousarray(a)
        arrays[f"in_{key}"] = a
        views[key] = nc.dram_tensor(f"in_{key}", a.shape, mybir.dt.from_np(a.dtype), kind="ExternalInput").ap()
    out = nc.dram_tensor("out_x", (P, TOK), F32, kind="ExternalOutput").ap()
    build_program(nc, views, out)
    r = run(nc, [arrays], core_ids=[0])
    return r.results[0]["out_x"].T.reshape(BATCH, SEQ, D)
```

```python
from contextlib import ExitStack

import numpy as np

import concourse.bass as bass
from concourse import mybir

ALU = mybir.AluOpType
ACT = mybir.ActivationFunctionType
AX = mybir.AxisListType
F32 = mybir.dt.float32
BF16 = mybir.dt.bfloat16
ds = bass.ds

P = 128
D = 128
BATCH, SEQ = 4, 1024
TOK = BATCH * SEQ
CH = 512
NCH = TOK // CH
TPB = SEQ // P
EPS = 1e-5

HEADS, HD = 16, 8
QUADS = 4
SCALE8 = float(1.0 / np.sqrt(8.0))
Q_PART = [0, 0, 1, 1, 0, 2]
K_PART = [0, 1, 0, 1, 2, 0]
M_ROW = 8 * len(Q_PART)


class Scope:

    def __init__(self, nc, ctx, name):
        self.nc, self.ctx, self.name = nc, ctx, name
        self.sems = []
        ctx.callback(self.release)

    def release(self):
        if self.sems:
            self.nc.clear_and_free_semaphores(self.sems)
            self.nc.all_engine_barrier()

    def sb(self, name, shape, dt=F32):
        return self.ctx.enter_context(self.nc.sbuf_tensor(f"{self.name}_{name}", shape, dt))

    def ps(self, name, shape, dt=F32):
        return self.ctx.enter_context(self.nc.psum_tensor(f"{self.name}_{name}", shape, dt))

    def sem(self, name):
        self.sems.append(self.nc.alloc_semaphore(f"{self.name}_{name}"))
        return self.sems[-1]


def load_phase(nc, name, loads):
    with ExitStack() as ctx:
        landed = Scope(nc, ctx, name).sem("landed")
        with nc.Block() as block:
            @block.sync
            def _(sp):
                for dst, src in loads:
                    sp.dma_start(dst, src).then_inc(landed, 16)
                sp.wait_ge(landed, 16 * len(loads))


def layernorm(nc, name, src, dst, mean_w, eps_col, gain=None, shift=None):
    with ExitStack() as ctx:
        s = Scope(nc, ctx, name)
        cen = s.sb("cen", [P, 2, CH])
        sq = s.sb("sq", [P, 2, CH])
        std = s.sb("std", [P, 2, CH])
        rstd = s.sb("rstd", [P, 2, CH])
        mean_ps = s.ps("mean_ps", [P, 2, CH])
        var_ps = s.ps("var_ps", [P, 2, CH])
        mean_ready, centred = s.sem("mean_ready"), s.sem("centred")
        squared, var_ready = s.sem("squared"), s.sem("var_ready")
        rooted, inverted, scaled = s.sem("rooted"), s.sem("inverted"), s.sem("scaled")
        affine = s.sem("affine")
        with nc.Block() as block:
            @block.tensor
            def _(pe):
                with nc.tensor.Fori(0, NCH // 2) as n:
                    for i in range(2):
                        pe.wait_ge(centred, n * 2 + i + 1)
                        nc.tensor.matmul(mean_ps[:, i], mean_w[:], src[:, ds(n * 2 * CH + i * CH, CH)],
                                         start=True, stop=True).then_inc(mean_ready, 1)
                    for i in range(2):
                        pe.wait_ge(squared, n * 2 + i + 1)
                        pe.wait_ge(rooted, n * 2 + i + 1)
                        nc.tensor.matmul(var_ps[:, i], mean_w[:], sq[:, i], start=True,
                                         stop=True).then_inc(var_ready, 1)

            @block.scalar
            def _(act):
                act.sem_inc(rooted, 2)
                with nc.scalar.Fori(0, NCH // 2) as n:
                    for i in range(2):
                        act.wait_ge(centred, n * 2 + i + 3)
                        nc.scalar.activation(sq[:, i], cen[:, i], ACT.Square).then_inc(squared, 1)
                    for i in range(2):
                        act.wait_ge(var_ready, n * 2 + i + 1)
                        act.wait_ge(inverted, n * 2 + i + 1)
                        nc.scalar.activation(std[:, i], var_ps[:, i], ACT.Sqrt,
                                             bias=eps_col[:]).then_inc(rooted, 1)

            @block.vector
            def _(dve):
                dve.sem_inc(centred, 2)
                dve.sem_inc(inverted, 2)
                dve.sem_inc(scaled, 2)
                with nc.vector.Fori(0, NCH // 2) as n:
                    for i in range(2):
                        dve.wait_ge(mean_ready, n * 2 + i + 1)
                        dve.wait_ge(scaled, n * 2 + i + 1)
                        nc.vector.tensor_tensor(cen[:, i], src[:, ds(n * 2 * CH + i * CH, CH)], mean_ps[:, i],
                                                ALU.subtract).then_inc(centred, 1)
                    for i in range(2):
                        dve.wait_ge(rooted, n * 2 + i + 3)
                        nc.vector.reciprocal(rstd[:, i], std[:, i]).then_inc(inverted, 1)
                        dve.wait_ge(inverted, n * 2 + i + 3)
                        nc.vector.tensor_tensor(dst[:, ds(n * 2 * CH + i * CH, CH)], cen[:, i], rstd[:, i],
                                                ALU.mult).then_inc(scaled, 1)
                        if gain is not None:
                            dve.wait_ge(scaled, n * 2 + i + 3)
                            nc.vector.tensor_scalar(dst[:, ds(n * 2 * CH + i * CH, CH)],
                                                    dst[:, ds(n * 2 * CH + i * CH, CH)],
                                                    gain, shift, ALU.mult, ALU.add).then_inc(affine, 1)


def split_projections(nc, name, w, xn, part):
    with ExitStack() as ctx:
        s = Scope(nc, ctx, name)
        wqk = s.sb("wqk", [P, 2, D])
        bqk = s.sb("bqk", [P, 4])
        load_phase(nc, name + "_load", [(wqk[:, 0], w["wq"]), (wqk[:, 1], w["wk"]), (bqk[:], w["bqk"])])
        raw, rest = s.sb("raw", [P, 2, CH]), s.sb("rest", [P, 2, CH])
        proj = s.ps("proj", [P, 2, CH])
        proj_full, raw_ready, high_ready, rest_ready, mid_ready, low_ready = (
            s.sem("proj_full"), s.sem("raw_ready"), s.sem("high_ready"), s.sem("rest_ready"), s.sem("mid_ready"),
            s.sem("low_ready"))

        def place(n, i, l):
            return part[:, i, l, n * CH:n * CH + CH] if isinstance(n, int) else part[:, i, l, ds(n * CH, CH)]

        with nc.Block() as block:
            @block.tensor
            def _(pe):
                with nc.tensor.Fori(0, NCH) as n:
                    for i in range(2):
                        pe.wait_ge(raw_ready, n * 2 + i + 1)
                        nc.tensor.matmul(proj[:, i], wqk[:, i], xn[:, ds(n * CH, CH)], start=True,
                                         stop=True).then_inc(proj_full, 1)

            @block.scalar
            def _(act):
                def high(n, i):
                    act.wait_ge(raw_ready, n * 2 + i + 3)
                    nc.scalar.activation(place(n, i, 0), raw[:, i], ACT.Copy).then_inc(high_ready, 1)

                def middle(n, i):
                    act.wait_ge(rest_ready, n * 2 + i + 1)
                    nc.scalar.activation(place(n, i, 1), rest[:, i], ACT.Copy).then_inc(mid_ready, 1)

                def chunk(n, first):
                    high(n, 0)
                    if not first:
                        middle(n - 1, 1)
                    high(n, 1)
                    middle(n, 0)

                chunk(0, True)
                with nc.scalar.Fori(1, NCH) as n:
                    chunk(n, False)
                middle(NCH - 1, 1)

            @block.vector
            def _(dve):
                dve.sem_inc(raw_ready, 2)

                def take(n, i, first):
                    dve.wait_ge(proj_full, n * 2 + i + 1)
                    if not first:
                        dve.wait_ge(rest_ready, n * 2 + i - 1)
                    nc.vector.tensor_scalar(raw[:, i], proj[:, i], bqk[:, i:i + 1], None, ALU.add).then_inc(raw_ready, 1)

                def rests(n, i, first):
                    dve.wait_ge(high_ready, n * 2 + i + 1)
                    if not first:
                        dve.wait_ge(low_ready, n * 2 + i - 1)
                    nc.vector.tensor_tensor(rest[:, i], raw[:, i], place(n, i, 0), ALU.subtract).then_inc(rest_ready, 1)

                def low(n, i):
                    dve.wait_ge(mid_ready, n * 2 + i + 1)
                    nc.vector.tensor_tensor(place(n, i, 2), rest[:, i], place(n, i, 1), ALU.subtract).then_inc(low_ready, 1)

                def chunk(n, first):
                    take(n, 0, first)
                    if not first:
                        rests(n - 1, 1, isinstance(n, int) and n == 1)
                        low(n - 1, 0)
                    take(n, 1, first)
                    rests(n, 0, first)
                    if not first:
                        low(n - 1, 1)

                chunk(0, True)
                chunk(1, False)
                with nc.vector.Fori(2, NCH) as n:
                    chunk(n, False)
                rests(NCH - 1, 1, False)
                low(NCH - 1, 0)
                low(NCH - 1, 1)


def narrow_attention(nc, name, w, c, xn, res):
    with ExitStack() as ctx:
        s = Scope(nc, ctx, name)
        wv, bv = s.sb("wv", [P, QUADS * P]), s.sb("bv", [1, QUADS * P])
        wo = s.sb("wo", [P, QUADS, D])
        selq = s.sb("selq", [P, QUADS * 2 * 3 * P], BF16)
        selk = s.sb("selk", [P, QUADS * 2 * 3 * P], BF16)
        sumbc = s.sb("sumbc", [P, P])
        kone = s.sb("kone", [P, 1])
        identb = s.sb("identb", [P, P], BF16)
        ones1 = s.sb("ones1", [1, P])
        mask_qk, mask_kq = s.sb("mask_qk", [P, P], BF16), s.sb("mask_kq", [P, P], BF16)
        part = s.sb("part", [P, 2, 3, TOK], BF16)
        split_projections(nc, name + "p", w, xn, part)
        load_phase(nc, name + "_load", [
            (wv[:], w["wv"]), (bv[:], w["bv"]), (wo[:], w["wo"].rearrange("q p n -> p q n")),
            (selq[:], c["selq"]), (selk[:], c["selk"]), (sumbc[:], c["sumbc"]), (kone[:], c["kone"]),
            (identb[:], c["identb"]), (ones1[:], c["ones1"]), (mask_qk[:], c["mask_qk"]),
            (mask_kq[:], c["mask_kq"])])

        UNITS = BATCH * QUADS
        RING = 4
        BANKS = 3
        xb = s.sb("xb", [P, SEQ])
        wo_u = s.sb("wo_u", [P, D])
        kx = s.sb("kx", [P, 2, 2, SEQ], BF16)
        qx = s.sb("qx", [P, 2, SEQ], BF16)
        qxm = s.sb("qxm", [P, 2, SEQ], BF16)
        vq = s.sb("vq", [P, 2, TPB, P])
        halfmax = s.sb("halfmax", [P, TPB, 4, 2])
        negmax = s.sb("negmax", [P, TPB, 4])
        negrest = s.sb("negrest", [P, TPB, 4])
        mst = s.sb("mst", [P, TPB, 2, P], BF16)
        pr = s.sb("pr", [P, RING, 2, CH])
        osum = s.sb("osum", [P, CH])
        rsum = s.sb("rsum", [P, CH])
        ctxt = s.sb("ctxt", [P, 2, CH])
        ab = s.ps("ab", [P, BANKS, CH])
        st = s.ps("st", [P, 2, 2, CH])
        ob = s.ps("ob", [P, CH])

        xb_ready, wo_ready = s.sem("xb_ready"), s.sem("wo_ready")
        ab_full, ab_done = s.sem("ab_full"), s.sem("ab_done")
        max_step, max_ready = s.sem("max_step"), s.sem("max_ready")
        st_full, exp_done, pv_done = s.sem("st_full"), s.sem("exp_done"), s.sem("pv_done")
        o_copied, ctx_ready, zeroed = s.sem("o_copied"), s.sem("ctx_ready"), s.sem("zeroed")

        halves = [(qb, half, h) for qb in range(TPB) for half in range(2) if half * CH < (qb + 1) * P
                  for h in range(4)]
        steps = [(ch, kb, g) for ch in range(2) for kb in range(4 * ch + 4) for g in range(2)]
        NA, NST = len(halves), len(steps)
        assert NST % RING == 0
        NST0 = sum(1 for ch, _, _ in steps if ch == 0)
        LEAD = 4
        AT_SUMS = NST0 + 4
        CARRY = [t for t in range(LEAD, NST) if t not in (AT_SUMS, AT_SUMS + 1, NST - 2, NST - 1)]
        PREP, TURN, OUT = 10, 4, 3
        MSTEPS = 5
        FIRST = (PREP + NA + TURN) + (PREP + NA + 1 + TURN)
        BODY = OUT + PREP + NA + 1 + TURN
        assert BODY % BANKS == 0

        def jobs_before(u):
            if isinstance(u, int) and u == 0:
                return PREP + NA + TURN, (PREP + NA + TURN) % BANKS
            return u * BODY + (FIRST - BODY), FIRST % BANKS

        def first_set_until(t):
            return sum(1 for x in CARRY if x < t) * NA // len(CARRY)

        def columns_of(qb, half):
            return min(CH, (qb + 1) * P - half * CH)

        def units(engine, setup, body):
            setup()
            body(0, 0, False, True)
            body(1, 1, True, True)
            with engine.Fori(1, UNITS // 2 - 1) as m:
                body(m * 2, 0, True, True)
                body(m * 2 + 1, 1, True, True)
            body(UNITS - 2, 0, True, True)
            body(UNITS - 1, 1, True, False)

        def sequence_and_quad(u):
            return u // QUADS, u % QUADS

        with nc.Block() as block:
            @block.gpsimd
            def _(pool):
                nc.gpsimd.memset(mst[:], 0.0).then_inc(zeroed, 1)
                nc.gpsimd.memset(halfmax[:], -3.0e38).then_inc(zeroed, 1)

            @block.tensor
            def _(pe):
                def job(base, bank0, k, products):
                    pe.wait_ge(ab_done, base + k + 1)
                    for i, (at, n, lhsT, rhs) in enumerate(products):
                        last = nc.tensor.matmul(ab[:, (bank0 + k) % BANKS, at:at + n], lhsT, rhs, start=i == 0,
                                                stop=i == len(products) - 1, skip_group_check=True)
                    last.then_inc(ab_full, 1)

                def stack(base, bank0, k, u, i, more=None):
                    b, q = sequence_and_quad(u)
                    sel = selk if i else selq
                    for g in range(2):
                        for ch in range(2):
                            job(base, bank0, k, [(0, CH, sel[:, ds(q * 6 * P + (g * 3 + l) * P, P)],
                                                part[:, i, l, ds(b * SEQ + ch * CH, CH)]) for l in range(3)]
                                + ([(j * P, P, mst[:, ch * 4 + j, g], identb[:]) for j in range(4)] if more else []))
                            k += 1

                def prepare(base, bank0, k, u, usl):
                    stack(base, bank0, k, u, 1)
                    stack(base, bank0, k + 4, u, 0)
                    b, q = sequence_and_quad(u)
                    pe.wait_ge(xb_ready, u // 2 + 1)
                    for half in range(2):
                        pe.wait_ge(ab_done, base + k + 8 + half + 1)
                        for j in range(4):
                            kb = half * 4 + j
                            out = ab[:, (bank0 + k + 8 + half) % BANKS, j * P:j * P + P]
                            nc.tensor.matmul(out, xb[:, kb * P:kb * P + P], wv[:, ds(q * P, P)], start=True, stop=False,
                                             skip_group_check=True)
                            last = nc.tensor.matmul(out, ones1[:], bv[:, ds(q * P, P)], start=False, stop=True,
                                                    skip_group_check=True)
                        last.then_inc(ab_full, 1)

                def first_set(base, bank0, k, usl, lo, hi):
                    for n in range(lo, hi):
                        qb, half, h = halves[n]
                        g, r, cols = h // 2, 64 * (h % 2), columns_of(qb, half)
                        diag = qb // 4 == half
                        bank = (bank0 + k + n) % BANKS
                        pe.wait_ge(ab_done, base + k + n + 1)
                        last = nc.tensor.matmul(ab[:, bank, 0:cols], qx[r:r + 64, g, qb * P:qb * P + P],
                                                kx[r:r + 64, usl, g, half * CH:half * CH + cols],
                                                start=True, stop=not diag, skip_group_check=True)
                        if diag:
                            last = nc.tensor.matmul(ab[:, bank, cols - P:cols], identb[:], mask_qk[:],
                                                    start=False, stop=True, skip_group_check=True)
                        last.then_inc(ab_full, 1)

                def turn(base, bank0, k, u):
                    pe.wait_ge(max_ready, u + 1)
                    stack(base, bank0, k, u, 0, more=True)

                def weigh(u, sl, t):
                    ch, kb, g = steps[t]
                    at = max(0, kb - 4 * ch) * P
                    pe.wait_ge(exp_done, u * NST + t + 3)
                    if kb == 0 and g == 0:
                        pe.wait_ge(o_copied, u * 2 + ch + 1)
                    for jj in range(2):
                        h = 2 * g + jj
                        mm = nc.tensor.matmul(ob[32 * h:32 * h + 32, at:CH], vq[:, sl, kb, 32 * h:32 * h + 32],
                                              pr[:, t % RING, jj, at:CH], start=kb == 0, stop=kb == 4 * ch + 3,
                                              skip_group_check=True)
                    mm.then_inc(pv_done, 1)

                def step(u, sl, t):
                    ch, kb, g = steps[t]
                    at = max(0, kb - 4 * ch) * P
                    diag = kb >= 4 * ch
                    pe.wait_ge(exp_done, u * NST + t + 1)
                    for jj in range(2):
                        r = 64 * jj
                        mm = nc.tensor.matmul(st[:, g, jj, at:CH], kx[r:r + 64, sl, g, kb * P:kb * P + P],
                                              qxm[r:r + 64, g, ch * CH + at:ch * CH + CH],
                                              start=True, stop=not diag, skip_group_check=True)
                        if diag:
                            mm = nc.tensor.matmul(st[:, g, jj, at:at + P], identb[:], mask_kq[:],
                                                  start=False, stop=True, skip_group_check=True)
                    mm.then_inc(st_full, 1)
                    if t >= 2:
                        weigh(u, sl, t - 2)

                def sums(base, bank0, k, u, ch):
                    pe.wait_ge(o_copied, u * 2 + ch + 2)
                    job(base, bank0, k, [(0, CH, sumbc[:], osum[:])])

                def output(base, bank0, k, u):
                    pe.wait_ge(wo_ready, u + 1)
                    pe.wait_ge(ctx_ready, u * 2 + 3)
                    for ch in range(2):
                        job(base, bank0, k + ch, [(0, CH, wo_u[:], ctxt[:, ch])])

                def setup():
                    pe.wait_ge(zeroed, 2)
                    prepare(0, 0, 0, 0, 0)
                    pe.wait_ge(ab_done, PREP + BANKS)
                    first_set(0, 0, PREP, 0, 0, NA)
                    turn(0, 0, PREP + NA, 0)

                def body(u, sl, after, before):
                    base, bank0 = jobs_before(u)
                    k = 0
                    pe.wait_ge(ab_done, base + BANKS)
                    if after:
                        sums(base, bank0, k, u - 1, 1)
                        k += 1
                    for t in range(LEAD):
                        step(u, sl, t)
                    if before:
                        prepare(base, bank0, k, u + 1, 1 - sl)
                        k += PREP
                    if after:
                        output(base, bank0, k, u - 1)
                        k += OUT - 1
                    if before:
                        pe.wait_ge(ab_done, base + k + BANKS)
                    for t in range(LEAD, NST):
                        step(u, sl, t)
                        if before:
                            first_set(base, bank0, k + (t >= AT_SUMS), 1 - sl, first_set_until(t), first_set_until(t + 1))
                        if t == AT_SUMS - 1:
                            sums(base, bank0, k + (first_set_until(t + 1) if before else 0), u, 0)
                    weigh(u, sl, NST - 2)
                    weigh(u, sl, NST - 1)
                    k += 1
                    if before:
                        turn(base, bank0, k + NA, u + 1)
                    else:
                        sums(base, bank0, k, u, 1)
                        output(base, bank0, k + 1, u)

                units(nc.tensor, setup, body)

            @block.scalar
            def _(act):
                act.sem_inc(exp_done, 2)
                act.sem_inc(o_copied, 1)

                def copy_context(u, ch):
                    act.wait_ge(pv_done, u * NST + (NST if ch else NST0) + RING)
                    act.wait_ge(ctx_ready, u * 2 + ch + 1)
                    nc.scalar.activation(osum[:], ob[:], ACT.Copy).then_inc(o_copied, 1)

                with nc.scalar.Fori(0, UNITS) as u:
                    for t, (ch, kb, g) in enumerate(steps):
                        at = max(0, kb - 4 * ch) * P
                        act.wait_ge(st_full, u * NST + t + 1)
                        act.wait_ge(pv_done, u * NST + t + 1)
                        nc.scalar.activation(pr[:, t % RING, :, at:CH], st[:, g, :, at:CH], ACT.Exp,
                                             scale=SCALE8).then_inc(exp_done, 1)
                        if t == NST0 + 1:
                            copy_context(u, 0)
                    copy_context(u, 1)

            @block.vector
            def _(dve):
                dve.sem_inc(ab_done, BANKS)
                dve.sem_inc(pv_done, RING)
                dve.sem_inc(ctx_ready, 1)

                def empty(base, bank0, k, dst, add=None):
                    dve.wait_ge(ab_full, base + k + 1)
                    if add is None:
                        nc.vector.tensor_copy(dst, ab[:, (bank0 + k) % BANKS]).then_inc(ab_done, 1)
                    else:
                        nc.vector.tensor_scalar(dst, ab[:, (bank0 + k) % BANKS], add, None, ALU.add).then_inc(ab_done, 1)

                def empty_stack(base, bank0, k, dst, add=None):
                    for g in range(2):
                        for ch in range(2):
                            empty(base, bank0, k, dst[:, g, ch * CH:ch * CH + CH], add)
                            k += 1

                def prepare(base, bank0, k, u, usl):
                    if usl == 0:
                        b, q = sequence_and_quad(u)
                        nc.vector.tensor_scalar(xb[:], xn[:, ds(b * SEQ, SEQ)], 1.0, None, ALU.mult).then_inc(xb_ready, 1)
                    empty_stack(base, bank0, k, kx[:, usl], kone[:])
                    empty_stack(base, bank0, k + 4, qx[:])
                    for half in range(2):
                        empty(base, bank0, k + 8 + half,
                              vq[:, usl, half * 4:half * 4 + 4].rearrange("p a b -> p (a b)"))

                def maxima(base, bank0, k, lo, hi):
                    for n in range(lo, hi):
                        qb, half, h = halves[n]
                        dve.wait_ge(ab_full, base + k + n + 1)
                        nc.vector.tensor_reduce(halfmax[:, qb, h, half:half + 1],
                                                ab[:, (bank0 + k + n) % BANKS, 0:columns_of(qb, half)], AX.X,
                                                ALU.max).then_inc(ab_done, 1)

                def split_maxima(base, k, u):
                    dve.wait_ge(ab_done, base + k + BANKS)
                    nc.vector.tensor_reduce(negmax[:], halfmax[:], AX.X, ALU.max, negate=True).then_inc(max_step, 1)
                    cols = [mst[:].rearrange("p t g (j r) -> p t (g j) r", j=2)[:, :, :, M_ROW + l] for l in range(3)]
                    dve.wait_ge(max_step, u * MSTEPS + 1)
                    nc.vector.tensor_copy(cols[0], negmax[:]).then_inc(max_step, 1)
                    dve.wait_ge(max_step, u * MSTEPS + 2)
                    nc.vector.tensor_tensor(negrest[:], negmax[:], cols[0], ALU.subtract).then_inc(max_step, 1)
                    dve.wait_ge(max_step, u * MSTEPS + 3)
                    nc.vector.tensor_copy(cols[1], negrest[:]).then_inc(max_step, 1)
                    dve.wait_ge(max_step, u * MSTEPS + 4)
                    nc.vector.tensor_tensor(cols[2], negrest[:], cols[1], ALU.subtract).then_inc(max_step, 1)
                    dve.wait_ge(max_step, u * MSTEPS + 5)
                    dve.sem_inc(max_ready, 1)

                def normalise(base, bank0, k, u, ch):
                    dve.wait_ge(ab_full, base + k + 1)
                    nc.vector.reciprocal(rsum[:], ab[:, (bank0 + k) % BANKS]).then_inc(ab_done, 1)
                    dve.wait_ge(ab_done, base + k + 1 + BANKS)
                    nc.vector.tensor_tensor(ctxt[:, ch], osum[:], rsum[:], ALU.mult).then_inc(ctx_ready, 1)
                    dve.wait_ge(ctx_ready, u * 2 + ch + 2)

                def bring_wo(u):
                    b, q = sequence_and_quad(u)
                    nc.vector.tensor_scalar(wo_u[:], wo[:, ds(q, 1)].rearrange("p a n -> p (a n)"), 1.0, None,
                                            ALU.mult).then_inc(wo_ready, 1)

                def store(base, bank0, k, u):
                    b, q = sequence_and_quad(u)
                    for ch in range(2):
                        dve.wait_ge(ab_full, base + k + ch + 1)
                        cols = ds(b * SEQ + ch * CH, CH)
                        nc.vector.tensor_tensor(res[:, cols], res[:, cols], ab[:, (bank0 + k + ch) % BANKS],
                                                ALU.add).then_inc(ab_done, 1)

                def setup():
                    dve.wait_ge(zeroed, 2)
                    prepare(0, 0, 0, 0, 0)
                    maxima(0, 0, PREP, 0, NA)
                    split_maxima(0, PREP + NA, 0)
                    empty_stack(0, 0, PREP + NA, qxm[:])

                def body(u, sl, after, before):
                    base, bank0 = jobs_before(u)
                    k = 0
                    if after:
                        bring_wo(u - 1)
                        normalise(base, bank0, k, u - 1, 1)
                        k += 1
                    if before:
                        prepare(base, bank0, k, u + 1, 1 - sl)
                        k += PREP
                    if after:
                        store(base, bank0, k, u - 1)
                        k += OUT - 1
                    at_sums = first_set_until(AT_SUMS) if before else 0
                    maxima(base, bank0, k, 0, at_sums)
                    normalise(base, bank0, k + at_sums, u, 0)
                    k += 1
                    if before:
                        maxima(base, bank0, k, at_sums, NA)
                        split_maxima(base, k + NA, u + 1)
                        empty_stack(base, bank0, k + NA, qxm[:])
                    else:
                        bring_wo(u)
                        normalise(base, bank0, k, u, 1)
                        store(base, bank0, k + 1, u)

                units(nc.vector, setup, body)


def headwise_attention(nc, name, w, c, xn, res, latent=False):
    NB = TOK // P
    HH = HEADS * HEADS
    with ExitStack() as ctx:
        s = Scope(nc, ctx, name)
        wqkv = s.sb("wqkv", [P, D if latent else 3 * D])
        bqkv = s.sb("bqkv", [P, 3 * D])
        wo, bo = s.sb("wo", [P, D]), s.sb("bo", [P, 1])
        ident = s.sb("ident", [P, P])
        loads = [(wqkv[:], w["wqkv"]), (bqkv[:], w["bqkv"].broadcast_to([P, 3 * D])), (wo[:], w["wo"]),
                 (bo[:], w["bo"]), (ident[:], c["ident"])]
        if latent:
            RANK = w["wdown"].shape[1]
            wdown, bdown, wup = s.sb("wdown", [P, RANK]), s.sb("bdown", [RANK, 1]), s.sb("wup", [RANK, 2 * D])
            cos, sin = s.sb("cos", [P, TPB, HD]), s.sb("sin", [P, TPB, HD])
            loads += [(wdown[:], w["wdown"]), (bdown[:], w["bdown"]), (wup[:], w["wup"]),
                      (cos[:], c["cos8"]), (sin[:], c["sin8"])]
            latb = s.sb("latb", [RANK, 2, P])
            cosqk, sinqk = s.sb("cosqk", [P, 2, 2 * D]), s.sb("sinqk", [P, 2, 2 * D])
            roped = s.sb("roped", [P, 2, 2 * D])
            lat_ps = s.ps("lat_ps", [RANK, 2, CH])
        load_phase(nc, name + "_load", loads)

        xblk = s.sb("xblk", [P, 2, P])
        qkv = s.sb("qkv", [P, 2, 3 * D])
        prod = s.sb("prod", [P, 2, HEADS, HEADS, HD])
        score = s.sb("score", [P, 2, HEADS, HEADS])
        top = s.sb("top", [P, 2, HEADS])
        less = s.sb("less", [P, 2, HEADS, HEADS])
        ex = s.sb("ex", [P, 2, HEADS, HEADS])
        total = s.sb("total", [P, 2, HEADS])
        inv = s.sb("inv", [P, 2, HEADS])
        prob = s.sb("prob", [P, 2, HEADS, HEADS])
        pv = s.sb("pv", [P, 2, HEADS, HEADS, HD])
        ct = s.sb("ct", [P, 2, P])
        qkv_ps = s.ps("qkv_ps", [P, 2, CH])
        ct_ps = s.ps("ct_ps", [P, CH])
        out_ps = s.ps("out_ps", [P, CH])

        x_copied, qkv_full, qkv_read = s.sem("x_copied"), s.sem("qkv_full"), s.sem("qkv_read")
        prod_ready, scored, topped = s.sem("prod_ready"), s.sem("scored"), s.sem("topped")
        less_ready, ex_ready, summed, inverted = (s.sem("less_ready"), s.sem("ex_ready"), s.sem("summed"),
                                                  s.sem("inverted"))
        prob_ready, pv_ready = s.sem("prob_ready"), s.sem("pv_ready")
        ct_full, ct_copied, out_full, out_added = (s.sem("ct_full"), s.sem("ct_copied"), s.sem("out_full"),
                                                   s.sem("out_added"))
        if latent:
            lat_full, lat_ready, rope_part, rope_done = (s.sem("lat_full"), s.sem("lat_ready"),
                                                         s.sem("rope_part"), s.sem("rope_done"))

        def q_of(i):
            return roped[:, i % 2, 0:D] if latent else qkv[:, i % 2, 0:D]

        def k_of(i):
            return roped[:, i % 2, D:2 * D] if latent else qkv[:, i % 2, D:2 * D]

        def blocks(engine, body):
            body(0, 0, 2)
            body(1, 1, 2)
            with engine.Fori(1, (NB - 2) // 2) as n:
                body(n * 2, 0, 2)
                body(n * 2 + 1, 1, 2)
            body(NB - 2, 0, 1)
            body(NB - 1, 1, 0)

        with nc.Block() as block:
            @block.tensor
            def _(pe):
                def project(i, sl):
                    pe.wait_ge(x_copied, i + 1)
                    pe.wait_ge(qkv_read, i + 1)
                    if latent:
                        nc.tensor.matmul(lat_ps[:, sl, 0:P], wdown[:], xblk[:, sl], start=True,
                                         stop=True).then_inc(lat_full, 1)
                    mm = nc.tensor.matmul(qkv_ps[:, sl, 0:wqkv.shape[1]], xblk[:, sl], wqkv[:], start=True,
                                          stop=True)
                    if not latent:
                        mm.then_inc(qkv_full, 1)

                def project_up(i, sl):
                    if latent:
                        pe.wait_ge(lat_ready, i + 1)
                        nc.tensor.matmul(qkv_ps[:, sl, D:3 * D], latb[:, sl], wup[:], start=True,
                                         stop=True).then_inc(qkv_full, 1)

                for i in range(2):
                    project(i, i)
                    project_up(i, i)

                def body(i, sl, left):
                    if left == 2:
                        project(i + 2, sl)
                    pe.wait_ge(pv_ready, i + 1)
                    pe.wait_ge(ct_copied, i + 1)
                    for g in range(HEADS):
                        mm = nc.tensor.matmul(ct_ps[:, 0:P], pv[:, sl, g].rearrange("p h d -> p (h d)"), ident[:],
                                              start=g == 0, stop=g == HEADS - 1)
                    mm.then_inc(ct_full, 1)
                    if left == 2:
                        project_up(i + 2, sl)
                    pe.wait_ge(ct_copied, i + 2)
                    pe.wait_ge(out_added, i + 1)
                    nc.tensor.matmul(out_ps[:, 0:P], wo[:], ct[:, sl], start=True, stop=True).then_inc(out_full, 1)

                blocks(nc.tensor, body)

            @block.scalar
            def _(act):
                act.sem_inc(ct_copied, 1)

                def latent_copy(i, sl):
                    if latent:
                        act.wait_ge(lat_full, i + 1)
                        nc.scalar.activation(latb[:, sl], lat_ps[:, sl, 0:P], ACT.Identity,
                                             bias=bdown[:]).then_inc(lat_ready, 1)

                for i in range(2):
                    latent_copy(i, i)

                def body(i, sl, left):
                    act.wait_ge(less_ready, i + 1)
                    nc.scalar.activation(ex[:, sl], less[:, sl], ACT.Exp, scale=SCALE8).then_inc(ex_ready, 1)
                    if left == 2:
                        latent_copy(i + 2, sl)
                    act.wait_ge(ct_full, i + 1)
                    nc.scalar.activation(ct[:, sl], ct_ps[:, 0:P], ACT.Copy).then_inc(ct_copied, 1)

                blocks(nc.scalar, body)

            @block.gpsimd
            def _(pool):
                def products(i, sl):
                    pool.wait_ge(qkv_read, i + 3)
                    if latent:
                        v4 = qkv[:, sl, 0:2 * D].rearrange("p (n a b) -> p n a b", a=2, b=HD // 2)
                        s4 = sinqk[:, sl].rearrange("p (n a b) -> p n a b", a=2, b=HD // 2)
                        n_heads = 2 * HEADS
                        half = HD // 2
                        pool.wait_ge(scored, i + 1)
                        tab = lambda t, lo, hi: (t[:, ds(i % TPB, 1) if not isinstance(i, int)
                                                   else slice(i % TPB, i % TPB + 1), lo:hi]
                                                 .broadcast_to([P, n_heads, hi - lo]))
                        nc.gpsimd.tensor_tensor(cosqk[:, sl].rearrange("p (n b) -> p n b", b=HD),
                                                qkv[:, sl, 0:2 * D].rearrange("p (n b) -> p n b", b=HD),
                                                tab(cos, 0, HD), ALU.mult).then_inc(rope_part, 1)
                        nc.gpsimd.tensor_tensor(s4[:, :, 0], v4[:, :, 1], tab(sin, 0, half),
                                                ALU.mult).then_inc(rope_part, 1)
                        nc.gpsimd.tensor_tensor(s4[:, :, 1], v4[:, :, 0], tab(sin, half, HD),
                                                ALU.mult).then_inc(rope_part, 1)
                        pool.wait_ge(rope_part, i * 3 + 3)
                        nc.gpsimd.tensor_tensor(roped[:, sl], cosqk[:, sl], sinqk[:, sl],
                                                ALU.add).then_inc(rope_done, 1)
                        pool.wait_ge(rope_done, i + 1)
                    q3 = q_of(sl).rearrange("p (h a d) -> p h a d", a=1, d=HD).broadcast_to([P, HEADS, HEADS, HD])
                    k3 = k_of(sl).rearrange("p (a g d) -> p a g d", a=1, d=HD).broadcast_to([P, HEADS, HEADS, HD])
                    nc.gpsimd.tensor_tensor(prod[:, sl], q3, k3, ALU.mult).then_inc(prod_ready, 1)

                products(0, 0)

                def body(i, sl, left):
                    pool.wait_ge(topped, i + 1)
                    nc.gpsimd.tensor_tensor(less[:, sl], score[:, sl],
                                            top[:, sl].rearrange("p (h a) -> p h a", a=1)
                                            .broadcast_to([P, HEADS, HEADS]), ALU.subtract).then_inc(less_ready, 1)
                    if left:
                        products(i + 1, 1 - sl)

                blocks(nc.gpsimd, body)

            @block.vector
            def _(dve):
                dve.sem_inc(qkv_read, 2)
                dve.sem_inc(scored, 2)
                dve.sem_inc(out_added, 1)

                def bring(i, sl):
                    nc.vector.tensor_scalar(xblk[:, sl], xn[:, ds(i * P, P)], 1.0, None,
                                            ALU.mult).then_inc(x_copied, 1)

                def evacuate(i, sl):
                    dve.wait_ge(qkv_full, i + 1)
                    nc.vector.tensor_tensor(qkv[:, sl], qkv_ps[:, sl, 0:3 * D], bqkv[:], ALU.add).then_inc(qkv_read, 1)

                def store(i):
                    dve.wait_ge(out_full, i + 1)
                    cols = ds(i * P, P)
                    nc.vector.scalar_tensor_tensor(out=res[:, cols], in0=out_ps[:, 0:P], scalar=bo[:],
                                                   in1=res[:, cols], op0=ALU.add, op1=ALU.add).then_inc(out_added, 1)

                bring(0, 0)
                bring(1, 1)
                evacuate(0, 0)

                def body(i, sl, left):
                    dve.wait_ge(prod_ready, i + 1)
                    nc.vector.tensor_reduce(score[:, sl], prod[:, sl], AX.X, ALU.add).then_inc(scored, 1)
                    dve.wait_ge(scored, i + 3)
                    nc.vector.tensor_reduce(top[:, sl], score[:, sl], AX.X, ALU.max).then_inc(topped, 1)
                    if left:
                        evacuate(i + 1, 1 - sl)
                    if left == 2:
                        bring(i + 2, sl)
                    if not (isinstance(i, int) and i == 0):
                        store(i - 1)
                    dve.wait_ge(ex_ready, i + 1)
                    nc.vector.tensor_reduce(total[:, sl], ex[:, sl], AX.X, ALU.add).then_inc(summed, 1)
                    dve.wait_ge(summed, i + 1)
                    nc.vector.reciprocal(inv[:, sl], total[:, sl]).then_inc(inverted, 1)
                    dve.wait_ge(inverted, i + 1)
                    nc.vector.tensor_tensor(prob[:, sl], ex[:, sl],
                                            inv[:, sl].rearrange("p (h a) -> p h a", a=1)
                                            .broadcast_to([P, HEADS, HEADS]), ALU.mult).then_inc(prob_ready, 1)
                    dve.wait_ge(prob_ready, i + 1)
                    pgh = (prob[:, sl].rearrange("p h (g a) -> p g h a", a=1)
                           .broadcast_to([P, HEADS, HEADS, HD]))
                    vgd = (qkv[:, sl, 2 * D:3 * D].rearrange("p (g a d) -> p g a d", a=1, d=HD)
                           .broadcast_to([P, HEADS, HEADS, HD]))
                    nc.vector.tensor_tensor(pv[:, sl], pgh, vgd, ALU.mult).then_inc(pv_ready, 1)

                blocks(nc.vector, body)
                store(NB - 1)


EXPERTS, HID = 8, 256
NBLK = TOK // P


def route(nc, name, wg, c, xn, kind, rows, rows_f=None):
    CAP = TOK // EXPERTS
    wide = 1 if kind == "switch" else EXPERTS
    with ExitStack() as ctx:
        s = Scope(nc, ctx, name)
        gate = s.sb("gate", [P, EXPERTS])
        rev = s.sb("rev", [P, 1, EXPERTS])
        identb = s.sb("identb", [P, P], BF16)
        loads = [(gate[:], wg), (rev[:], c["rev"]), (identb[:], c["identb"])]
        if kind == "switch":
            tri, onesb = s.sb("tri", [P, P], BF16), s.sb("onesb", [P, P], BF16)
            loads += [(tri[:], c["tri"]), (onesb[:], c["onesb"])]
        load_phase(nc, name + "_load", loads)

        def field(n, dt=F32):
            return s.sb(n, [P, NBLK, EXPERTS], dt)

        prob, less, a, b2, hot1, hot2 = (field("prob"), field("less"), field("a"), field("b2"), field("hot1"),
                                         field("hot2"))
        hotb = field("hotb", BF16)
        top, inv = s.sb("top", [P, NBLK]), s.sb("inv", [P, NBLK])
        wt = s.sb("wt", [P, NBLK, wide])
        rest = s.sb("rest", [P, NBLK, wide])
        parts = s.sb("parts", [P, NBLK, 3, wide], BF16)
        logit_ps = s.ps("logit_ps", [P, NBLK, EXPERTS])
        count_ps = s.ps("count_ps", [P, NBLK, EXPERTS])
        row_ps = s.ps("row_ps", [3 * wide, 2, CH])
        logits, less_ready, exped, step = s.sem("logits"), s.sem("less_ready"), s.sem("exped"), s.sem("step")
        hot_ready, counted, parted = s.sem("hot_ready"), s.sem("counted"), s.sem("parted")
        row_full, row_copied = s.sem("row_full"), s.sem("row_copied")
        rev_b = rev[:].broadcast_to([P, NBLK, EXPERTS])

        def over(t):
            return t[:].rearrange("p (n a) -> p n a", a=1).broadcast_to([P, NBLK, EXPERTS])

        with nc.Block() as block:
            @block.tensor
            def _(pe):
                for i in range(NBLK):
                    mm = nc.tensor.matmul(logit_ps[:, i], xn[:, i * P:i * P + P], gate[:], start=True, stop=True)
                mm.then_inc(logits, 1)
                if kind == "switch":
                    pe.wait_ge(hot_ready, 1)
                    nc.tensor.matmul(count_ps[:].rearrange("p n e -> p (n e)"), tri[:],
                                     hotb[:].rearrange("p n e -> p (n e)"), start=True, stop=False,
                                     skip_group_check=True)
                    for i in range(NBLK - 1):
                        mm = nc.tensor.matmul(count_ps[:, i + 1:], onesb[:],
                                              hotb[:, i:i + 1].broadcast_to([P, NBLK - 1 - i, EXPERTS]),
                                              start=False, stop=i == NBLK - 2, skip_group_check=True)
                    mm.then_inc(counted, 1)
                pe.wait_ge(parted, 1)
                for n in range(NCH):
                    if n >= 2:
                        pe.wait_ge(row_copied, n - 1)
                    for j in range(4):
                        mm = nc.tensor.matmul(row_ps[:, n % 2, j * P:j * P + P],
                                              parts[:, n * 4 + j].rearrange("p l e -> p (l e)"), identb[:],
                                              start=True, stop=True)
                    mm.then_inc(row_full, 1)

            @block.scalar
            def _(act):
                act.wait_ge(less_ready, 1)
                nc.scalar.activation(a[:], less[:], ACT.Exp).then_inc(exped, 1)
                for n in range(NCH):
                    act.wait_ge(row_full, n + 1)
                    if rows_f is not None:
                        nc.scalar.activation(rows_f[:, n * CH:n * CH + CH], row_ps[:, n % 2], ACT.Copy)
                    nc.scalar.activation(rows[:, n * CH:n * CH + CH], row_ps[:, n % 2],
                                         ACT.Copy).then_inc(row_copied, 1)

            @block.vector
            def _(dve):
                k = 0

                def chained(instruction):
                    nonlocal k
                    k += 1
                    instruction.then_inc(step, 1)
                    dve.wait_ge(step, k)

                dve.wait_ge(logits, 1)
                chained(nc.vector.tensor_reduce(top[:], logit_ps[:], AX.X, ALU.max))
                nc.vector.tensor_tensor(less[:], logit_ps[:], over(top), ALU.subtract).then_inc(less_ready, 1)
                dve.wait_ge(exped, 1)
                chained(nc.vector.tensor_reduce(top[:], a[:], AX.X, ALU.add))
                chained(nc.vector.reciprocal(inv[:], top[:]))
                chained(nc.vector.tensor_tensor(prob[:], a[:], over(inv), ALU.mult))

                def first_max(src, hot):
                    chained(nc.vector.tensor_reduce(top[:], src[:], AX.X, ALU.max))
                    chained(nc.vector.tensor_tensor(b2[:], src[:], over(top), ALU.is_equal))
                    chained(nc.vector.tensor_tensor(b2[:], b2[:], rev_b, ALU.mult))
                    chained(nc.vector.tensor_reduce(top[:], b2[:], AX.X, ALU.max))
                    chained(nc.vector.tensor_tensor(hot[:], b2[:], over(top), ALU.is_equal))

                first_max(prob, hot1)
                if kind == "switch":
                    nc.vector.tensor_copy(hotb[:], hot1[:]).then_inc(hot_ready, 1)
                    dve.wait_ge(counted, 1)
                    chained(nc.vector.scalar_tensor_tensor(out=hot2[:], in0=count_ps[:], scalar=float(CAP),
                                                           in1=hot1[:], op0=ALU.is_le, op1=ALU.mult))
                    chained(nc.vector.tensor_tensor(less[:], prob[:], hot2[:], ALU.mult))
                    chained(nc.vector.tensor_reduce(wt[:].rearrange("p n e -> p (n e)"), less[:], AX.X, ALU.add))
                else:
                    chained(nc.vector.scalar_tensor_tensor(out=less[:], in0=hot1[:], scalar=-2.0, in1=prob[:],
                                                           op0=ALU.mult, op1=ALU.add))
                    first_max(less, hot2)
                    chained(nc.vector.tensor_tensor(hot1[:], hot1[:], hot2[:], ALU.add))
                    chained(nc.vector.tensor_tensor(wt[:], prob[:], hot1[:], ALU.mult))
                    if kind == "two_normed":
                        chained(nc.vector.tensor_reduce(top[:], wt[:], AX.X, ALU.add))
                        chained(nc.vector.tensor_scalar(top[:], top[:], 1e-9, None, ALU.add))
                        chained(nc.vector.reciprocal(inv[:], top[:]))
                        chained(nc.vector.tensor_tensor(wt[:], wt[:], over(inv), ALU.mult))
                chained(nc.vector.tensor_copy(parts[:, :, 0], wt[:]))
                chained(nc.vector.tensor_tensor(rest[:], wt[:], parts[:, :, 0], ALU.subtract))
                chained(nc.vector.tensor_copy(parts[:, :, 1], rest[:]))
                nc.vector.tensor_tensor(parts[:, :, 2], rest[:], parts[:, :, 1], ALU.subtract).then_inc(parted, 1)


def experts(nc, name, w, c, xn, res, biased):
    KR = 3 * EXPERTS
    with ExitStack() as ctx:
        s = Scope(nc, ctx, name)
        rows = s.sb("rows", [KR, TOK], BF16)
        rows_f = s.sb("rows_f", [KR, TOK]) if biased else None
        w1, w3 = s.sb("w1", [P, EXPERTS, HID]), s.sb("w3", [P, EXPERTS, HID])
        w2 = s.sb("w2", [P, EXPERTS, 2, D])
        spread = s.sb("spread", [KR, EXPERTS, P], BF16)
        loads = [(w1[:], w["w1"].rearrange("e d h -> d e h")), (w3[:], w["w3"].rearrange("e d h -> d e h")),
                 (w2[:], w["w2"].rearrange("e (f p) d -> p e f d", p=P)), (spread[:], c["spread"])]
        if biased:
            b13, b2 = s.sb("b13", [P, 2, EXPERTS, 2]), s.sb("b2", [KR, D])
            loads += [(b13[:], w["b13"]), (b2[:], w["b2"])]
        load_phase(nc, name + "_load", loads)
        route(nc, name + "r", w["gate"], c, xn, "two_normed" if biased else "two", rows, rows_f)

        act1 = s.sb("act1", [P, 2, CH])
        mixed = s.sb("mixed", [P, 2, CH])
        weighed = s.sb("weighed", [P, 2, CH])
        wb = s.sb("wb", [P, 2, CH])
        h1, h3 = s.ps("h1", [P, 2, CH]), s.ps("h3", [P, 2, CH])
        wb_ps, y_ps = s.ps("wb_ps", [P, 2, CH]), s.ps("y_ps", [P, CH])
        h_full, act_done, mixed_done, weighed_done = (s.sem("h_full"), s.sem("act_done"), s.sem("mixed_done"),
                                                      s.sem("weighed_done"))
        wb_full, wb_copied, used, y_full, y_added = (s.sem("wb_full"), s.sem("wb_copied"), s.sem("used"),
                                                     s.sem("y_full"), s.sem("y_added"))
        J = 2 * EXPERTS

        with nc.Block() as block:
            @block.tensor
            def _(pe):
                with nc.tensor.Fori(0, NCH) as n:
                    cols = ds(n * CH, CH)

                    def down(j):
                        e, f = j // 2, j % 2
                        pe.wait_ge(weighed_done, n * J + j + 3)
                        if j == 0:
                            pe.wait_ge(y_added, n + 1)
                        nc.tensor.matmul(y_ps[:], w2[:, e, f], weighed[:, f], start=j == 0,
                                         stop=j == J - 1).then_inc(used, 1)
                        if j == 0 and biased:
                            nc.tensor.matmul(y_ps[:], b2[:], rows_f[:, cols], start=False, stop=False)

                    for j in range(J):
                        e, f = j // 2, j % 2
                        if f == 0:
                            pe.wait_ge(wb_copied, n * EXPERTS + e + 1)
                        pe.wait_ge(mixed_done, n * J + j + 1)
                        nc.tensor.matmul(h1[:, f], w1[:, e, f * P:f * P + P], xn[:, cols], start=True, stop=True)
                        nc.tensor.matmul(h3[:, f], w3[:, e, f * P:f * P + P], xn[:, cols], start=True,
                                         stop=True).then_inc(h_full, 1)
                        if f == 0:
                            nc.tensor.matmul(wb_ps[:, e % 2], spread[:, e], rows[:, cols], start=True,
                                             stop=True).then_inc(wb_full, 1)
                        if j >= 2:
                            down(j - 2)
                    down(J - 2)
                    down(J - 1)
                    pe.wait_ge(used, n * J + J + 2)
                    pe.sem_inc(y_full, 1)

            @block.scalar
            def _(act):
                act.sem_inc(wb_copied, 2)
                with nc.scalar.Fori(0, NCH) as n:
                    for j in range(J):
                        e, f = j // 2, j % 2
                        act.wait_ge(h_full, n * J + j + 1)
                        act.wait_ge(mixed_done, n * J + j + 1)
                        bias = dict(bias=b13[:, 0, e, f:f + 1]) if biased else {}
                        nc.scalar.activation(act1[:, f], h1[:, f], ACT.Silu, **bias).then_inc(act_done, 1)
                        if f == 0:
                            act.wait_ge(wb_full, n * EXPERTS + e + 1)
                            act.wait_ge(weighed_done, n * J + j + 1)
                            nc.scalar.activation(wb[:, e % 2], wb_ps[:, e % 2], ACT.Copy).then_inc(wb_copied, 1)

            @block.vector
            def _(dve):
                dve.sem_inc(mixed_done, 2)
                dve.sem_inc(y_added, 1)
                dve.sem_inc(used, 2)
                with nc.vector.Fori(0, NCH) as n:
                    for j in range(J):
                        e, f = j // 2, j % 2
                        dve.wait_ge(act_done, n * J + j + 1)
                        dve.wait_ge(weighed_done, n * J + j + 1)
                        if biased:
                            nc.vector.scalar_tensor_tensor(out=mixed[:, f], in0=h3[:, f],
                                                           scalar=b13[:, 1, e, f:f + 1], in1=act1[:, f],
                                                           op0=ALU.add, op1=ALU.mult).then_inc(mixed_done, 1)
                        else:
                            nc.vector.tensor_tensor(mixed[:, f], h3[:, f], act1[:, f],
                                                    ALU.mult).then_inc(mixed_done, 1)
                    dve.wait_ge(y_full, n + 1)
                    cols = ds(n * CH, CH)
                    nc.vector.tensor_tensor(res[:, cols], res[:, cols], y_ps[:], ALU.add).then_inc(y_added, 1)

            @block.gpsimd
            def _(pool):
                pool.sem_inc(weighed_done, 2)
                with nc.gpsimd.Fori(0, NCH) as n:
                    for j in range(J):
                        e, f = j // 2, j % 2
                        pool.wait_ge(wb_copied, n * EXPERTS + e + 3)
                        pool.wait_ge(mixed_done, n * J + j + 3)
                        pool.wait_ge(used, n * J + j + 1)
                        nc.gpsimd.tensor_tensor(weighed[:, f], mixed[:, f], wb[:, e % 2],
                                                ALU.mult).then_inc(weighed_done, 1)


def switch_ffn(nc, name, w, c, xn, res):
    with ExitStack() as ctx:
        s = Scope(nc, ctx, name)
        rows = s.sb("rows", [3, TOK], BF16)
        we, be, ones3 = s.sb("we", [P, D]), s.sb("be", [P, 1]), s.sb("ones3", [3, P], BF16)
        load_phase(nc, name + "_load", [(we[:], w["we"]), (be[:], w["be"]), (ones3[:], c["onesb"][0:3])])
        route(nc, name + "r", w["wg"], c, xn, "switch", rows)
        y = s.sb("y", [P, 2, CH])
        gated = s.sb("gated", [P, 2, CH])
        y_ps, g_ps = s.ps("y_ps", [P, 2, CH]), s.ps("g_ps", [P, 2, CH])
        full, y_ready, gated_done, added = s.sem("full"), s.sem("y_ready"), s.sem("gated_done"), s.sem("added")
        with nc.Block() as block:
            @block.tensor
            def _(pe):
                with nc.tensor.Fori(0, NCH // 2) as n:
                    for i in range(2):
                        cols = ds(n * 2 * CH + i * CH, CH)
                        pe.wait_ge(gated_done, n * 2 + i + 1)
                        nc.tensor.matmul(y_ps[:, i], we[:], xn[:, cols], start=True, stop=True)
                        nc.tensor.matmul(g_ps[:, i], ones3[:], rows[:, cols], start=True, stop=True).then_inc(full, 1)

            @block.scalar
            def _(act):
                with nc.scalar.Fori(0, NCH // 2) as n:
                    for i in range(2):
                        act.wait_ge(full, n * 2 + i + 1)
                        act.wait_ge(gated_done, n * 2 + i + 1)
                        nc.scalar.activation(y[:, i], y_ps[:, i], ACT.Identity, bias=be[:]).then_inc(y_ready, 1)

            @block.vector
            def _(dve):
                dve.sem_inc(gated_done, 2)
                with nc.vector.Fori(0, NCH // 2) as n:
                    for i in range(2):
                        cols = ds(n * 2 * CH + i * CH, CH)
                        dve.wait_ge(y_ready, n * 2 + i + 1)
                        nc.vector.tensor_tensor(gated[:, i], y[:, i], g_ps[:, i], ALU.mult).then_inc(gated_done, 1)
                        dve.wait_ge(gated_done, n * 2 + i + 3)
                        nc.vector.tensor_tensor(res[:, cols], res[:, cols], gated[:, i], ALU.add).then_inc(added, 1)
                        dve.wait_ge(added, n * 2 + i + 1)


def constants_experts(c):
    bf = np.dtype("bfloat16")
    c["rev"] = np.tile(np.arange(EXPERTS, 0, -1, dtype=np.float32), (P, 1)).reshape(P, 1, EXPERTS)
    i, j = np.arange(P)[:, None], np.arange(P)[None, :]
    c["tri"] = (i <= j).astype(bf)
    c["onesb"] = np.ones((P, P), bf)
    spread = np.zeros((3, EXPERTS, EXPERTS, P), np.float32)
    for e in range(EXPERTS):
        spread[:, e, e] = 1
    c["spread"] = spread.reshape(3 * EXPERTS, EXPERTS, P).astype(bf)


def layout_experts(I, t):
    t["f1_gate"] = I["L1_ffn_gate_w"].T
    t["f1_w1"], t["f1_w3"], t["f1_w2"] = I["L1_ffn_w1"], I["L1_ffn_w3"], I["L1_ffn_w2"]
    t["f2_gate"] = I["L2_ffn_router_w"].T
    t["f2_w1"], t["f2_w3"], t["f2_w2"] = I["L2_ffn_gate_w"], I["L2_ffn_up_w"], I["L2_ffn_down_w"]
    b13 = np.stack([I["L2_ffn_gate_b"], I["L2_ffn_up_b"]]).reshape(2, EXPERTS, 2, P)
    t["f2_b13"] = b13.transpose(3, 0, 1, 2)
    t["f2_b2"] = np.concatenate([I["L2_ffn_down_b"]] * 3)


def retention(nc, name, w, c, xn, res, eps_col):
    with ExitStack() as ctx:
        s = Scope(nc, ctx, name)
        wqk = s.sb("wqk", [P, 4, D])
        wv, wgate, wproj = s.sb("wv", [P, D]), s.sb("wgate", [P, D]), s.sb("wproj", [P, D])
        gn = s.sb("gn", [P, 2])
        rope = s.sb("rope", [P, 4, SEQ])
        decay = s.sb("decay", [P, HEADS, P])
        dq, dk = s.sb("dq", [P, 1, P]), s.sb("dk", [P, 1, P])
        dchunk = s.sb("dchunk", [P, 1])
        headmask = s.sb("headmask", [P, HEADS])
        blockmask = s.sb("blockmask", [P, 1, P])
        headmean = s.sb("headmean", [P, P])
        ident = s.sb("ident", [P, P])
        load_phase(nc, name + "_load", [
            (wqk[:], w["wqk"]), (wv[:], w["wv"]), (wgate[:], w["wgate"]), (wproj[:], w["wproj"]), (gn[:], w["gn"]),
            (rope[:], c["ret_rope"]), (decay[:], c["ret_decay"]), (dq[:], c["ret_dq"]), (dk[:], c["ret_dk"]),
            (dchunk[:], c["ret_dchunk"]), (headmask[:], c["headmask"]), (blockmask[:], c["blockmask"]),
            (headmean[:], c["headmean"]), (ident[:], c["ident"])])

        xb = s.sb("xb", [P, SEQ])
        qk = s.sb("qk", [P, 4, SEQ])
        qr, kr = s.sb("qr", [P, SEQ]), s.sb("kr", [P, SEQ])
        qdec, kdec = s.sb("qdec", [P, TPB, P]), s.sb("kdec", [P, TPB, P])
        kt = s.sb("kt", [P, TPB, P])
        v = s.sb("v", [P, TPB, P])
        kv = s.sb("kv", [P, TPB - 1, P])
        state = s.sb("state", [P, TPB, P])
        km = s.sb("km", [P, 2, SEQ])
        sd = s.sb("sd", [P, 2, TPB, P])
        gate = s.sb("gate", [P, SEQ])
        yt = s.sb("yt", [P, TPB, P])
        yf, cen, z, zg = s.sb("yf", [P, SEQ]), s.sb("cen", [P, SEQ]), s.sb("z", [P, SEQ]), s.sb("zg", [P, SEQ])
        sq = s.sb("sq", [P, SEQ])
        stat = s.sb("stat", [P, 6])
        ab = s.ps("ab", [P, 2, CH])
        st = s.ps("st", [P, 2, TPB, P])
        y_ps = s.ps("y_ps", [P, TPB, P])

        copied, ab_full, ab_done = s.sem("copied"), s.sem("ab_full"), s.sem("ab_done")
        roped, decayed = s.sem("roped"), s.sem("decayed")
        gate_full, gate_done = s.sem("gate_full"), s.sem("gate_done")
        kt_full, kt_copied, kv_full, kv_copied, state_step = (s.sem("kt_full"), s.sem("kt_copied"), s.sem("kv_full"),
                                                              s.sem("kv_copied"), s.sem("state_step"))
        km_ready, st_full, sd_ready, y_step, y_full, y_copied = (s.sem("km_ready"), s.sem("st_full"),
                                                                 s.sem("sd_ready"), s.sem("y_step"),
                                                                 s.sem("y_full"), s.sem("y_copied"))
        stat_step, squared, rooted, z_ready, zg_ready, added = (s.sem("stat_step"), s.sem("squared"), s.sem("rooted"),
                                                                s.sem("z_ready"), s.sem("zg_ready"), s.sem("added"))
        zeroed = s.sem("zeroed")
        JOBS = 16
        V_JOB, YT_JOB, MEAN_JOB, VAR_JOB, OUT_JOB = 8, 10, 12, 13, 14
        STATS = 7

        with nc.Block() as block:
            @block.tensor
            def _(pe):
                with nc.tensor.Fori(0, BATCH) as b:
                    base = b * JOBS

                    def take(k):
                        pe.wait_ge(ab_done, base + k + 1)
                        return k % 2

                    pe.wait_ge(copied, b + 1)
                    for i in range(4):
                        for ch in range(2):
                            sl = take(2 * i + ch)
                            nc.tensor.matmul(ab[:, sl], wqk[:, i], xb[:, ch * CH:ch * CH + CH], start=True,
                                             stop=True).then_inc(ab_full, 1)
                    for half in range(2):
                        sl = take(V_JOB + half)
                        for j in range(4):
                            t = half * 4 + j
                            mm = nc.tensor.matmul(ab[:, sl, j * P:j * P + P], xb[:, t * P:t * P + P], wv[:],
                                                  start=True, stop=True)
                        mm.then_inc(ab_full, 1)
                    pe.wait_ge(y_copied, b + 1)
                    for ch in range(2):
                        mm = nc.tensor.matmul(y_ps[:, 4 * ch:4 * ch + 4].rearrange("p a b -> p (a b)"), wgate[:],
                                              xb[:, ch * CH:ch * CH + CH], start=True, stop=True)
                    mm.then_inc(gate_full, 1)
                    pe.wait_ge(decayed, b * 2 + 2)
                    for t in range(TPB):
                        mm = nc.tensor.matmul(st[:, 0, t], kdec[:, t], ident[:], start=True, stop=True)
                    mm.then_inc(kt_full, 1)
                    pe.wait_ge(kt_copied, b + 1)
                    pe.wait_ge(ab_done, base + V_JOB + 2 + 2)
                    for t in range(TPB - 1):
                        mm = nc.tensor.matmul(st[:, 1, t], kt[:, t], v[:, t], start=True, stop=True)
                    mm.then_inc(kv_full, 1)
                    pe.wait_ge(state_step, b * (TPB - 1) + TPB - 1)
                    pe.wait_ge(gate_done, b + 1)
                    for t in range(TPB):
                        nc.tensor.matmul(y_ps[:, t], qdec[:, t], state[:, t], start=t % 4 == 0, stop=False,
                                         skip_group_check=True)

                    def within(h):
                        pe.wait_ge(sd_ready, b * HEADS + h + 3)
                        for t in range(TPB):
                            mm = nc.tensor.matmul(y_ps[:, t, h * HD:h * HD + HD], sd[:, h % 2, t],
                                                  v[:, t, h * HD:h * HD + HD], start=False, stop=h == HEADS - 1,
                                                  skip_group_check=True)
                        mm.then_inc(y_step, 1)

                    for h in range(HEADS):
                        pe.wait_ge(km_ready, b * HEADS + h + 1)
                        pe.wait_ge(sd_ready, b * HEADS + h + 1)
                        for t in range(TPB):
                            mm = nc.tensor.matmul(st[:, h % 2, t], km[:, h % 2, t * P:t * P + P],
                                                  qr[:, t * P:t * P + P], start=True, stop=True)
                        mm.then_inc(st_full, 1)
                        if h:
                            within(h - 1)
                    within(HEADS - 1)
                    pe.wait_ge(y_copied, b + 2)
                    for half in range(2):
                        sl = take(YT_JOB + half)
                        for j in range(4):
                            mm = nc.tensor.matmul(ab[:, sl, j * P:j * P + P], yt[:, half * 4 + j], ident[:],
                                                  start=True, stop=True)
                        mm.then_inc(ab_full, 1)
                    pe.wait_ge(stat_step, b * STATS + 1)
                    nc.tensor.matmul(ab[:, take(MEAN_JOB), 0:1], headmean[:], stat[:, 0:1], start=True,
                                     stop=True).then_inc(ab_full, 1)
                    pe.wait_ge(squared, b + 1)
                    nc.tensor.matmul(ab[:, take(VAR_JOB), 0:1], headmean[:], stat[:, 1:2], start=True,
                                     stop=True).then_inc(ab_full, 1)
                    pe.wait_ge(zg_ready, b + 1)
                    for ch in range(2):
                        sl = take(OUT_JOB + ch)
                        nc.tensor.matmul(ab[:, sl], wproj[:], zg[:, ch * CH:ch * CH + CH], start=True,
                                         stop=True).then_inc(ab_full, 1)

            @block.scalar
            def _(act):
                act.sem_inc(y_copied, 1)
                with nc.scalar.Fori(0, BATCH) as b:
                    act.wait_ge(gate_full, b + 1)
                    nc.scalar.activation(gate[:], y_ps[:].rearrange("p a b -> p (a b)"), ACT.Silu).then_inc(gate_done, 1)
                    act.wait_ge(kt_full, b + 1)
                    nc.scalar.activation(kt[:], st[:, 0], ACT.Copy).then_inc(kt_copied, 1)
                    act.wait_ge(y_step, b * HEADS + HEADS + 2)
                    nc.scalar.activation(yt[:], y_ps[:], ACT.Copy).then_inc(y_copied, 1)
                    act.wait_ge(stat_step, b * STATS + 2)
                    nc.scalar.activation(sq[:], cen[:], ACT.Square, accum_out=stat[:, 1:2]).then_inc(squared, 1)
                    act.wait_ge(stat_step, b * STATS + 3)
                    nc.scalar.activation(stat[:, 3:4], stat[:, 2:3], ACT.Sqrt).then_inc(rooted, 1)

            @block.gpsimd
            def _(pool):
                nc.gpsimd.memset(state[:], 0.0).then_inc(zeroed, 1)
                with nc.gpsimd.Fori(0, BATCH) as b:
                    pool.wait_ge(ab_done, b * JOBS + 4 + 2)
                    nc.gpsimd.tensor_tensor(qr[:], qk[:, 0], qk[:, 1], ALU.add).then_inc(roped, 1)
                    pool.wait_ge(ab_done, b * JOBS + 8 + 2)
                    nc.gpsimd.tensor_tensor(kr[:], qk[:, 2], qk[:, 3], ALU.add).then_inc(roped, 1)
                    pool.wait_ge(roped, b * 2 + 2)
                    nc.gpsimd.tensor_tensor(kdec[:], kr[:].rearrange("p (t n) -> p t n", n=P),
                                            dk[:].broadcast_to([P, TPB, P]), ALU.mult).then_inc(decayed, 1)
                    nc.gpsimd.tensor_tensor(qdec[:], qr[:].rearrange("p (t n) -> p t n", n=P),
                                            dq[:].broadcast_to([P, TPB, P]), ALU.mult).then_inc(decayed, 1)
                    pool.wait_ge(z_ready, b + 1)
                    nc.gpsimd.tensor_tensor(zg[:], z[:], gate[:], ALU.mult).then_inc(zg_ready, 1)

            @block.vector
            def _(dve):
                dve.sem_inc(ab_done, 2)
                dve.sem_inc(sd_ready, 2)
                dve.sem_inc(y_step, 2)
                dve.wait_ge(zeroed, 1)
                with nc.vector.Fori(0, BATCH) as b:
                    base = b * JOBS
                    nc.vector.tensor_scalar(xb[:], xn[:, ds(b * SEQ, SEQ)], 1.0, None, ALU.mult).then_inc(copied, 1)
                    for i in range(4):
                        for ch in range(2):
                            k = 2 * i + ch
                            cols = slice(ch * CH, ch * CH + CH)
                            dve.wait_ge(ab_full, base + k + 1)
                            nc.vector.tensor_tensor(qk[:, i, cols], ab[:, k % 2], rope[:, i, cols],
                                                    ALU.mult).then_inc(ab_done, 1)
                    for half in range(2):
                        k = V_JOB + half
                        dve.wait_ge(ab_full, base + k + 1)
                        nc.vector.tensor_copy(v[:, 4 * half:4 * half + 4].rearrange("p a b -> p (a b)"),
                                              ab[:, k % 2]).then_inc(ab_done, 1)
                    dve.wait_ge(kv_full, b + 1)
                    nc.vector.tensor_tensor(kv[:], st[:, 1, 0:TPB - 1], blockmask[:].broadcast_to([P, TPB - 1, P]),
                                            ALU.mult).then_inc(kv_copied, 1)
                    dve.wait_ge(kv_copied, b + 1)
                    for t in range(TPB - 1):
                        nc.vector.scalar_tensor_tensor(out=state[:, t + 1], in0=state[:, t], scalar=dchunk[:],
                                                       in1=kv[:, t], op0=ALU.mult, op1=ALU.add).then_inc(state_step, 1)
                        dve.wait_ge(state_step, b * (TPB - 1) + t + 1)

                    def mask_k(h):
                        dve.wait_ge(roped, b * 2 + 2)
                        nc.vector.tensor_scalar(km[:, h % 2], kr[:], headmask[:, h:h + 1], None,
                                                ALU.mult).then_inc(km_ready, 1)

                    mask_k(0)
                    mask_k(1)
                    for h in range(HEADS):
                        dve.wait_ge(st_full, b * HEADS + h + 1)
                        dve.wait_ge(y_step, b * HEADS + h + 1)
                        nc.vector.tensor_tensor(sd[:, h % 2], st[:, h % 2],
                                                decay[:, h:h + 1].broadcast_to([P, TPB, P]),
                                                ALU.mult).then_inc(sd_ready, 1)
                        if h + 2 < HEADS:
                            mask_k(h + 2)
                    for half in range(2):
                        k = YT_JOB + half
                        dve.wait_ge(ab_full, base + k + 1)
                        nc.vector.tensor_copy(yf[:, half * CH:half * CH + CH], ab[:, k % 2]).then_inc(ab_done, 1)
                    dve.wait_ge(ab_done, base + YT_JOB + 2 + 2)
                    nc.vector.tensor_reduce(stat[:, 0:1], yf[:], AX.X, ALU.add).then_inc(stat_step, 1)
                    dve.wait_ge(ab_full, base + MEAN_JOB + 1)
                    nc.vector.tensor_scalar(cen[:], yf[:], ab[:, MEAN_JOB % 2, 0:1], None,
                                            ALU.subtract).then_inc(stat_step, 1)
                    dve.wait_ge(stat_step, b * STATS + 2)
                    dve.sem_inc(ab_done, 1)
                    dve.wait_ge(ab_full, base + VAR_JOB + 1)
                    nc.vector.tensor_scalar(stat[:, 2:3], ab[:, VAR_JOB % 2, 0:1], EPS, None,
                                            ALU.add).then_inc(stat_step, 1)
                    dve.wait_ge(stat_step, b * STATS + 3)
                    dve.sem_inc(ab_done, 1)
                    dve.wait_ge(rooted, b + 1)
                    nc.vector.reciprocal(stat[:, 4:5], stat[:, 3:4]).then_inc(stat_step, 1)
                    dve.wait_ge(stat_step, b * STATS + 4)
                    nc.vector.tensor_tensor(stat[:, 5:6], stat[:, 4:5], gn[:, 0:1], ALU.mult).then_inc(stat_step, 1)
                    dve.wait_ge(stat_step, b * STATS + 5)
                    nc.vector.tensor_scalar(z[:], cen[:], stat[:, 5:6], gn[:, 1:2], ALU.mult,
                                            ALU.add).then_inc(z_ready, 1)
                    dve.sem_inc(stat_step, 2)
                    for ch in range(2):
                        k = OUT_JOB + ch
                        dve.wait_ge(ab_full, base + k + 1)
                        cols = ds(b * SEQ + ch * CH, CH)
                        nc.vector.tensor_tensor(res[:, cols], res[:, cols], ab[:, k % 2], ALU.add).then_inc(ab_done, 1)


def constants_retention(c):
    f = np.float32
    half = np.arange(0, HD, 2, dtype=f)
    inv = (1.0 / f(10000.0) ** (half / f(HD))).astype(f)
    t = np.arange(SEQ, dtype=f)
    ang = np.repeat((t[:, None] * inv[None, :]).astype(f), 2, axis=-1)
    vec = ((half + f(0.4 * HD)) / f(1.4 * HD)).astype(f)
    power = ((t - SEQ // 2) / f(512.0)).astype(f)
    scale = np.repeat((vec[None, :] ** power[:, None]).astype(f), 2, axis=-1)
    cos, sin = np.cos(ang), np.sin(ang) * np.tile(np.array([-1, 1], f), HD // 2)
    four = [cos * scale, sin * scale, cos / scale, sin / scale]
    c["ret_rope"] = np.stack([np.tile(a.T, (HEADS, 1)) for a in four], axis=1).astype(f)
    gamma = 1.0 - 2.0 ** (-5.0 - np.arange(HEADS, dtype=np.float64))
    d = np.arange(P)[None, :] - np.arange(P)[:, None]
    dec = np.where(d[:, None, :] >= 0, gamma[None, :, None] ** np.maximum(d, 0)[:, None, :], 0.0)
    c["ret_decay"] = (dec * HD ** -0.5).astype(f)
    rows = np.repeat(gamma, HD)[:, None]
    c["ret_dq"] = (rows ** (np.arange(P)[None, :] + 1) * HD ** -0.5).astype(f).reshape(P, 1, P)
    c["ret_dk"] = (rows ** (P - 1 - np.arange(P)[None, :])).astype(f).reshape(P, 1, P)
    c["ret_dchunk"] = (rows ** P).astype(f)
    head = np.arange(P) // HD
    c["headmask"] = (head[:, None] == np.arange(HEADS)[None, :]).astype(f)
    same = (head[:, None] == head[None, :]).astype(f)
    c["blockmask"] = same.reshape(P, 1, P)
    c["headmean"] = same * f(1.0 / (HD * SEQ))


def layout_retention(I, t):
    q, k, v = (I["L2_attn_w_qkv"][i * D:i * D + D].T for i in range(3))
    partner = np.arange(D) ^ 1
    t["a2_wqk"] = np.stack([q, q[:, partner], k, k[:, partner]], axis=1)
    t["a2_wv"], t["a2_wgate"], t["a2_wproj"] = v, I["L2_attn_w_gated"].T, I["L2_attn_w_proj"].T
    t["a2_gn"] = columns(I["L2_attn_gn_weight"], I["L2_attn_gn_bias"])


WH, WD, WINDOW, DEPTH = 8, 64, 64, 2
INNER = WH * WD
SPAN = WINDOW + P
FF = int(D * 4 * 2 / 3)


def shift_tokens(nc, name, src, dst):
    HALF = D // 2
    with ExitStack() as ctx:
        s = Scope(nc, ctx, name)
        moved = s.sem("moved")
        seqs = lambda t, lo, hi: t[lo:hi].rearrange("p (b n) -> p b n", b=BATCH)
        with nc.Block() as block:
            @block.vector
            def _(dve):
                nc.vector.tensor_copy(dst[0:HALF], src[0:HALF]).then_inc(moved, 1)

            @block.scalar
            def _(act):
                nc.scalar.activation(seqs(dst, HALF, D)[:, :, 1:], seqs(src, HALF, D)[:, :, :SEQ - 1],
                                     ACT.Copy).then_inc(moved, 1)

            @block.gpsimd
            def _(pool):
                nc.gpsimd.memset(seqs(dst, HALF, D)[:, :, 0:1], 0.0).then_inc(moved, 1)


def window_attention(nc, name, w, c, ht, src, dst):
    NB = TOK // P
    PAIRS = INNER // P
    SLOT_HEAD = [4 * (bank // 2) + 2 * col + bank % 2 for bank in range(4) for col in range(2)]
    HALVES = (1, 0)
    WS = float(8.0)
    VW = WD + 1
    with ExitStack() as ctx:
        s = Scope(nc, ctx, name)
        wqkv, wo = s.sb("wqkv", [P, 3, INNER]), s.sb("wo", [P, PAIRS, D])
        table = s.sb("table", [P, TPB, 4, WD])
        gains = s.sb("gains", [P, 1, 4, WD])
        mask = s.sb("mask", [P, TPB, SPAN], BF16)
        ident, identb = s.sb("ident", [P, P]), s.sb("identb", [P, P], BF16)
        load_phase(nc, name + "_load", [
            (wqkv[:], w["wqkv"].rearrange("d (a n) -> d a n", a=3)), (wo[:], w["wo"].rearrange("(j p) d -> p j d", p=P)),
            (table[:], c["win_rope"]), (gains[:], w["gains"].broadcast_to([P, 4 * WD]).rearrange(
                "p (a f d) -> p a f d", a=1, f=4)), (mask[:], c["win_mask"]), (ident[:], c["ident"]),
            (identb[:], c["identb"])])
        hb = s.sb("hb", [P, 2, P])
        squares = s.sb("squares", [P, 2, 2 * WH, WD])
        norm2, clipped, rnorm = s.sb("norm2", [P, 2, 2 * WH]), s.sb("clipped", [P, 2, 2 * WH]), s.sb(
            "rnorm", [P, 2, 2 * WH])
        minus_half = s.sb("minus_half", [P, 2 * WH])
        rot_a, rot_b = s.sb("rot_a", [P, 2, 2, INNER]), s.sb("rot_b", [P, 2, 2, INNER])
        rot = s.sb("rot", [P, 2, 2, INNER])
        qk = s.sb("qk", [P, 2, 2, INNER])
        qt, kt = s.sb("qt", [P, 2, PAIRS, P]), s.sb("kt", [P, 2, PAIRS, SPAN])
        v, vprev = s.sb("v", [P, 2, WH, VW]), s.sb("vprev", [WINDOW, 2, WH, VW])
        top = s.sb("top", [P, 2, WH])
        less, ex = s.sb("less", [P, 2, WH, SPAN]), s.sb("ex", [P, 2, WH, SPAN])
        pt, ptprev = s.sb("pt", [P, WH, P]), s.sb("ptprev", [WINDOW, WH, P])
        inv = s.sb("inv", [P, 2, WH])
        o, ot = s.sb("o", [P, 2, INNER]), s.sb("ot", [P, 2, PAIRS, P])
        sets = s.ps("sets", [P, 2, 4, CH])

        ready = s.sem("ready")
        hb_ready, qk_full, v_full, squared, v_copied = (s.sem("hb_ready"), s.sem("qk_full"), s.sem("v_full"),
                                                        s.sem("squared"), s.sem("v_copied"))
        rotated, norm_step, norm_ready, rnorm_ready, qk_ready = (s.sem("rotated"), s.sem("norm_step"),
                                                               s.sem("norm_ready"), s.sem("rnorm_ready"),
                                                               s.sem("qk_ready"))
        t_full, qkt_copied, s_full, topped, less_ready, ex_ready = (
            s.sem("t_full"), s.sem("qkt_copied"), s.sem("s_full"), s.sem("topped"), s.sem("less_ready"),
            s.sem("ex_ready"))
        pt_full, pt_copied, o_full, inverted, o_ready, vprev_copied = (
            s.sem("pt_full"), s.sem("pt_copied"), s.sem("o_full"), s.sem("inverted"), s.sem("o_ready"),
            s.sem("vprev_copied"))
        ot_full, ot_copied, out_full, added = s.sem("ot_full"), s.sem("ot_copied"), s.sem("out_full"), s.sem("added")

        def of_block(i):
            return slice(i % TPB, i % TPB + 1) if isinstance(i, int) else ds(i % TPB, 1)

        def blocks(engine, first, body):
            first(0, 0)
            body(0, 0, 2)
            body(1, 1, 2)
            with engine.Fori(1, (NB - 2) // 2) as n:
                body(n * 2, 0, 2)
                body(n * 2 + 1, 1, 2)
            body(NB - 2, 0, 1)
            body(NB - 1, 1, 0)

        with nc.Block() as block:
            @block.gpsimd
            def _(pool):
                nc.gpsimd.memset(v[:], 1.0).then_inc(ready, 1)
                nc.gpsimd.memset(vprev[:], 0.0).then_inc(ready, 1)
                nc.gpsimd.memset(kt[:], 0.0).then_inc(ready, 1)
                nc.gpsimd.memset(minus_half[:], -0.5).then_inc(ready, 1)

            @block.vector
            def _(dve):
                nc.vector.tensor_tensor(table[:], table[:], gains[:].broadcast_to([P, TPB, 4, WD]),
                                        ALU.mult).then_inc(ready, 1)

        with nc.Block() as block:
            @block.tensor
            def _(pe):
                def project_qk(i, sl):
                    pe.wait_ge(hb_ready, i + 1)
                    for j in range(2):
                        mm = nc.tensor.matmul(sets[:, sl, j], hb[:, sl], wqkv[:, j], start=True, stop=True)
                    mm.then_inc(qk_full, 1)

                def project_v(i, sl):
                    nc.tensor.matmul(sets[:, sl, 2], hb[:, sl], wqkv[:, 2], start=True, stop=True).then_inc(v_full, 1)

                def turn_qk(i, sl):
                    pe.wait_ge(qk_ready, i + 1)
                    for a in range(2):
                        for j in range(PAIRS):
                            mm = nc.tensor.transpose(sets[:, sl, a, j * P:j * P + P], qk[:, sl, a, j * P:j * P + P],
                                                     ident[:])
                    mm.then_inc(t_full, 1)

                def scores(i, sl):
                    pe.wait_ge(v_copied, i + 1)
                    pe.wait_ge(added, i + 1)
                    for half in HALVES:
                        for bank in (2 * half, 2 * half + 1):
                            nc.tensor.matmul(sets[:, sl, bank, 0:2 * SPAN].rearrange("p (a n) -> p a n", a=2),
                                             identb[:], mask[:, of_block(i)].broadcast_to([P, 2, SPAN]), start=True,
                                             stop=False, skip_group_check=True)
                        if half == HALVES[0]:
                            pe.wait_ge(qkt_copied, i * 3 + 3)
                        for u in (4 * half, 4 * half + 2, 4 * half + 1, 4 * half + 3):
                            h = SLOT_HEAD[u]
                            r = WD * (h % 2)
                            mm = nc.tensor.matmul(sets[:, sl, u // 2, u % 2 * SPAN:u % 2 * SPAN + SPAN],
                                                  qt[r:r + WD, sl, h // 2], kt[r:r + WD, sl, h // 2], start=False,
                                                  stop=True, skip_group_check=True)
                        mm.then_inc(s_full, 1)

                def turn_p(i, sl):
                    for n, half in enumerate(HALVES):
                        pe.wait_ge(ex_ready, i * 2 + n + 1)
                        for a, lo, hi in ((0, WINDOW, SPAN), (1, 0, P)):
                            for j in range(4):
                                mm = nc.tensor.transpose(sets[:, sl, 2 * half + a, j * P:j * P + P],
                                                         ex[:, sl, 4 * half + j, lo:hi], ident[:])
                        mm.then_inc(pt_full, 1)

                def values(i, sl):
                    pe.wait_ge(vprev_copied, i + 1)
                    for n, half in enumerate(HALVES):
                        pe.wait_ge(pt_copied, i * 4 + 2 * n + 2)
                        for u in range(4 * half, 4 * half + 4):
                            h = SLOT_HEAD[u]
                            out = sets[:, sl, 2 * half, h % 4 * VW:h % 4 * VW + VW]
                            nc.tensor.matmul(out, pt[:, u], v[:, sl, h], start=True, stop=False,
                                             skip_group_check=True)
                            mm = nc.tensor.matmul(out, ptprev[:, u], vprev[:, sl, h], start=False, stop=True,
                                                  skip_group_check=True)
                    mm.then_inc(o_full, 1)

                def turn_o(i, sl):
                    pe.wait_ge(o_ready, i + 1)
                    for j in range(PAIRS):
                        mm = nc.tensor.transpose(sets[:, sl, 2, j * P:j * P + P], o[:, sl, j * P:j * P + P], ident[:])
                    mm.then_inc(ot_full, 1)

                def output(i, sl):
                    pe.wait_ge(ot_copied, i + 1)
                    for j in range(PAIRS):
                        mm = nc.tensor.matmul(sets[:, sl, 3, 0:P], wo[:, j], ot[:, sl, j], start=j == 0,
                                              stop=j == PAIRS - 1)
                    mm.then_inc(out_full, 1)

                def first(i, sl):
                    project_qk(i, sl)
                    project_v(i, sl)
                    turn_qk(i, sl)
                    scores(i, sl)

                def body(i, sl, left):
                    if left:
                        project_qk(i + 1, 1 - sl)
                    if not (isinstance(i, int) and i == 0):
                        output(i - 1, 1 - sl)
                    turn_p(i, sl)
                    if left:
                        project_v(i + 1, 1 - sl)
                    values(i, sl)
                    if left:
                        turn_qk(i + 1, 1 - sl)
                    turn_o(i, sl)
                    if left:
                        scores(i + 1, 1 - sl)
                    else:
                        output(i, sl)

                blocks(nc.tensor, first, body)

            @block.scalar
            def _(act):
                act.sem_inc(vprev_copied, 2)

                def square(i, sl):
                    act.wait_ge(qk_full, i + 1)
                    nc.scalar.activation(squares[:, sl].rearrange("p h d -> p (h d)"),
                                         sets[:, sl, 0:2].rearrange("p a n -> p (a n)"), ACT.Square).then_inc(squared, 1)

                def copy_v(i, sl):
                    act.wait_ge(v_full, i + 1)
                    nc.scalar.activation(v[:, sl, :, 0:WD], sets[:, sl, 2].rearrange("p (h d) -> p h d", h=WH),
                                         ACT.Copy).then_inc(v_copied, 1)

                def copy_qkt(i, sl):
                    act.wait_ge(t_full, i + 1)
                    nc.scalar.activation(qt[:, sl].rearrange("p j n -> p (j n)"), sets[:, sl, 0],
                                         ACT.Copy).then_inc(qkt_copied, 1)
                    keys = sets[:, sl, 1].rearrange("p (j n) -> p j n", j=PAIRS)
                    nc.scalar.activation(kt[:, sl, :, WINDOW:SPAN], keys, ACT.Copy).then_inc(qkt_copied, 1)
                    nc.scalar.activation(kt[:, 1 - sl, :, 0:WINDOW], keys[:, :, P - WINDOW:P],
                                         ACT.Copy).then_inc(qkt_copied, 1)

                def exponentials(i, sl):
                    for n, half in enumerate(HALVES):
                        act.wait_ge(less_ready, i * 2 + n + 1)
                        nc.scalar.activation(ex[:, sl, 4 * half:4 * half + 4], less[:, sl, 4 * half:4 * half + 4],
                                             ACT.Exp, scale=WS).then_inc(ex_ready, 1)

                def copy_pt(i, sl):
                    for n, half in enumerate(HALVES):
                        act.wait_ge(pt_full, i * 2 + n + 1)
                        for a, to in ((0, pt), (1, ptprev)):
                            nc.scalar.activation(to[:, 4 * half:4 * half + 4].rearrange("p u n -> p (u n)"),
                                                 sets[0:to.shape[0], sl, 2 * half + a], ACT.Copy).then_inc(pt_copied, 1)

                def copy_vprev(i, sl):
                    act.wait_ge(o_full, i + 1)
                    act.wait_ge(v_copied, i + 2)
                    nc.scalar.activation(vprev[:, sl], v[P - WINDOW:P, 1 - sl], ACT.Copy).then_inc(vprev_copied, 1)

                def copy_ot(i, sl):
                    act.wait_ge(ot_full, i + 1)
                    nc.scalar.activation(ot[:, sl].rearrange("p j n -> p (j n)"), sets[:, sl, 2],
                                         ACT.Copy).then_inc(ot_copied, 1)

                def first(i, sl):
                    square(i, sl)
                    copy_v(i, sl)
                    copy_qkt(i, sl)
                    exponentials(i, sl)
                    act.wait_ge(v_copied, 1)
                    nc.scalar.activation(vprev[:, 1], v[P - WINDOW:P, 0], ACT.Copy).then_inc(vprev_copied, 1)

                def body(i, sl, left):
                    if left:
                        square(i + 1, 1 - sl)
                    copy_pt(i, sl)
                    if left:
                        copy_v(i + 1, 1 - sl)
                        copy_qkt(i + 1, 1 - sl)
                    copy_ot(i, sl)
                    if left == 2:
                        copy_vprev(i, sl)
                    if left:
                        exponentials(i + 1, 1 - sl)

                blocks(nc.scalar, first, body)

            @block.gpsimd
            def _(pool):
                def inverse_norm(i, sl):
                    pool.wait_ge(norm_ready, i + 1)
                    nc.gpsimd.tensor_tensor(rnorm[:, sl], clipped[:, sl], minus_half[:], ALU.pow).then_inc(rnorm_ready, 1)

                def body(i, sl, left):
                    if left:
                        inverse_norm(i + 1, 1 - sl)

                blocks(nc.gpsimd, inverse_norm, body)

            @block.vector
            def _(dve):
                dve.sem_inc(added, 2)

                def bring(i, sl):
                    nc.vector.tensor_scalar(hb[:, sl], ht[:, ds(i * P, P)], 1.0, None, ALU.mult).then_inc(hb_ready, 1)

                def rotate(i, sl):
                    dve.wait_ge(squared, i + 1)
                    nc.vector.tensor_reduce(norm2[:, sl], squares[:, sl], AX.X, ALU.add).then_inc(norm_step, 1)
                    dve.wait_ge(norm_step, i + 1)
                    nc.vector.tensor_scalar(clipped[:, sl], norm2[:, sl], 1e-24, None, ALU.max).then_inc(norm_ready, 1)
                    proj = sets[:, sl, 0:2].rearrange("p a (h d) -> p a h d", d=WD)
                    half = WD // 2

                    def factor(f, lo, hi):
                        t4 = table[:, of_block(i), f:f + 2, lo:hi].rearrange("p t f (a d) -> p (t f) a d", a=1)
                        return t4.broadcast_to([P, 2, WH, hi - lo])

                    nc.vector.tensor_tensor(rot_a[:, sl].rearrange("p a (h d) -> p a h d", d=WD), proj,
                                            factor(0, 0, WD), ALU.mult).then_inc(rotated, 1)
                    part = rot_b[:, sl].rearrange("p a (h d) -> p a h d", d=WD)
                    nc.vector.tensor_tensor(part[:, :, :, 0:half], proj[:, :, :, half:WD], factor(2, 0, half),
                                            ALU.mult).then_inc(rotated, 1)
                    nc.vector.tensor_tensor(part[:, :, :, half:WD], proj[:, :, :, 0:half], factor(2, half, WD),
                                            ALU.mult).then_inc(rotated, 1)
                    dve.wait_ge(rotated, i * 4 + 3)
                    nc.vector.tensor_tensor(rot[:, sl], rot_a[:, sl], rot_b[:, sl], ALU.add).then_inc(rotated, 1)
                    dve.wait_ge(rotated, i * 4 + 4)
                    dve.wait_ge(rnorm_ready, i + 1)
                    nc.vector.tensor_tensor(qk[:, sl].rearrange("p a (h d) -> p (a h) d", d=WD),
                                            rot[:, sl].rearrange("p a (h d) -> p (a h) d", d=WD),
                                            rnorm[:, sl].rearrange("p (h a) -> p h a", a=1)
                                            .broadcast_to([P, 2 * WH, WD]), ALU.mult).then_inc(qk_ready, 1)

                def softmax_arguments(i, sl):
                    for n, half in enumerate(HALVES):
                        dve.wait_ge(s_full, i * 2 + n + 1)
                        slots = slice(4 * half, 4 * half + 4)
                        got = sets[:, sl, 2 * half:2 * half + 2, 0:2 * SPAN].rearrange("p b (c n) -> p b c n", c=2)
                        nc.vector.tensor_reduce(top[:, sl, slots].rearrange("p (b c) -> p b c", c=2), got, AX.X,
                                                ALU.max).then_inc(topped, 1)
                        dve.wait_ge(topped, i * 2 + n + 1)
                        nc.vector.tensor_tensor(less[:, sl, slots].rearrange("p (b c) n -> p b c n", c=2), got,
                                                top[:, sl, slots].rearrange("p (b c a) -> p b c a", c=2, a=1)
                                                .broadcast_to([P, 2, 2, SPAN]), ALU.subtract).then_inc(less_ready, 1)

                def normalise(i, sl):
                    dve.wait_ge(o_full, i + 1)
                    got = (sets[:, sl].rearrange("p (b x) n -> p b x n", x=2)[:, :, 0, 0:4 * VW]
                           .rearrange("p b (c n) -> p b c n", n=VW))
                    nc.vector.reciprocal(inv[:, sl].rearrange("p (b c a) -> p b c a", b=2, a=1),
                                         got[:, :, :, WD:VW]).then_inc(inverted, 1)
                    dve.wait_ge(inverted, i + 1)
                    nc.vector.tensor_tensor(o[:, sl].rearrange("p (b c n) -> p b c n", b=2, n=WD), got[:, :, :, 0:WD],
                                            inv[:, sl].rearrange("p (b c a) -> p b c a", b=2, a=1)
                                            .broadcast_to([P, 2, 4, WD]), ALU.mult).then_inc(o_ready, 1)

                def store(i, sl):
                    dve.wait_ge(out_full, i + 1)
                    cols = ds(i * P, P)
                    nc.vector.tensor_tensor(dst[:, cols], src[:, cols], sets[:, sl, 3, 0:P], ALU.add).then_inc(added, 1)

                def first(i, sl):
                    bring(0, 0)
                    bring(1, 1)
                    rotate(i, sl)
                    softmax_arguments(i, sl)

                def body(i, sl, left):
                    if left:
                        rotate(i + 1, 1 - sl)
                    if not (isinstance(i, int) and i == 0):
                        store(i - 1, 1 - sl)
                    if left == 2:
                        bring(i + 2, sl)
                    normalise(i, sl)
                    if left:
                        softmax_arguments(i + 1, 1 - sl)
                    else:
                        store(i, sl)

                blocks(nc.vector, first, body)


def geglu(nc, name, w, hn, xf, total=None):
    parts = [(j * P, min(P, FF - j * P)) for j in range((FF + P - 1) // P)]
    J = len(parts)
    with ExitStack() as ctx:
        s = Scope(nc, ctx, name)
        w1, w2 = s.sb("w1", [P, 2 * FF]), s.sb("w2", [P, J, D])
        b1, b2 = s.sb("b1", [P, 2 * J]), s.sb("b2", [P, 1])
        load_phase(nc, name + "_load", [(w1[:], w["w1"]), (w2[:], w["w2"].rearrange("(j p) d -> p j d", p=P)),
                                        (b1[:], w["b1"]), (b2[:], w["b2"])])
        g_act, u = s.sb("g_act", [P, 2, CH]), s.sb("u", [P, 2, CH])
        a_ps, g_ps, y_ps = s.ps("a_ps", [P, 2, CH]), s.ps("g_ps", [P, 2, CH]), s.ps("y_ps", [P, 2, CH])
        full, act_done, u_ready, used, y_full, y_added, total_added = (
            s.sem("full"), s.sem("act_done"), s.sem("u_ready"), s.sem("used"), s.sem("y_full"), s.sem("y_added"),
            s.sem("total_added"))
        jobs = [(i, j, (i * J + j) % 2, lo, n) for i in range(2) for j, (lo, n) in enumerate(parts)]
        NJ = len(jobs)
        with nc.Block() as block:
            @block.tensor
            def _(pe):
                with nc.tensor.Fori(0, NCH // 2) as n:
                    def down(k):
                        i, j, sl, lo, m = jobs[k]
                        pe.wait_ge(u_ready, n * NJ + k + 3)
                        if j == 0:
                            pe.wait_ge(y_added, n * 2 + i + 1)
                        mm = nc.tensor.matmul(y_ps[:, i], w2[0:m, j], u[0:m, sl], start=j == 0, stop=j == J - 1)
                        mm.then_inc(used, 1)

                    for k, (i, j, sl, lo, m) in enumerate(jobs):
                        cols = ds(n * 2 * CH + i * CH, CH)
                        pe.wait_ge(u_ready, n * NJ + k + 1)
                        nc.tensor.matmul(a_ps[0:m, sl], w1[:, lo:lo + m], hn[:, cols], start=True, stop=True)
                        nc.tensor.matmul(g_ps[0:m, sl], w1[:, FF + lo:FF + lo + m], hn[:, cols], start=True,
                                         stop=True).then_inc(full, 1)
                        if k:
                            down(k - 1)
                    down(NJ - 1)

            @block.scalar
            def _(act):
                with nc.scalar.Fori(0, NCH // 2) as n:
                    for k, (i, j, sl, lo, m) in enumerate(jobs):
                        act.wait_ge(full, n * NJ + k + 1)
                        act.wait_ge(u_ready, n * NJ + k + 1)
                        nc.scalar.activation(g_act[0:m, sl], g_ps[0:m, sl], ACT.Gelu,
                                             bias=b1[0:m, J + j:J + j + 1]).then_inc(act_done, 1)

            @block.vector
            def _(dve):
                dve.sem_inc(u_ready, 2)
                dve.sem_inc(used, 2)
                dve.sem_inc(y_added, 2)
                with nc.vector.Fori(0, NCH // 2) as n:
                    for k, (i, j, sl, lo, m) in enumerate(jobs):
                        dve.wait_ge(act_done, n * NJ + k + 1)
                        dve.wait_ge(used, n * NJ + k + 1)
                        nc.vector.scalar_tensor_tensor(out=u[0:m, sl], in0=a_ps[0:m, sl], scalar=b1[0:m, j:j + 1],
                                                       in1=g_act[0:m, sl], op0=ALU.add,
                                                       op1=ALU.mult).then_inc(u_ready, 1)
                        if j == J - 1:
                            cols = ds(n * 2 * CH + i * CH, CH)
                            dve.wait_ge(used, n * NJ + k + 3)
                            nc.vector.scalar_tensor_tensor(out=xf[:, cols], in0=y_ps[:, i], scalar=b2[:],
                                                           in1=xf[:, cols], op0=ALU.add,
                                                           op1=ALU.add).then_inc(y_added, 1)
                            if total is not None:
                                dve.wait_ge(y_added, n * 2 + i + 3)
                                nc.vector.tensor_tensor(total[:, cols], total[:, cols], xf[:, cols],
                                                        ALU.add).then_inc(total_added, 1)


def local_transformer(nc, name, w, c, xn, res, mean_w, eps_col):
    with ExitStack() as ctx:
        s = Scope(nc, ctx, name)
        xf, ht = s.sb("xf", [P, TOK]), s.sb("ht", [P, TOK])
        ln = s.sb("ln", [P, 2 * DEPTH])
        load_phase(nc, name + "_load", [(ln[:], w["ln"])])
        for l in range(DEPTH):
            wl = {k[1:]: v for k, v in w.items() if k[0] == str(l)}
            src = xf if l else xn
            shift_tokens(nc, f"{name}s{l}", src, ht)
            window_attention(nc, f"{name}w{l}", wl, c, ht, src, xf)
            shift_tokens(nc, f"{name}t{l}", xf, ht)
            layernorm(nc, f"{name}n{l}", ht, ht, mean_w, eps_col, gain=ln[:, 2 * l:2 * l + 1],
                      shift=ln[:, 2 * l + 1:2 * l + 2])
            geglu(nc, f"{name}g{l}", wl, ht, xf, res if l == DEPTH - 1 else None)


def constants_local(c):
    f = np.float32
    half = np.arange(0, WD, 2, dtype=f)
    inv = (1.0 / f(10000.0) ** (half / f(WD))).astype(f)
    t = np.arange(SEQ, dtype=f)
    ang = (t[:, None] * inv[None, :]).astype(f)
    ang = np.concatenate([ang, ang], axis=-1)
    base = ((half + f(0.4 * WD)) / f(1.4 * WD)).astype(f)
    power = ((t - SEQ // 2) / f(WINDOW // 2)).astype(f)
    scale = (base[None, :].astype(np.float64) ** power[:, None]).astype(f)
    scale = np.concatenate([scale, scale], axis=-1)
    cos = np.cos(ang)
    sin = np.sin(ang) * np.concatenate([-np.ones(WD // 2, f), np.ones(WD // 2, f)])
    four = [cos * scale, cos / scale, sin * scale, sin / scale]
    c["win_rope"] = np.stack([a.reshape(TPB, P, WD).transpose(1, 0, 2) for a in four], axis=2).astype(f)
    q, k = np.arange(P)[:, None], np.arange(SPAN)[None, :] - WINDOW
    seen = (k <= q) & (k >= q - WINDOW)
    mask = np.where(seen, 0.0, -1e30)[:, None, :].repeat(TPB, axis=1)
    mask[:, 0, :WINDOW] = -1e30
    c["win_mask"] = mask.astype(np.dtype("bfloat16"))


def layout_local(I, t):
    partner = (np.arange(WD) + WD // 2) % WD
    J = (FF + P - 1) // P
    t["f0_ln"] = columns(*[I[k][l] for l in range(DEPTH) for k in ("L0_ffn_ln_g", "L0_ffn_ln_b")])
    for l in range(DEPTH):
        qs, ks = I["L0_ffn_q_scale"][l], I["L0_ffn_k_scale"][l]
        t[f"f0_{l}wqkv"], t[f"f0_{l}wo"] = I["L0_ffn_wqkv"][l], I["L0_ffn_wo"][l]
        t[f"f0_{l}gains"] = np.concatenate([qs, ks, qs[partner], ks[partner]]).reshape(1, 4 * WD)
        t[f"f0_{l}w1"] = I["L0_ffn_w1"][l]
        w2 = np.zeros((J * P, D), np.float32)
        w2[:FF] = I["L0_ffn_w2"][l]
        t[f"f0_{l}w2"] = w2
        b1 = np.zeros((2, J * P), np.float32)
        b1[:, :FF] = I["L0_ffn_b1"][l].reshape(2, FF)
        t[f"f0_{l}b1"] = b1.reshape(2 * J, P).T
        t[f"f0_{l}b2"] = I["L0_ffn_b2"][l].reshape(D, 1)


ONLY = 0


def build_program(nc, t, out):
    with ExitStack() as ctx:
        s = Scope(nc, ctx, "all")
        x = s.sb("x", [P, TOK])
        xn = s.sb("xn", [P, TOK])
        mean_w, eps_col = s.sb("mean_w", [P, P]), s.sb("eps_col", [P, 1])
        load_phase(nc, "load_x", [(x[:], t["xT"]), (mean_w[:], t["mean_w"]), (eps_col[:], t["eps_col"])])

        def part(prefix):
            return {k[len(prefix):]: v for k, v in t.items() if k.startswith(prefix)}

        phases = [
            lambda: headwise_attention(nc, "a0", part("a0_"), t, xn, x),
            lambda: local_transformer(nc, "f0", part("f0_"), t, xn, x, mean_w, eps_col),
            lambda: narrow_attention(nc, "a1", part("a1_"), t, xn, x),
            lambda: experts(nc, "f1", part("f1_"), t, xn, x, biased=False),
            lambda: retention(nc, "a2", part("a2_"), t, xn, x, eps_col),
            lambda: experts(nc, "f2", part("f2_"), t, xn, x, biased=True),
            lambda: headwise_attention(nc, "a3", part("a3_"), t, xn, x, latent=True),
            lambda: switch_ffn(nc, "f3", part("f3_"), t, xn, x),
        ]
        for n, phase in enumerate(phases):
            if n % 2 == 0 and not ONLY:
                layernorm(nc, f"ln{n // 2}", x, xn, mean_w, eps_col)
            if ONLY and ONLY == n + 1:
                layernorm(nc, f"ln{n // 2}", x, xn, mean_w, eps_col)
            if not ONLY or ONLY == n + 1:
                phase()
        stored = s.sem("stored")
        with nc.Block() as block:
            @block.sync
            def _(sp):
                sp.dma_start(out, x[:]).then_inc(stored, 16)
                sp.wait_ge(stored, 16)


def constants():
    bf = np.dtype("bfloat16")
    f = np.float32
    c = {}
    c["mean_w"] = np.full((P, P), 1.0 / P, f)
    c["eps_col"] = np.full((P, 1), EPS, f)
    c["ident"] = np.eye(P, dtype=f)
    c["identb"] = np.eye(P).astype(bf)
    c["ones1"] = np.ones((1, P), f)
    for key, parts in (("selq", Q_PART), ("selk", K_PART)):
        sel = np.zeros((P, QUADS, 2, 3, P), f)
        for q in range(QUADS):
            for g in range(2):
                for jj in range(2):
                    head = 4 * q + 2 * g + jj
                    for slot, l in enumerate(parts):
                        for d in range(HD):
                            sel[head * HD + d, q, g, l, 64 * jj + 8 * slot + d] = 1
        c[key] = sel.reshape(P, -1).astype(bf)
    kone = np.zeros((P, 1), f)
    for jj in range(2):
        kone[64 * jj + M_ROW:64 * jj + M_ROW + 3] = 1
    c["kone"] = kone
    sumbc = np.zeros((P, P), f)
    for j in range(4):
        sumbc[32 * j + HD, 32 * j:32 * j + 32] = 1
    c["sumbc"] = sumbc
    i, j = np.arange(P)[:, None], np.arange(P)[None, :]
    c["mask_qk"] = np.where(j > i, -1e30, 0).astype(bf)
    c["mask_kq"] = np.where(i > j, -1e30, 0).astype(bf)
    inv = (1.0 / f(10000.0) ** (np.arange(0, HD, 2, dtype=f) / f(HD))).astype(f)
    ang = (np.arange(SEQ, dtype=f)[:, None] * inv[None, :]).astype(f)
    cos, sin = np.cos(ang), np.sin(ang)
    by_block = lambda a: a.reshape(TPB, P, HD).transpose(1, 0, 2)
    c["cos8"] = by_block(np.concatenate([cos, cos], 1)).astype(f)
    c["sin8"] = by_block(np.concatenate([-sin, sin], 1)).astype(f)
    constants_experts(c)
    constants_local(c)
    constants_retention(c)
    return c


def quad_columns(wv, bias):
    k = wv.shape[0]
    out = np.zeros((k, HEADS, 32), np.float32)
    out[:, :, :HD] = wv.reshape(k, HEADS, HD)
    row = np.zeros((1, HEADS, 32), np.float32)
    if bias is not None:
        row[0, :, :HD] = bias.reshape(HEADS, HD)
    row[0, :, HD] = 1
    return out.reshape(k, -1), row.reshape(1, -1)


def quad_rows(wo, bias):
    out = np.zeros((HEADS, 32, D), np.float32)
    out[:, :HD] = wo.reshape(HEADS, HD, D)
    if bias is not None:
        out[0, HD] = bias
    return out.reshape(QUADS, P, D)


def columns(*vectors):
    out = np.zeros((P, len(vectors)), np.float32)
    for i, v in enumerate(vectors):
        if v is not None:
            out[:, i] = v
    return out


def layout(I):
    t = {"xT": I["L0_attn_x"].reshape(TOK, D).T}
    wqkv = I["L0_attn_W_qkv"].reshape(D, HEADS, 3, HD)
    bqkv = I["L0_attn_b_qkv"].reshape(HEADS, 3, HD)
    t["a0_wqkv"] = wqkv.transpose(0, 2, 1, 3).reshape(D, 3 * D)
    t["a0_bqkv"] = bqkv.transpose(1, 0, 2).reshape(1, 3 * D)
    t["a0_wo"], t["a0_bo"] = I["L0_attn_W_out"], I["L0_attn_b_out"].reshape(D, 1)

    t["a1_wq"], t["a1_wk"] = I["L1_attn_Wq"], I["L1_attn_Wk"]
    t["a1_bqk"] = columns(None, None, None, None)
    t["a1_wv"], t["a1_bv"] = quad_columns(I["L1_attn_Wv"], None)
    t["a1_wo"] = quad_rows(I["L1_attn_Wo"], None)

    wup, bup = I["L3_attn_Wup"].reshape(-1, HEADS, 2, HD), I["L3_attn_bup"].reshape(HEADS, 2, HD)
    t["a3_wqkv"] = I["L3_attn_Wq"]
    t["a3_bqkv"] = np.concatenate([I["L3_attn_bq"], bup[:, 0].reshape(-1), bup[:, 1].reshape(-1)]).reshape(1, 3 * D)
    t["a3_wdown"], t["a3_bdown"] = I["L3_attn_Wdown"], I["L3_attn_bdown"].reshape(-1, 1)
    t["a3_wup"] = wup.transpose(0, 2, 1, 3).reshape(-1, 2 * D)
    t["a3_wo"], t["a3_bo"] = I["L3_attn_Wout"], I["L3_attn_bout"].reshape(D, 1)
    layout_local(I, t)
    layout_experts(I, t)
    layout_retention(I, t)
    t["f3_wg"], t["f3_we"], t["f3_be"] = I["L3_ffn_Wg"], I["L3_ffn_We"], I["L3_ffn_be"].reshape(-1, 1)
    return t


def kernel(**inputs):
    import concourse.bacc as bacc
    from concourse.bass_utils import run_bass_kernel_spmd as run

    nc = bacc.Bacc("TRN2", target_bir_lowering=False, num_devices=1)
    arrays, views = {}, {}
    for key, a in {**constants(), **layout({k: np.asarray(v) for k, v in inputs.items()})}.items():
        a = np.ascontiguousarray(a)
        arrays[f"in_{key}"] = a
        views[key] = nc.dram_tensor(f"in_{key}", a.shape, mybir.dt.from_np(a.dtype), kind="ExternalInput").ap()
    out = nc.dram_tensor("out_x", (P, TOK), F32, kind="ExternalOutput").ap()
    build_program(nc, views, out)
    r = run(nc, [arrays], core_ids=[0])
    return r.results[0]["out_x"].T.reshape(BATCH, SEQ, D)
```

```python
from contextlib import ExitStack

import numpy as np

import concourse.bass as bass
from concourse import mybir

ALU = mybir.AluOpType
ACT = mybir.ActivationFunctionType
AX = mybir.AxisListType
F32 = mybir.dt.float32
BF16 = mybir.dt.bfloat16
ds = bass.ds

P = 128
D = 128
BATCH, SEQ = 4, 1024
TOK = BATCH * SEQ
CH = 512
NCH = TOK // CH
TPB = SEQ // P
EPS = 1e-5

HEADS, HD = 16, 8
QUADS = 4
SCALE8 = float(1.0 / np.sqrt(8.0))
Q_PART = [0, 0, 1, 1, 0, 2]
K_PART = [0, 1, 0, 1, 2, 0]
M_ROW = 8 * len(Q_PART)


class Scope:

    def __init__(self, nc, ctx, name):
        self.nc, self.ctx, self.name = nc, ctx, name
        self.sems = []
        ctx.callback(self.release)

    def release(self):
        if self.sems:
            self.nc.clear_and_free_semaphores(self.sems)
            self.nc.all_engine_barrier()

    def sb(self, name, shape, dt=F32):
        return self.ctx.enter_context(self.nc.sbuf_tensor(f"{self.name}_{name}", shape, dt))

    def ps(self, name, shape, dt=F32):
        return self.ctx.enter_context(self.nc.psum_tensor(f"{self.name}_{name}", shape, dt))

    def sem(self, name):
        self.sems.append(self.nc.alloc_semaphore(f"{self.name}_{name}"))
        return self.sems[-1]


def load_phase(s, loads, meanwhile=None):
    nc = s.nc
    landed = s.sem(f"landed{len(s.sems)}")

    def start(sp):
        for dst, src in loads:
            sp.dma_start(dst, src).then_inc(landed, 16)

    if meanwhile:
        with nc.Block() as block:
            @block.sync
            def _(sp):
                start(sp)
        meanwhile()
    with nc.Block() as block:
        @block.sync
        def _(sp):
            if not meanwhile:
                start(sp)
            sp.wait_ge(landed, 16 * len(loads))


def layernorm(nc, name, src, dst, tables, gain=None, shift=None):
    centre, collect, spread, eps_col = tables
    with ExitStack() as ctx:
        s = Scope(nc, ctx, name)
        sq = s.sb("sq", [P, 2, CH])
        std, rstd = s.sb("std", [NCH, CH]), s.sb("rstd", [NCH, CH])
        cen_ps, bc_ps = s.ps("cen_ps", [P, 2, CH]), s.ps("bc_ps", [P, 2, CH])
        var_ps = s.ps("var_ps", [NCH, CH])
        centred, kept, squared, collected = s.sem("centred"), s.sem("kept"), s.sem("squared"), s.sem("collected")
        rooted, inverted, spread_out, scaled, shifted = (s.sem("rooted"), s.sem("inverted"), s.sem("spread_out"),
                                                         s.sem("scaled"), s.sem("shifted"))

        def chunk(t, n):
            return t[:, n * CH:n * CH + CH]

        with nc.Block() as block:
            @block.tensor
            def _(pe):
                def variance(n):
                    pe.wait_ge(squared, n + 1)
                    nc.tensor.matmul(var_ps[:], collect[:, n], sq[:, n % 2], start=n == 0,
                                     stop=n == NCH - 1).then_inc(collected, 1)

                for n in range(NCH):
                    if n >= 2:
                        pe.wait_ge(kept, n - 1)
                    nc.tensor.matmul(cen_ps[:, n % 2], centre[:], chunk(src, n), start=True,
                                     stop=True).then_inc(centred, 1)
                    if n:
                        variance(n - 1)
                variance(NCH - 1)
                pe.wait_ge(inverted, 1)
                for n in range(NCH):
                    if n >= 2:
                        pe.wait_ge(scaled, n - 1)
                    nc.tensor.matmul(bc_ps[:, n % 2], spread[:, n], rstd[:], start=True,
                                     stop=True).then_inc(spread_out, 1)

            @block.scalar
            def _(act):
                for n in range(NCH):
                    act.wait_ge(kept, n + 1)
                    if n >= 2:
                        act.wait_ge(collected, n - 1)
                    nc.scalar.activation(sq[:, n % 2], chunk(dst, n), ACT.Square).then_inc(squared, 1)
                act.wait_ge(collected, NCH)
                nc.scalar.activation(std[:], var_ps[:], ACT.Sqrt, bias=eps_col[0:NCH]).then_inc(rooted, 1)
                if gain is not None:
                    for n in range(NCH):
                        act.wait_ge(scaled, n + 1)
                        nc.scalar.activation(chunk(dst, n), chunk(dst, n), ACT.Identity, bias=shift).then_inc(shifted, 1)

            @block.vector
            def _(dve):
                for n in range(NCH):
                    dve.wait_ge(centred, n + 1)
                    nc.vector.tensor_copy(chunk(dst, n), cen_ps[:, n % 2]).then_inc(kept, 1)
                dve.wait_ge(rooted, 1)
                nc.vector.reciprocal(rstd[:], std[:]).then_inc(inverted, 1)
                for n in range(NCH):
                    dve.wait_ge(spread_out, n + 1)
                    if gain is None:
                        nc.vector.tensor_tensor(chunk(dst, n), chunk(dst, n), bc_ps[:, n % 2],
                                                ALU.mult).then_inc(scaled, 1)
                    else:
                        nc.vector.scalar_tensor_tensor(out=chunk(dst, n), in0=chunk(dst, n), scalar=gain,
                                                       in1=bc_ps[:, n % 2], op0=ALU.mult,
                                                       op1=ALU.mult).then_inc(scaled, 1)


def split_projections(nc, name, wqk, xn, part):
    with ExitStack() as ctx:
        s = Scope(nc, ctx, name)
        raw, rest = s.sb("raw", [P, 2, CH]), s.sb("rest", [P, 2, CH])
        proj = s.ps("proj", [P, 2, CH])
        proj_full, raw_ready, high_ready, rest_ready, mid_ready, low_ready = (
            s.sem("proj_full"), s.sem("raw_ready"), s.sem("high_ready"), s.sem("rest_ready"), s.sem("mid_ready"),
            s.sem("low_ready"))

        def place(n, i, l):
            return part[:, i, l, n * CH:n * CH + CH] if isinstance(n, int) else part[:, i, l, ds(n * CH, CH)]

        with nc.Block() as block:
            @block.tensor
            def _(pe):
                with nc.tensor.Fori(0, NCH) as n:
                    for i in range(2):
                        pe.wait_ge(raw_ready, n * 2 + i + 1)
                        nc.tensor.matmul(proj[:, i], wqk[:, i], xn[:, ds(n * CH, CH)], start=True,
                                         stop=True).then_inc(proj_full, 1)

            @block.scalar
            def _(act):
                def high(n, i):
                    act.wait_ge(raw_ready, n * 2 + i + 3)
                    nc.scalar.activation(place(n, i, 0), raw[:, i], ACT.Copy).then_inc(high_ready, 1)

                def middle(n, i):
                    act.wait_ge(rest_ready, n * 2 + i + 1)
                    nc.scalar.activation(place(n, i, 1), rest[:, i], ACT.Copy).then_inc(mid_ready, 1)

                def chunk(n, first):
                    high(n, 0)
                    if not first:
                        middle(n - 1, 1)
                    high(n, 1)
                    middle(n, 0)

                chunk(0, True)
                with nc.scalar.Fori(1, NCH) as n:
                    chunk(n, False)
                middle(NCH - 1, 1)

            @block.vector
            def _(dve):
                dve.sem_inc(raw_ready, 2)

                def take(n, i, first):
                    dve.wait_ge(proj_full, n * 2 + i + 1)
                    if not first:
                        dve.wait_ge(rest_ready, n * 2 + i - 1)
                    nc.vector.tensor_copy(raw[:, i], proj[:, i]).then_inc(raw_ready, 1)

                def rests(n, i, first):
                    dve.wait_ge(high_ready, n * 2 + i + 1)
                    if not first:
                        dve.wait_ge(low_ready, n * 2 + i - 1)
                    nc.vector.tensor_tensor(rest[:, i], raw[:, i], place(n, i, 0), ALU.subtract).then_inc(rest_ready, 1)

                def low(n, i):
                    dve.wait_ge(mid_ready, n * 2 + i + 1)
                    nc.vector.tensor_tensor(place(n, i, 2), rest[:, i], place(n, i, 1),
                                            ALU.subtract).then_inc(low_ready, 1)

                def chunk(n, first):
                    take(n, 0, first)
                    if not first:
                        rests(n - 1, 1, isinstance(n, int) and n == 1)
                        low(n - 1, 0)
                    take(n, 1, first)
                    rests(n, 0, first)
                    if not first:
                        low(n - 1, 1)

                chunk(0, True)
                chunk(1, False)
                with nc.vector.Fori(2, NCH) as n:
                    chunk(n, False)
                rests(NCH - 1, 1, False)
                low(NCH - 1, 0)
                low(NCH - 1, 1)


def narrow_attention(nc, name, w, c, xn, res, norm):
    with ExitStack() as ctx:
        s = Scope(nc, ctx, name)
        wv, bv = s.sb("wv", [P, QUADS * P]), s.sb("bv", [1, QUADS * P])
        wo = s.sb("wo", [P, QUADS, D])
        selq = s.sb("selq", [P, QUADS * 2 * 3 * P], BF16)
        selk = s.sb("selk", [P, QUADS * 2 * 3 * P], BF16)
        sumbc = s.sb("sumbc", [P, P])
        kone = s.sb("kone", [P, 1])
        identb = s.sb("identb", [P, P], BF16)
        ones1 = s.sb("ones1", [1, P])
        mask_qk, mask_kq = s.sb("mask_qk", [P, P], BF16), s.sb("mask_kq", [P, P], BF16)
        part = s.sb("part", [P, 2, 3, TOK], BF16)

        wqk = s.sb("wqk", [P, 2, D])
        load_phase(s, [(wqk[:, 0], w["wq"]), (wqk[:, 1], w["wk"])], norm)
        load_phase(s, [
            (wv[:], w["wv"]), (bv[:], w["bv"]), (wo[:], w["wo"].rearrange("q p n -> p q n")),
            (selq[:], c["selq"]), (selk[:], c["selk"]), (sumbc[:], c["sumbc"]), (kone[:], c["kone"]),
            (identb[:], c["identb"]), (ones1[:], c["ones1"]), (mask_qk[:], c["mask_qk"]),
            (mask_kq[:], c["mask_kq"])], lambda: split_projections(nc, name + "p", wqk, xn, part))

        UNITS = BATCH * QUADS
        RING = 4
        BANKS = 3
        xb = s.sb("xb", [P, SEQ])
        wo_u = s.sb("wo_u", [P, D])
        kx = s.sb("kx", [P, 2, 2, SEQ], BF16)
        qx = s.sb("qx", [P, 2, SEQ], BF16)
        qxm = s.sb("qxm", [P, 2, SEQ], BF16)
        vq = s.sb("vq", [P, 2, TPB, P])
        halfmax = s.sb("halfmax", [P, TPB, 4, 2])
        negmax = s.sb("negmax", [P, TPB, 4])
        negrest = s.sb("negrest", [P, TPB, 4])
        mst = s.sb("mst", [P, TPB, 2, P], BF16)
        pr = s.sb("pr", [P, RING, 2, CH])
        osum = s.sb("osum", [P, CH])
        rsum = s.sb("rsum", [P, CH])
        ctxt = s.sb("ctxt", [P, 2, CH])
        ab = s.ps("ab", [P, BANKS, CH])
        st = s.ps("st", [P, 2, 2, CH])
        ob = s.ps("ob", [P, CH])

        xb_ready, wo_ready = s.sem("xb_ready"), s.sem("wo_ready")
        ab_full, ab_done = s.sem("ab_full"), s.sem("ab_done")
        max_step, max_ready = s.sem("max_step"), s.sem("max_ready")
        st_full, exp_done, pv_done = s.sem("st_full"), s.sem("exp_done"), s.sem("pv_done")
        o_copied, ctx_ready, zeroed = s.sem("o_copied"), s.sem("ctx_ready"), s.sem("zeroed")

        halves = [(qb, half, h) for qb in range(TPB) for half in range(2) if half * CH < (qb + 1) * P
                  for h in range(4)]
        steps = [(ch, kb, g) for ch in range(2) for kb in range(4 * ch + 4) for g in range(2)]
        NA, NST = len(halves), len(steps)
        assert NST % RING == 0
        NST0 = sum(1 for ch, _, _ in steps if ch == 0)
        LEAD = 4
        AT_SUMS = NST0 + 3
        CARRY = [t for t in range(LEAD, NST) if t not in (AT_SUMS, AT_SUMS + 1, NST - 2, NST - 1)]
        PREP, TURN, OUT = 10, 4, 3
        MSTEPS = 5
        FIRST = (PREP + NA + TURN) + (PREP + NA + 1 + TURN)
        BODY = OUT + PREP + NA + 1 + TURN
        assert BODY % BANKS == 0

        def jobs_before(u):
            if isinstance(u, int) and u == 0:
                return PREP + NA + TURN, (PREP + NA + TURN) % BANKS
            return u * BODY + (FIRST - BODY), FIRST % BANKS

        def first_set_until(t):
            return sum(1 for x in CARRY if x < t) * NA // len(CARRY)

        def columns_of(qb, half):
            return min(CH, (qb + 1) * P - half * CH)

        def units(engine, setup, body):
            setup()
            body(0, 0, False, True)
            body(1, 1, True, True)
            with engine.Fori(1, UNITS // 2 - 1) as m:
                body(m * 2, 0, True, True)
                body(m * 2 + 1, 1, True, True)
            body(UNITS - 2, 0, True, True)
            body(UNITS - 1, 1, True, False)

        def sequence_and_quad(u):
            return u // QUADS, u % QUADS

        with nc.Block() as block:
            @block.gpsimd
            def _(pool):
                nc.gpsimd.memset(mst[:], 0.0).then_inc(zeroed, 1)
                nc.gpsimd.memset(halfmax[:], -3.0e38).then_inc(zeroed, 1)

            @block.tensor
            def _(pe):
                def job(base, bank0, k, products):
                    pe.wait_ge(ab_done, base + k + 1)
                    for i, (at, n, lhsT, rhs) in enumerate(products):
                        last = nc.tensor.matmul(ab[:, (bank0 + k) % BANKS, at:at + n], lhsT, rhs, start=i == 0,
                                                stop=i == len(products) - 1, skip_group_check=True)
                    last.then_inc(ab_full, 1)

                def stack(base, bank0, k, u, i, more=None):
                    b, q = sequence_and_quad(u)
                    sel = selk if i else selq
                    for g in range(2):
                        for ch in range(2):
                            job(base, bank0, k, [(0, CH, sel[:, ds(q * 6 * P + (g * 3 + l) * P, P)],
                                                part[:, i, l, ds(b * SEQ + ch * CH, CH)]) for l in range(3)]
                                + ([(j * P, P, mst[:, ch * 4 + j, g], identb[:]) for j in range(4)] if more else []))
                            k += 1

                def prepare(base, bank0, k, u):
                    stack(base, bank0, k, u, 1)
                    stack(base, bank0, k + 4, u, 0)
                    b, q = sequence_and_quad(u)
                    pe.wait_ge(xb_ready, u // 2 + 1)
                    for half in range(2):
                        pe.wait_ge(ab_done, base + k + 8 + half + 1)
                        for j in range(4):
                            kb = half * 4 + j
                            out = ab[:, (bank0 + k + 8 + half) % BANKS, j * P:j * P + P]
                            nc.tensor.matmul(out, xb[:, kb * P:kb * P + P], wv[:, ds(q * P, P)], start=True, stop=False,
                                             skip_group_check=True)
                            last = nc.tensor.matmul(out, ones1[:], bv[:, ds(q * P, P)], start=False, stop=True,
                                                    skip_group_check=True)
                        last.then_inc(ab_full, 1)

                def first_set(base, bank0, k, usl, lo, hi):
                    for n in range(lo, hi):
                        qb, half, h = halves[n]
                        g, r, cols = h // 2, 64 * (h % 2), columns_of(qb, half)
                        diag = qb // 4 == half
                        bank = (bank0 + k + n) % BANKS
                        pe.wait_ge(ab_done, base + k + n + 1)
                        last = nc.tensor.matmul(ab[:, bank, 0:cols], qx[r:r + 64, g, qb * P:qb * P + P],
                                                kx[r:r + 64, usl, g, half * CH:half * CH + cols],
                                                start=True, stop=not diag, skip_group_check=True)
                        if diag:
                            last = nc.tensor.matmul(ab[:, bank, cols - P:cols], identb[:], mask_qk[:],
                                                    start=False, stop=True, skip_group_check=True)
                        last.then_inc(ab_full, 1)

                def turn(base, bank0, k, u):
                    pe.wait_ge(max_ready, u + 1)
                    stack(base, bank0, k, u, 0, more=True)

                def weigh(u, sl, t):
                    ch, kb, g = steps[t]
                    at = max(0, kb - 4 * ch) * P
                    pe.wait_ge(exp_done, u * NST + t + 3)
                    if kb == 0 and g == 0:
                        pe.wait_ge(o_copied, u * 2 + ch + 1)
                    for jj in range(2):
                        h = 2 * g + jj
                        mm = nc.tensor.matmul(ob[32 * h:32 * h + 32, at:CH], vq[:, sl, kb, 32 * h:32 * h + 32],
                                              pr[:, t % RING, jj, at:CH], start=kb == 0, stop=kb == 4 * ch + 3,
                                              skip_group_check=True)
                    mm.then_inc(pv_done, 1)

                def step(u, sl, t):
                    ch, kb, g = steps[t]
                    at = max(0, kb - 4 * ch) * P
                    diag = kb >= 4 * ch
                    pe.wait_ge(exp_done, u * NST + t + 1)
                    for jj in range(2):
                        r = 64 * jj
                        mm = nc.tensor.matmul(st[:, g, jj, at:CH], kx[r:r + 64, sl, g, kb * P:kb * P + P],
                                              qxm[r:r + 64, g, ch * CH + at:ch * CH + CH],
                                              start=True, stop=not diag, skip_group_check=True)
                        if diag:
                            mm = nc.tensor.matmul(st[:, g, jj, at:at + P], identb[:], mask_kq[:],
                                                  start=False, stop=True, skip_group_check=True)
                    mm.then_inc(st_full, 1)
                    if t >= 2:
                        weigh(u, sl, t - 2)

                def sums(base, bank0, k, u, ch):
                    pe.wait_ge(o_copied, u * 2 + ch + 2)
                    job(base, bank0, k, [(0, CH, sumbc[:], osum[:])])

                def output(base, bank0, k, u):
                    pe.wait_ge(wo_ready, u + 1)
                    pe.wait_ge(ctx_ready, u * 2 + 3)
                    for ch in range(2):
                        job(base, bank0, k + ch, [(0, CH, wo_u[:], ctxt[:, ch])])

                def setup():
                    pe.wait_ge(zeroed, 2)
                    prepare(0, 0, 0, 0)
                    pe.wait_ge(ab_done, PREP + BANKS)
                    first_set(0, 0, PREP, 0, 0, NA)
                    turn(0, 0, PREP + NA, 0)

                def body(u, sl, after, before):
                    base, bank0 = jobs_before(u)
                    k = 0
                    pe.wait_ge(ab_done, base + BANKS)
                    if after:
                        sums(base, bank0, k, u - 1, 1)
                        k += 1
                    for t in range(LEAD):
                        step(u, sl, t)
                    if before:
                        prepare(base, bank0, k, u + 1)
                        k += PREP
                    if after:
                        output(base, bank0, k, u - 1)
                        k += OUT - 1
                    if before:
                        pe.wait_ge(ab_done, base + k + BANKS)
                    for t in range(LEAD, NST):
                        step(u, sl, t)
                        if before:
                            first_set(base, bank0, k + (t >= AT_SUMS), 1 - sl, first_set_until(t), first_set_until(t + 1))
                        if t == AT_SUMS - 1:
                            sums(base, bank0, k + (first_set_until(t + 1) if before else 0), u, 0)
                    weigh(u, sl, NST - 2)
                    weigh(u, sl, NST - 1)
                    k += 1
                    if before:
                        turn(base, bank0, k + NA, u + 1)
                    else:
                        sums(base, bank0, k, u, 1)
                        output(base, bank0, k + 1, u)

                units(nc.tensor, setup, body)

            @block.scalar
            def _(act):
                act.sem_inc(exp_done, 2)
                act.sem_inc(o_copied, 1)

                def copy_context(u, ch):
                    act.wait_ge(pv_done, u * NST + (NST if ch else NST0) + RING)
                    act.wait_ge(ctx_ready, u * 2 + ch + 1)
                    nc.scalar.activation(osum[:], ob[:], ACT.Copy).then_inc(o_copied, 1)

                with nc.scalar.Fori(0, UNITS) as u:
                    for t, (ch, kb, g) in enumerate(steps):
                        at = max(0, kb - 4 * ch) * P
                        act.wait_ge(st_full, u * NST + t + 1)
                        act.wait_ge(pv_done, u * NST + t + 1)
                        nc.scalar.activation(pr[:, t % RING, :, at:CH], st[:, g, :, at:CH], ACT.Exp,
                                             scale=SCALE8).then_inc(exp_done, 1)
                        if t == NST0 + 1:
                            copy_context(u, 0)
                    copy_context(u, 1)

            @block.vector
            def _(dve):
                dve.sem_inc(ab_done, BANKS)
                dve.sem_inc(pv_done, RING)
                dve.sem_inc(ctx_ready, 1)

                def empty(base, bank0, k, dst, add=None):
                    dve.wait_ge(ab_full, base + k + 1)
                    if add is None:
                        nc.vector.tensor_copy(dst, ab[:, (bank0 + k) % BANKS]).then_inc(ab_done, 1)
                    else:
                        nc.vector.tensor_scalar(dst, ab[:, (bank0 + k) % BANKS], add, None, ALU.add).then_inc(ab_done, 1)

                def empty_stack(base, bank0, k, dst, add=None):
                    for g in range(2):
                        for ch in range(2):
                            empty(base, bank0, k, dst[:, g, ch * CH:ch * CH + CH], add)
                            k += 1

                def prepare(base, bank0, k, u, usl):
                    if usl == 0:
                        b, q = sequence_and_quad(u)
                        nc.vector.tensor_scalar(xb[:], xn[:, ds(b * SEQ, SEQ)], 1.0, None, ALU.mult).then_inc(xb_ready, 1)
                    empty_stack(base, bank0, k, kx[:, usl], kone[:])
                    empty_stack(base, bank0, k + 4, qx[:])
                    for half in range(2):
                        empty(base, bank0, k + 8 + half,
                              vq[:, usl, half * 4:half * 4 + 4].rearrange("p a b -> p (a b)"))

                def maxima(base, bank0, k, lo, hi):
                    for n in range(lo, hi):
                        qb, half, h = halves[n]
                        dve.wait_ge(ab_full, base + k + n + 1)
                        nc.vector.tensor_reduce(halfmax[:, qb, h, half:half + 1],
                                                ab[:, (bank0 + k + n) % BANKS, 0:columns_of(qb, half)], AX.X,
                                                ALU.max).then_inc(ab_done, 1)

                def split_maxima(base, k, u):
                    dve.wait_ge(ab_done, base + k + BANKS)
                    nc.vector.tensor_reduce(negmax[:], halfmax[:], AX.X, ALU.max, negate=True).then_inc(max_step, 1)
                    cols = [mst[:].rearrange("p t g (j r) -> p t (g j) r", j=2)[:, :, :, M_ROW + l] for l in range(3)]
                    dve.wait_ge(max_step, u * MSTEPS + 1)
                    nc.vector.tensor_copy(cols[0], negmax[:]).then_inc(max_step, 1)
                    dve.wait_ge(max_step, u * MSTEPS + 2)
                    nc.vector.tensor_tensor(negrest[:], negmax[:], cols[0], ALU.subtract).then_inc(max_step, 1)
                    dve.wait_ge(max_step, u * MSTEPS + 3)
                    nc.vector.tensor_copy(cols[1], negrest[:]).then_inc(max_step, 1)
                    dve.wait_ge(max_step, u * MSTEPS + 4)
                    nc.vector.tensor_tensor(cols[2], negrest[:], cols[1], ALU.subtract).then_inc(max_step, 1)
                    dve.wait_ge(max_step, u * MSTEPS + 5)
                    dve.sem_inc(max_ready, 1)

                def normalise(base, bank0, k, u, ch):
                    dve.wait_ge(ab_full, base + k + 1)
                    nc.vector.reciprocal(rsum[:], ab[:, (bank0 + k) % BANKS]).then_inc(ab_done, 1)
                    dve.wait_ge(ab_done, base + k + 1 + BANKS)
                    nc.vector.tensor_tensor(ctxt[:, ch], osum[:], rsum[:], ALU.mult).then_inc(ctx_ready, 1)
                    dve.wait_ge(ctx_ready, u * 2 + ch + 2)

                def bring_wo(u):
                    b, q = sequence_and_quad(u)
                    nc.vector.tensor_scalar(wo_u[:], wo[:, ds(q, 1)].rearrange("p a n -> p (a n)"), 1.0, None,
                                            ALU.mult).then_inc(wo_ready, 1)

                def store(base, bank0, k, u):
                    b, q = sequence_and_quad(u)
                    for ch in range(2):
                        dve.wait_ge(ab_full, base + k + ch + 1)
                        cols = ds(b * SEQ + ch * CH, CH)
                        nc.vector.tensor_tensor(res[:, cols], res[:, cols], ab[:, (bank0 + k + ch) % BANKS],
                                                ALU.add).then_inc(ab_done, 1)

                def setup():
                    dve.wait_ge(zeroed, 2)
                    prepare(0, 0, 0, 0, 0)
                    maxima(0, 0, PREP, 0, NA)
                    split_maxima(0, PREP + NA, 0)
                    empty_stack(0, 0, PREP + NA, qxm[:])

                def body(u, sl, after, before):
                    base, bank0 = jobs_before(u)
                    k = 0
                    if after:
                        bring_wo(u - 1)
                        normalise(base, bank0, k, u - 1, 1)
                        k += 1
                    if before:
                        prepare(base, bank0, k, u + 1, 1 - sl)
                        k += PREP
                    if after:
                        store(base, bank0, k, u - 1)
                        k += OUT - 1
                    at_sums = first_set_until(AT_SUMS) if before else 0
                    maxima(base, bank0, k, 0, at_sums)
                    normalise(base, bank0, k + at_sums, u, 0)
                    k += 1
                    if before:
                        maxima(base, bank0, k, at_sums, NA)
                        split_maxima(base, k + NA, u + 1)
                        empty_stack(base, bank0, k + NA, qxm[:])
                    else:
                        bring_wo(u)
                        normalise(base, bank0, k, u, 1)
                        store(base, bank0, k + 1, u)

                units(nc.vector, setup, body)


def headwise_attention(nc, name, w, c, xn, res, norm, latent=False):
    NB = TOK // P
    with ExitStack() as ctx:
        s = Scope(nc, ctx, name)
        wqkv = s.sb("wqkv", [P, D if latent else 3 * D])
        bqkv = s.sb("bqkv", [P, 3 * D])
        wo, bo = s.sb("wo", [P, D]), s.sb("bo", [P, 1])
        ident = s.sb("ident", [P, P])
        loads = [(wqkv[:], w["wqkv"]), (bqkv[:], w["bqkv"].broadcast_to([P, 3 * D])), (wo[:], w["wo"]),
                 (bo[:], w["bo"]), (ident[:], c["ident"])]
        if latent:
            RANK = w["wdown"].shape[1]
            wdown, bdown, wup = s.sb("wdown", [P, RANK]), s.sb("bdown", [RANK, 1]), s.sb("wup", [RANK, 2 * D])
            cos, sin = s.sb("cos", [P, TPB, HD]), s.sb("sin", [P, TPB, HD])
            loads += [(wdown[:], w["wdown"]), (bdown[:], w["bdown"]), (wup[:], w["wup"]),
                      (cos[:], c["cos8"]), (sin[:], c["sin8"])]
            latb = s.sb("latb", [RANK, 2, P])
            cosqk, sinqk = s.sb("cosqk", [P, 2, 2 * D]), s.sb("sinqk", [P, 2, 2 * D])
            roped = s.sb("roped", [P, 2, 2 * D])
            lat_ps = s.ps("lat_ps", [RANK, 2, CH])
        load_phase(s, loads, norm)

        xblk = s.sb("xblk", [P, 2, P])
        qkv = s.sb("qkv", [P, 2, 3 * D])
        prod = s.sb("prod", [P, 2, HEADS, HEADS, HD])
        score = s.sb("score", [P, 2, HEADS, HEADS])
        top = s.sb("top", [P, 2, HEADS])
        less = s.sb("less", [P, 2, HEADS, HEADS])
        ex = s.sb("ex", [P, 2, HEADS, HEADS])
        total = s.sb("total", [P, 2, HEADS])
        inv = s.sb("inv", [P, 2, HEADS])
        prob = s.sb("prob", [P, 2, HEADS, HEADS])
        pv = s.sb("pv", [P, 2, HEADS, HEADS, HD])
        ct = s.sb("ct", [P, 2, P])
        qkv_ps = s.ps("qkv_ps", [P, 2, CH])
        ct_ps = s.ps("ct_ps", [P, CH])
        out_ps = s.ps("out_ps", [P, CH])

        x_copied, qkv_full, qkv_read = s.sem("x_copied"), s.sem("qkv_full"), s.sem("qkv_read")
        prod_ready, scored, topped = s.sem("prod_ready"), s.sem("scored"), s.sem("topped")
        less_ready, ex_ready, summed, inverted = (s.sem("less_ready"), s.sem("ex_ready"), s.sem("summed"),
                                                  s.sem("inverted"))
        prob_ready, pv_ready = s.sem("prob_ready"), s.sem("pv_ready")
        ct_full, ct_copied, out_full, out_added = (s.sem("ct_full"), s.sem("ct_copied"), s.sem("out_full"),
                                                   s.sem("out_added"))
        if latent:
            lat_full, lat_ready, rope_part, rope_done = (s.sem("lat_full"), s.sem("lat_ready"),
                                                         s.sem("rope_part"), s.sem("rope_done"))

        def q_of(i):
            return roped[:, i % 2, 0:D] if latent else qkv[:, i % 2, 0:D]

        def k_of(i):
            return roped[:, i % 2, D:2 * D] if latent else qkv[:, i % 2, D:2 * D]

        def blocks(engine, body):
            body(0, 0, 2)
            body(1, 1, 2)
            with engine.Fori(1, (NB - 2) // 2) as n:
                body(n * 2, 0, 2)
                body(n * 2 + 1, 1, 2)
            body(NB - 2, 0, 1)
            body(NB - 1, 1, 0)

        with nc.Block() as block:
            @block.tensor
            def _(pe):
                def project(i, sl):
                    pe.wait_ge(x_copied, i + 1)
                    pe.wait_ge(qkv_read, i + 1)
                    if latent:
                        nc.tensor.matmul(lat_ps[:, sl, 0:P], wdown[:], xblk[:, sl], start=True,
                                         stop=True).then_inc(lat_full, 1)
                    mm = nc.tensor.matmul(qkv_ps[:, sl, 0:wqkv.shape[1]], xblk[:, sl], wqkv[:], start=True,
                                          stop=True)
                    if not latent:
                        mm.then_inc(qkv_full, 1)

                def project_up(i, sl):
                    if latent:
                        pe.wait_ge(lat_ready, i + 1)
                        nc.tensor.matmul(qkv_ps[:, sl, D:3 * D], latb[:, sl], wup[:], start=True,
                                         stop=True).then_inc(qkv_full, 1)

                def output(i, sl):
                    pe.wait_ge(ct_copied, i + 2)
                    pe.wait_ge(out_added, i + 1)
                    nc.tensor.matmul(out_ps[:, 0:P], wo[:], ct[:, sl], start=True, stop=True).then_inc(out_full, 1)

                for i in range(2):
                    project(i, i)
                    project_up(i, i)

                def body(i, sl, left):
                    if left == 2:
                        project(i + 2, sl)
                        project_up(i + 2, sl)
                    if not (isinstance(i, int) and i == 0):
                        output(i - 1, 1 - sl)
                    pe.wait_ge(pv_ready, i + 1)
                    pe.wait_ge(ct_copied, i + 1)
                    for g in range(HEADS):
                        mm = nc.tensor.matmul(ct_ps[:, 0:P], pv[:, sl, g].rearrange("p h d -> p (h d)"), ident[:],
                                              start=g == 0, stop=g == HEADS - 1)
                    mm.then_inc(ct_full, 1)

                blocks(nc.tensor, body)
                output(NB - 1, 1)

            @block.scalar
            def _(act):
                act.sem_inc(ct_copied, 1)

                def latent_copy(i, sl):
                    if latent:
                        act.wait_ge(lat_full, i + 1)
                        nc.scalar.activation(latb[:, sl], lat_ps[:, sl, 0:P], ACT.Identity,
                                             bias=bdown[:]).then_inc(lat_ready, 1)

                for i in range(2):
                    latent_copy(i, i)

                def copy_context(i, sl):
                    act.wait_ge(ct_full, i + 1)
                    nc.scalar.activation(ct[:, sl], ct_ps[:, 0:P], ACT.Copy).then_inc(ct_copied, 1)

                def body(i, sl, left):
                    if left == 2:
                        latent_copy(i + 2, sl)
                    act.wait_ge(less_ready, i + 1)
                    nc.scalar.activation(ex[:, sl], less[:, sl], ACT.Exp, scale=SCALE8).then_inc(ex_ready, 1)
                    if not (isinstance(i, int) and i == 0):
                        copy_context(i - 1, 1 - sl)

                blocks(nc.scalar, body)
                copy_context(NB - 1, 1)

            @block.gpsimd
            def _(pool):
                def products(i, sl):
                    pool.wait_ge(qkv_read, i + 3)
                    if latent:
                        v4 = qkv[:, sl, 0:2 * D].rearrange("p (n a b) -> p n a b", a=2, b=HD // 2)
                        s4 = sinqk[:, sl].rearrange("p (n a b) -> p n a b", a=2, b=HD // 2)
                        n_heads = 2 * HEADS
                        half = HD // 2
                        pool.wait_ge(scored, i + 1)
                        tab = lambda t, lo, hi: (t[:, ds(i % TPB, 1) if not isinstance(i, int)
                                                   else slice(i % TPB, i % TPB + 1), lo:hi]
                                                 .broadcast_to([P, n_heads, hi - lo]))
                        nc.gpsimd.tensor_tensor(cosqk[:, sl].rearrange("p (n b) -> p n b", b=HD),
                                                qkv[:, sl, 0:2 * D].rearrange("p (n b) -> p n b", b=HD),
                                                tab(cos, 0, HD), ALU.mult).then_inc(rope_part, 1)
                        nc.gpsimd.tensor_tensor(s4[:, :, 0], v4[:, :, 1], tab(sin, 0, half),
                                                ALU.mult).then_inc(rope_part, 1)
                        nc.gpsimd.tensor_tensor(s4[:, :, 1], v4[:, :, 0], tab(sin, half, HD),
                                                ALU.mult).then_inc(rope_part, 1)
                        pool.wait_ge(rope_part, i * 3 + 3)
                        nc.gpsimd.tensor_tensor(roped[:, sl], cosqk[:, sl], sinqk[:, sl],
                                                ALU.add).then_inc(rope_done, 1)
                        pool.wait_ge(rope_done, i + 1)
                    q3 = q_of(sl).rearrange("p (h a d) -> p h a d", a=1, d=HD).broadcast_to([P, HEADS, HEADS, HD])
                    k3 = k_of(sl).rearrange("p (a g d) -> p a g d", a=1, d=HD).broadcast_to([P, HEADS, HEADS, HD])
                    nc.gpsimd.tensor_tensor(prod[:, sl], q3, k3, ALU.mult).then_inc(prod_ready, 1)

                products(0, 0)

                def body(i, sl, left):
                    if left:
                        products(i + 1, 1 - sl)

                blocks(nc.gpsimd, body)

            @block.vector
            def _(dve):
                dve.sem_inc(qkv_read, 2)
                dve.sem_inc(scored, 2)
                dve.sem_inc(out_added, 1)

                def bring(i, sl):
                    nc.vector.tensor_scalar(xblk[:, sl], xn[:, ds(i * P, P)], 1.0, None,
                                            ALU.mult).then_inc(x_copied, 1)

                def evacuate(i, sl):
                    dve.wait_ge(qkv_full, i + 1)
                    nc.vector.tensor_tensor(qkv[:, sl], qkv_ps[:, sl, 0:3 * D], bqkv[:], ALU.add).then_inc(qkv_read, 1)

                def store(i):
                    dve.wait_ge(out_full, i + 1)
                    cols = ds(i * P, P)
                    nc.vector.scalar_tensor_tensor(out=res[:, cols], in0=out_ps[:, 0:P], scalar=bo[:],
                                                   in1=res[:, cols], op0=ALU.add, op1=ALU.add).then_inc(out_added, 1)

                bring(0, 0)
                bring(1, 1)
                evacuate(0, 0)

                def body(i, sl, left):
                    if left:
                        if not (isinstance(i, int) and i == 0):
                            dve.wait_ge(pv_ready, i)
                        evacuate(i + 1, 1 - sl)
                    if left == 2:
                        bring(i + 2, sl)
                    dve.wait_ge(prod_ready, i + 1)
                    nc.vector.tensor_reduce(score[:, sl], prod[:, sl], AX.X, ALU.add).then_inc(scored, 1)
                    dve.wait_ge(scored, i + 3)
                    nc.vector.tensor_reduce(top[:, sl], score[:, sl], AX.X, ALU.max).then_inc(topped, 1)
                    dve.wait_ge(topped, i + 1)
                    nc.vector.tensor_tensor(less[:, sl], score[:, sl],
                                            top[:, sl].rearrange("p (h a) -> p h a", a=1)
                                            .broadcast_to([P, HEADS, HEADS]), ALU.subtract).then_inc(less_ready, 1)
                    dve.wait_ge(ex_ready, i + 1)
                    nc.vector.tensor_reduce(total[:, sl], ex[:, sl], AX.X, ALU.add).then_inc(summed, 1)
                    dve.wait_ge(summed, i + 1)
                    nc.vector.reciprocal(inv[:, sl], total[:, sl]).then_inc(inverted, 1)
                    dve.wait_ge(inverted, i + 1)
                    nc.vector.tensor_tensor(prob[:, sl], ex[:, sl],
                                            inv[:, sl].rearrange("p (h a) -> p h a", a=1)
                                            .broadcast_to([P, HEADS, HEADS]), ALU.mult).then_inc(prob_ready, 1)
                    dve.wait_ge(prob_ready, i + 1)
                    pgh = (prob[:, sl].rearrange("p h (g a) -> p g h a", a=1)
                           .broadcast_to([P, HEADS, HEADS, HD]))
                    vgd = (qkv[:, sl, 2 * D:3 * D].rearrange("p (g a d) -> p g a d", a=1, d=HD)
                           .broadcast_to([P, HEADS, HEADS, HD]))
                    nc.vector.tensor_tensor(pv[:, sl], pgh, vgd, ALU.mult).then_inc(pv_ready, 1)
                    if not (isinstance(i, int) and i == 0):
                        store(i - 1)

                blocks(nc.vector, body)
                store(NB - 1)


EXPERTS, HID = 8, 256
NBLK = TOK // P


def route(nc, name, gate, tables, xn, kind, rows, rows_f=None):
    CAP = TOK // EXPERTS
    wide = 1 if kind == "switch" else EXPERTS
    with ExitStack() as ctx:
        s = Scope(nc, ctx, name)
        rev, identb, tri, onesb = tables

        def field(n, dt=F32):
            return s.sb(n, [P, NBLK, EXPERTS], dt)

        prob, less, a, b2, hot1, hot2 = (field("prob"), field("less"), field("a"), field("b2"), field("hot1"),
                                         field("hot2"))
        hotb = field("hotb", BF16)
        top, inv = s.sb("top", [P, NBLK]), s.sb("inv", [P, NBLK])
        wt = s.sb("wt", [P, NBLK, wide])
        rest = s.sb("rest", [P, NBLK, wide])
        parts = s.sb("parts", [P, NBLK, 3, wide], BF16)
        logit_ps = s.ps("logit_ps", [P, NBLK, EXPERTS])
        count_ps = s.ps("count_ps", [P, NBLK, EXPERTS])
        row_ps = s.ps("row_ps", [3 * wide, 2, CH])
        logits, less_ready, exped, step = s.sem("logits"), s.sem("less_ready"), s.sem("exped"), s.sem("step")
        hot_ready, counted, parted = s.sem("hot_ready"), s.sem("counted"), s.sem("parted")
        row_full, row_copied = s.sem("row_full"), s.sem("row_copied")
        rev_b = rev[:].broadcast_to([P, NBLK, EXPERTS])

        def over(t):
            return t[:].rearrange("p (n a) -> p n a", a=1).broadcast_to([P, NBLK, EXPERTS])

        with nc.Block() as block:
            @block.tensor
            def _(pe):
                for i in range(NBLK):
                    mm = nc.tensor.matmul(logit_ps[:, i], xn[:, i * P:i * P + P], gate, start=True, stop=True)
                mm.then_inc(logits, 1)
                if kind == "switch":
                    pe.wait_ge(hot_ready, 1)
                    nc.tensor.matmul(count_ps[:].rearrange("p n e -> p (n e)"), tri[:],
                                     hotb[:].rearrange("p n e -> p (n e)"), start=True, stop=False,
                                     skip_group_check=True)
                    for i in range(NBLK - 1):
                        mm = nc.tensor.matmul(count_ps[:, i + 1:], onesb[:],
                                              hotb[:, i:i + 1].broadcast_to([P, NBLK - 1 - i, EXPERTS]),
                                              start=False, stop=i == NBLK - 2, skip_group_check=True)
                    mm.then_inc(counted, 1)
                pe.wait_ge(parted, 1)
                for n in range(NCH):
                    if n >= 2:
                        pe.wait_ge(row_copied, n - 1)
                    for j in range(4):
                        mm = nc.tensor.matmul(row_ps[:, n % 2, j * P:j * P + P],
                                              parts[:, n * 4 + j].rearrange("p l e -> p (l e)"), identb[:],
                                              start=True, stop=True)
                    mm.then_inc(row_full, 1)

            @block.scalar
            def _(act):
                act.wait_ge(less_ready, 1)
                nc.scalar.activation(a[:], less[:], ACT.Exp).then_inc(exped, 1)
                for n in range(NCH):
                    act.wait_ge(row_full, n + 1)
                    if rows_f is not None:
                        nc.scalar.activation(rows_f[:, n * CH:n * CH + CH], row_ps[:, n % 2], ACT.Copy)
                    nc.scalar.activation(rows[:, n * CH:n * CH + CH], row_ps[:, n % 2],
                                         ACT.Copy).then_inc(row_copied, 1)

            @block.vector
            def _(dve):
                k = 0

                def chained(instruction):
                    nonlocal k
                    k += 1
                    instruction.then_inc(step, 1)
                    dve.wait_ge(step, k)

                dve.wait_ge(logits, 1)
                chained(nc.vector.tensor_reduce(top[:], logit_ps[:], AX.X, ALU.max))
                nc.vector.tensor_tensor(less[:], logit_ps[:], over(top), ALU.subtract).then_inc(less_ready, 1)
                dve.wait_ge(exped, 1)
                chained(nc.vector.tensor_reduce(top[:], a[:], AX.X, ALU.add))
                chained(nc.vector.reciprocal(inv[:], top[:]))
                chained(nc.vector.tensor_tensor(prob[:], a[:], over(inv), ALU.mult))

                def first_max(src, hot):
                    chained(nc.vector.tensor_reduce(top[:], src[:], AX.X, ALU.max))
                    chained(nc.vector.tensor_tensor(b2[:], src[:], over(top), ALU.is_equal))
                    chained(nc.vector.tensor_tensor(b2[:], b2[:], rev_b, ALU.mult))
                    chained(nc.vector.tensor_reduce(top[:], b2[:], AX.X, ALU.max))
                    chained(nc.vector.tensor_tensor(hot[:], b2[:], over(top), ALU.is_equal))

                first_max(prob, hot1)
                if kind == "switch":
                    nc.vector.tensor_copy(hotb[:], hot1[:]).then_inc(hot_ready, 1)
                    dve.wait_ge(counted, 1)
                    chained(nc.vector.scalar_tensor_tensor(out=hot2[:], in0=count_ps[:], scalar=float(CAP),
                                                           in1=hot1[:], op0=ALU.is_le, op1=ALU.mult))
                    chained(nc.vector.tensor_tensor(less[:], prob[:], hot2[:], ALU.mult))
                    chained(nc.vector.tensor_reduce(wt[:].rearrange("p n e -> p (n e)"), less[:], AX.X, ALU.add))
                else:
                    chained(nc.vector.scalar_tensor_tensor(out=less[:], in0=hot1[:], scalar=-2.0, in1=prob[:],
                                                           op0=ALU.mult, op1=ALU.add))
                    first_max(less, hot2)
                    chained(nc.vector.tensor_tensor(hot1[:], hot1[:], hot2[:], ALU.add))
                    chained(nc.vector.tensor_tensor(wt[:], prob[:], hot1[:], ALU.mult))
                    if kind == "two_normed":
                        chained(nc.vector.tensor_reduce(top[:], wt[:], AX.X, ALU.add))
                        chained(nc.vector.tensor_scalar(top[:], top[:], 1e-9, None, ALU.add))
                        chained(nc.vector.reciprocal(inv[:], top[:]))
                        chained(nc.vector.tensor_tensor(wt[:], wt[:], over(inv), ALU.mult))
                chained(nc.vector.tensor_copy(parts[:, :, 0], wt[:]))
                chained(nc.vector.tensor_tensor(rest[:], wt[:], parts[:, :, 0], ALU.subtract))
                chained(nc.vector.tensor_copy(parts[:, :, 1], rest[:]))
                nc.vector.tensor_tensor(parts[:, :, 2], rest[:], parts[:, :, 1], ALU.subtract).then_inc(parted, 1)


def experts(nc, name, w, c, xn, res, gate, tables, biased):
    KR = 3 * EXPERTS
    with ExitStack() as ctx:
        s = Scope(nc, ctx, name)
        rows = s.sb("rows", [KR, TOK], BF16)
        rows_f = s.sb("rows_f", [KR, TOK]) if biased else None
        w1, w3 = s.sb("w1", [P, EXPERTS, HID]), s.sb("w3", [P, EXPERTS, HID])
        w2 = s.sb("w2", [P, EXPERTS, 2, D])
        spread = s.sb("spread", [KR, EXPERTS, P], BF16)
        loads = [(w1[:], w["w1"].rearrange("e d h -> d e h")), (w3[:], w["w3"].rearrange("e d h -> d e h")),
                 (w2[:], w["w2"].rearrange("e (f p) d -> p e f d", p=P)), (spread[:], c["spread"])]
        if biased:
            b13, b2 = s.sb("b13", [P, 2, EXPERTS, 2]), s.sb("b2", [KR, D])
            loads += [(b13[:], w["b13"]), (b2[:], w["b2"])]
        load_phase(s, loads, lambda: route(nc, name + "r", gate, tables, xn, "two_normed" if biased else "two", rows,
                                           rows_f))

        act1 = s.sb("act1", [P, 2, CH])
        mixed = s.sb("mixed", [P, 2, CH])
        weighed = s.sb("weighed", [P, 2, CH])
        wb = s.sb("wb", [P, 2, CH])
        h1, h3 = s.ps("h1", [P, 2, CH]), s.ps("h3", [P, 2, CH])
        wb_ps, y_ps = s.ps("wb_ps", [P, 2, CH]), s.ps("y_ps", [P, CH])
        h_full, act_done, mixed_done, weighed_done = (s.sem("h_full"), s.sem("act_done"), s.sem("mixed_done"),
                                                      s.sem("weighed_done"))
        wb_full, wb_copied, used, y_full, y_added = (s.sem("wb_full"), s.sem("wb_copied"), s.sem("used"),
                                                     s.sem("y_full"), s.sem("y_added"))
        J = 2 * EXPERTS

        with nc.Block() as block:
            @block.tensor
            def _(pe):
                with nc.tensor.Fori(0, NCH) as n:
                    cols = ds(n * CH, CH)

                    def down(j):
                        e, f = j // 2, j % 2
                        pe.wait_ge(weighed_done, n * J + j + 3)
                        if j == 0:
                            pe.wait_ge(y_added, n + 1)
                        nc.tensor.matmul(y_ps[:], w2[:, e, f], weighed[:, f], start=j == 0,
                                         stop=j == J - 1).then_inc(used, 1)
                        if j == 0 and biased:
                            nc.tensor.matmul(y_ps[:], b2[:], rows_f[:, cols], start=False, stop=False)

                    for j in range(J):
                        e, f = j // 2, j % 2
                        if f == 0:
                            pe.wait_ge(wb_copied, n * EXPERTS + e + 1)
                        pe.wait_ge(mixed_done, n * J + j + 1)
                        nc.tensor.matmul(h1[:, f], w1[:, e, f * P:f * P + P], xn[:, cols], start=True, stop=True)
                        nc.tensor.matmul(h3[:, f], w3[:, e, f * P:f * P + P], xn[:, cols], start=True,
                                         stop=True).then_inc(h_full, 1)
                        if f == 0:
                            nc.tensor.matmul(wb_ps[:, e % 2], spread[:, e], rows[:, cols], start=True,
                                             stop=True).then_inc(wb_full, 1)
                        if j >= 2:
                            down(j - 2)
                    down(J - 2)
                    down(J - 1)
                    pe.wait_ge(used, n * J + J + 2)
                    pe.sem_inc(y_full, 1)

            @block.scalar
            def _(act):
                act.sem_inc(wb_copied, 2)
                with nc.scalar.Fori(0, NCH) as n:
                    for j in range(J):
                        e, f = j // 2, j % 2
                        act.wait_ge(h_full, n * J + j + 1)
                        act.wait_ge(mixed_done, n * J + j + 1)
                        bias = dict(bias=b13[:, 0, e, f:f + 1]) if biased else {}
                        nc.scalar.activation(act1[:, f], h1[:, f], ACT.Silu, **bias).then_inc(act_done, 1)
                        if f == 0:
                            act.wait_ge(wb_full, n * EXPERTS + e + 1)
                            act.wait_ge(weighed_done, n * J + j + 1)
                            nc.scalar.activation(wb[:, e % 2], wb_ps[:, e % 2], ACT.Copy).then_inc(wb_copied, 1)

            @block.vector
            def _(dve):
                dve.sem_inc(mixed_done, 2)
                dve.sem_inc(y_added, 1)
                dve.sem_inc(used, 2)
                with nc.vector.Fori(0, NCH) as n:
                    for j in range(J):
                        e, f = j // 2, j % 2
                        dve.wait_ge(act_done, n * J + j + 1)
                        dve.wait_ge(weighed_done, n * J + j + 1)
                        if biased:
                            nc.vector.scalar_tensor_tensor(out=mixed[:, f], in0=h3[:, f],
                                                           scalar=b13[:, 1, e, f:f + 1], in1=act1[:, f],
                                                           op0=ALU.add, op1=ALU.mult).then_inc(mixed_done, 1)
                        else:
                            nc.vector.tensor_tensor(mixed[:, f], h3[:, f], act1[:, f],
                                                    ALU.mult).then_inc(mixed_done, 1)
                    dve.wait_ge(y_full, n + 1)
                    cols = ds(n * CH, CH)
                    nc.vector.tensor_tensor(res[:, cols], res[:, cols], y_ps[:], ALU.add).then_inc(y_added, 1)

            @block.gpsimd
            def _(pool):
                pool.sem_inc(weighed_done, 2)
                with nc.gpsimd.Fori(0, NCH) as n:
                    for j in range(J):
                        e, f = j // 2, j % 2
                        pool.wait_ge(wb_copied, n * EXPERTS + e + 3)
                        pool.wait_ge(mixed_done, n * J + j + 3)
                        pool.wait_ge(used, n * J + j + 1)
                        nc.gpsimd.tensor_tensor(weighed[:, f], mixed[:, f], wb[:, e % 2],
                                                ALU.mult).then_inc(weighed_done, 1)


def switch_ffn(nc, name, w, c, xn, res, gate, tables):
    with ExitStack() as ctx:
        s = Scope(nc, ctx, name)
        rows = s.sb("rows", [3, TOK], BF16)
        we, be, ones3 = s.sb("we", [P, D]), s.sb("be", [P, 1]), s.sb("ones3", [3, P], BF16)
        load_phase(s, [(we[:], w["we"]), (be[:], w["be"]), (ones3[:], c["onesb"][0:3])],
                   lambda: route(nc, name + "r", gate, tables, xn, "switch", rows))
        y = s.sb("y", [P, 2, CH])
        gated = s.sb("gated", [P, 2, CH])
        y_ps, g_ps = s.ps("y_ps", [P, 2, CH]), s.ps("g_ps", [P, 2, CH])
        full, y_ready, gated_done, added = s.sem("full"), s.sem("y_ready"), s.sem("gated_done"), s.sem("added")
        with nc.Block() as block:
            @block.tensor
            def _(pe):
                with nc.tensor.Fori(0, NCH // 2) as n:
                    for i in range(2):
                        cols = ds(n * 2 * CH + i * CH, CH)
                        pe.wait_ge(gated_done, n * 2 + i + 1)
                        nc.tensor.matmul(y_ps[:, i], we[:], xn[:, cols], start=True, stop=True)
                        nc.tensor.matmul(g_ps[:, i], ones3[:], rows[:, cols], start=True, stop=True).then_inc(full, 1)

            @block.scalar
            def _(act):
                with nc.scalar.Fori(0, NCH // 2) as n:
                    for i in range(2):
                        act.wait_ge(full, n * 2 + i + 1)
                        act.wait_ge(gated_done, n * 2 + i + 1)
                        nc.scalar.activation(y[:, i], y_ps[:, i], ACT.Identity, bias=be[:]).then_inc(y_ready, 1)

            @block.vector
            def _(dve):
                dve.sem_inc(gated_done, 2)
                with nc.vector.Fori(0, NCH // 2) as n:
                    for i in range(2):
                        cols = ds(n * 2 * CH + i * CH, CH)
                        dve.wait_ge(y_ready, n * 2 + i + 1)
                        nc.vector.tensor_tensor(gated[:, i], y[:, i], g_ps[:, i], ALU.mult).then_inc(gated_done, 1)
                        dve.wait_ge(gated_done, n * 2 + i + 3)
                        nc.vector.tensor_tensor(res[:, cols], res[:, cols], gated[:, i], ALU.add).then_inc(added, 1)
                        dve.wait_ge(added, n * 2 + i + 1)


def constants_experts(c):
    bf = np.dtype("bfloat16")
    c["rev"] = np.tile(np.arange(EXPERTS, 0, -1, dtype=np.float32), (P, 1)).reshape(P, 1, EXPERTS)
    i, j = np.arange(P)[:, None], np.arange(P)[None, :]
    c["tri"] = (i <= j).astype(bf)
    c["onesb"] = np.ones((P, P), bf)
    spread = np.zeros((3, EXPERTS, EXPERTS, P), np.float32)
    for e in range(EXPERTS):
        spread[:, e, e] = 1
    c["spread"] = spread.reshape(3 * EXPERTS, EXPERTS, P).astype(bf)


def layout_experts(I, t):
    t["f1_gate"] = I["L1_ffn_gate_w"].T
    t["f1_w1"], t["f1_w3"], t["f1_w2"] = I["L1_ffn_w1"], I["L1_ffn_w3"], I["L1_ffn_w2"]
    t["f2_gate"] = I["L2_ffn_router_w"].T
    t["f2_w1"], t["f2_w3"], t["f2_w2"] = I["L2_ffn_gate_w"], I["L2_ffn_up_w"], I["L2_ffn_down_w"]
    b13 = np.stack([I["L2_ffn_gate_b"], I["L2_ffn_up_b"]]).reshape(2, EXPERTS, 2, P)
    t["f2_b13"] = b13.transpose(3, 0, 1, 2)
    t["f2_b2"] = np.concatenate([I["L2_ffn_down_b"]] * 3)


def retention(nc, name, w, c, xn, res, norm):
    with ExitStack() as ctx:
        s = Scope(nc, ctx, name)
        wqk = s.sb("wqk", [P, 4, D])
        wv, wgate, wproj = s.sb("wv", [P, D]), s.sb("wgate", [P, D]), s.sb("wproj", [P, D])
        gn = s.sb("gn", [P, 2])
        rope = s.sb("rope", [P, 4, SEQ])
        decay = s.sb("decay", [P, HEADS, P])
        dq, dk = s.sb("dq", [P, 1, P]), s.sb("dk", [P, 1, P])
        dchunk = s.sb("dchunk", [P, 1])
        headmask = s.sb("headmask", [P, HEADS])
        blockmask = s.sb("blockmask", [P, 1, P])
        headmean = s.sb("headmean", [P, P])
        ident = s.sb("ident", [P, P])
        load_phase(s, [
            (wqk[:], w["wqk"]), (wv[:], w["wv"]), (wgate[:], w["wgate"]), (wproj[:], w["wproj"]), (gn[:], w["gn"]),
            (rope[:], c["ret_rope"]), (decay[:], c["ret_decay"]), (dq[:], c["ret_dq"]), (dk[:], c["ret_dk"]),
            (dchunk[:], c["ret_dchunk"]), (headmask[:], c["headmask"]), (blockmask[:], c["blockmask"]),
            (headmean[:], c["headmean"]), (ident[:], c["ident"])], norm)

        xb = s.sb("xb", [P, SEQ])
        qk = s.sb("qk", [P, 4, SEQ])
        qr, kr = s.sb("qr", [P, SEQ]), s.sb("kr", [P, SEQ])
        qdec, kdec = s.sb("qdec", [P, TPB, P]), s.sb("kdec", [P, TPB, P])
        kt = s.sb("kt", [P, TPB, P])
        v = s.sb("v", [P, TPB, P])
        kv = s.sb("kv", [P, TPB - 1, P])
        state = s.sb("state", [P, TPB, P])
        km = s.sb("km", [P, 2, SEQ])
        sd = s.sb("sd", [P, 2, TPB, P])
        gate = s.sb("gate", [P, SEQ])
        yt = s.sb("yt", [P, TPB, P])
        yf, cen, z, zg = s.sb("yf", [P, SEQ]), s.sb("cen", [P, SEQ]), s.sb("z", [P, SEQ]), s.sb("zg", [P, SEQ])
        sq = s.sb("sq", [P, SEQ])
        stat = s.sb("stat", [P, 6])
        ab = s.ps("ab", [P, 2, CH])
        st = s.ps("st", [P, 2, TPB, P])
        y_ps = s.ps("y_ps", [P, TPB, P])

        copied, ab_full, ab_done = s.sem("copied"), s.sem("ab_full"), s.sem("ab_done")
        kr_ready, roped, decayed = s.sem("kr_ready"), s.sem("roped"), s.sem("decayed")
        gate_full, gate_done = s.sem("gate_full"), s.sem("gate_done")
        kt_full, kt_copied, kv_full, kv_copied, state_step = (s.sem("kt_full"), s.sem("kt_copied"), s.sem("kv_full"),
                                                              s.sem("kv_copied"), s.sem("state_step"))
        km_ready, st_full, sd_ready, y_step, y_copied = (s.sem("km_ready"), s.sem("st_full"),
                                                                 s.sem("sd_ready"), s.sem("y_step"),
                                                         s.sem("y_copied"))
        stat_step, squared, rooted, z_ready, zg_ready = (s.sem("stat_step"), s.sem("squared"), s.sem("rooted"),
                                                                s.sem("z_ready"), s.sem("zg_ready"))
        zeroed = s.sem("zeroed")
        JOBS = 16
        V_JOB, YT_JOB, MEAN_JOB, VAR_JOB, OUT_JOB = 8, 10, 12, 13, 14
        STATS = 7
        ORDER = (2, 3, 0, 1)

        with nc.Block() as block:
            @block.tensor
            def _(pe):
                with nc.tensor.Fori(0, BATCH) as b:
                    base = b * JOBS

                    def take(k):
                        pe.wait_ge(ab_done, base + k + 1)
                        return k % 2

                    pe.wait_ge(copied, b + 1)
                    for n, i in enumerate(ORDER):
                        for ch in range(2):
                            sl = take(2 * n + ch)
                            nc.tensor.matmul(ab[:, sl], wqk[:, i], xb[:, ch * CH:ch * CH + CH], start=True,
                                             stop=True).then_inc(ab_full, 1)
                    for half in range(2):
                        sl = take(V_JOB + half)
                        for j in range(4):
                            t = half * 4 + j
                            mm = nc.tensor.matmul(ab[:, sl, j * P:j * P + P], xb[:, t * P:t * P + P], wv[:],
                                                  start=True, stop=True)
                        mm.then_inc(ab_full, 1)
                    pe.wait_ge(y_copied, b + 1)
                    for ch in range(2):
                        mm = nc.tensor.matmul(y_ps[:, 4 * ch:4 * ch + 4].rearrange("p a b -> p (a b)"), wgate[:],
                                              xb[:, ch * CH:ch * CH + CH], start=True, stop=True)
                    mm.then_inc(gate_full, 1)
                    pe.wait_ge(decayed, b * 2 + 1)
                    for t in range(TPB):
                        mm = nc.tensor.matmul(st[:, 0, t], kdec[:, t], ident[:], start=True, stop=True)
                    mm.then_inc(kt_full, 1)
                    pe.wait_ge(kt_copied, b + 1)
                    pe.wait_ge(ab_done, base + V_JOB + 2 + 2)
                    for t in range(TPB - 1):
                        mm = nc.tensor.matmul(st[:, 1, t], kt[:, t], v[:, t], start=True, stop=True)
                    mm.then_inc(kv_full, 1)

                    def from_state():
                        pe.wait_ge(decayed, b * 2 + 2)
                        pe.wait_ge(state_step, b * (TPB - 1) + TPB - 1)
                        pe.wait_ge(gate_done, b + 1)
                        for t in range(TPB):
                            nc.tensor.matmul(y_ps[:, t], qdec[:, t], state[:, t], start=t % 4 == 0, stop=False,
                                             skip_group_check=True)

                    def within(h):
                        pe.wait_ge(sd_ready, b * HEADS + h + 3)
                        for t in range(TPB):
                            mm = nc.tensor.matmul(y_ps[:, t, h * HD:h * HD + HD], sd[:, h % 2, t],
                                                  v[:, t, h * HD:h * HD + HD], start=False, stop=h == HEADS - 1,
                                                  skip_group_check=True)
                        mm.then_inc(y_step, 1)

                    pe.wait_ge(roped, b + 1)
                    for h in range(HEADS):
                        if h == 1:
                            pe.wait_ge(kv_copied, b + 1)
                        pe.wait_ge(km_ready, b * HEADS + h + 1)
                        pe.wait_ge(sd_ready, b * HEADS + h + 1)
                        for t in range(TPB):
                            mm = nc.tensor.matmul(st[:, h % 2, t], km[:, h % 2, t * P:t * P + P],
                                                  qr[:, t * P:t * P + P], start=True, stop=True)
                        mm.then_inc(st_full, 1)
                        if h == 1:
                            from_state()
                        if h:
                            within(h - 1)
                    within(HEADS - 1)
                    pe.wait_ge(y_copied, b + 2)
                    for half in range(2):
                        sl = take(YT_JOB + half)
                        for j in range(4):
                            mm = nc.tensor.matmul(ab[:, sl, j * P:j * P + P], yt[:, half * 4 + j], ident[:],
                                                  start=True, stop=True)
                        mm.then_inc(ab_full, 1)
                    pe.wait_ge(stat_step, b * STATS + 1)
                    nc.tensor.matmul(ab[:, take(MEAN_JOB), 0:1], headmean[:], stat[:, 0:1], start=True,
                                     stop=True).then_inc(ab_full, 1)
                    pe.wait_ge(squared, b + 1)
                    nc.tensor.matmul(ab[:, take(VAR_JOB), 0:1], headmean[:], stat[:, 1:2], start=True,
                                     stop=True).then_inc(ab_full, 1)
                    for ch in range(2):
                        pe.wait_ge(zg_ready, b * 2 + ch + 1)
                        sl = take(OUT_JOB + ch)
                        nc.tensor.matmul(ab[:, sl], wproj[:], zg[:, ch * CH:ch * CH + CH], start=True,
                                         stop=True).then_inc(ab_full, 1)

            @block.scalar
            def _(act):
                act.sem_inc(y_copied, 1)
                with nc.scalar.Fori(0, BATCH) as b:
                    act.wait_ge(gate_full, b + 1)
                    nc.scalar.activation(gate[:], y_ps[:].rearrange("p a b -> p (a b)"), ACT.Silu).then_inc(gate_done, 1)
                    act.wait_ge(kt_full, b + 1)
                    nc.scalar.activation(kt[:], st[:, 0], ACT.Copy).then_inc(kt_copied, 1)
                    act.wait_ge(y_step, b * HEADS + HEADS + 2)
                    nc.scalar.activation(yt[:], y_ps[:], ACT.Copy).then_inc(y_copied, 1)
                    act.wait_ge(stat_step, b * STATS + 2)
                    nc.scalar.activation(sq[:], cen[:], ACT.Square, accum_out=stat[:, 1:2]).then_inc(squared, 1)
                    act.wait_ge(stat_step, b * STATS + 3)
                    nc.scalar.activation(stat[:, 3:4], stat[:, 2:3], ACT.Sqrt).then_inc(rooted, 1)

            @block.gpsimd
            def _(pool):
                nc.gpsimd.memset(state[:], 0.0).then_inc(zeroed, 1)
                with nc.gpsimd.Fori(0, BATCH) as b:
                    pool.wait_ge(kr_ready, b + 1)
                    nc.gpsimd.tensor_tensor(kdec[:], kr[:].rearrange("p (t n) -> p t n", n=P),
                                            dk[:].broadcast_to([P, TPB, P]), ALU.mult).then_inc(decayed, 1)
                    pool.wait_ge(ab_done, b * JOBS + 8 + 2)
                    nc.gpsimd.tensor_tensor(qr[:], qk[:, 0], qk[:, 1], ALU.add).then_inc(roped, 1)
                    pool.wait_ge(roped, b + 1)
                    nc.gpsimd.tensor_tensor(qdec[:], qr[:].rearrange("p (t n) -> p t n", n=P),
                                            dq[:].broadcast_to([P, TPB, P]), ALU.mult).then_inc(decayed, 1)

            @block.vector
            def _(dve):
                dve.sem_inc(ab_done, 2)
                dve.sem_inc(sd_ready, 2)
                dve.sem_inc(y_step, 2)
                dve.wait_ge(zeroed, 1)
                with nc.vector.Fori(0, BATCH) as b:
                    base = b * JOBS
                    nc.vector.tensor_scalar(xb[:], xn[:, ds(b * SEQ, SEQ)], 1.0, None, ALU.mult).then_inc(copied, 1)
                    for n, i in enumerate(ORDER):
                        if n == 2:
                            dve.wait_ge(ab_done, base + 4 + 2)
                            nc.vector.tensor_tensor(kr[:], qk[:, 2], qk[:, 3], ALU.add).then_inc(kr_ready, 1)
                        for ch in range(2):
                            k = 2 * n + ch
                            cols = slice(ch * CH, ch * CH + CH)
                            dve.wait_ge(ab_full, base + k + 1)
                            nc.vector.tensor_tensor(qk[:, i, cols], ab[:, k % 2], rope[:, i, cols],
                                                    ALU.mult).then_inc(ab_done, 1)
                    for half in range(2):
                        k = V_JOB + half
                        dve.wait_ge(ab_full, base + k + 1)
                        nc.vector.tensor_copy(v[:, 4 * half:4 * half + 4].rearrange("p a b -> p (a b)"),
                                              ab[:, k % 2]).then_inc(ab_done, 1)
                    def mask_k(h):
                        dve.wait_ge(kr_ready, b + 1)
                        nc.vector.tensor_scalar(km[:, h % 2], kr[:], headmask[:, h:h + 1], None,
                                                ALU.mult).then_inc(km_ready, 1)

                    mask_k(0)
                    mask_k(1)
                    dve.wait_ge(kv_full, b + 1)
                    nc.vector.tensor_tensor(kv[:], st[:, 1, 0:TPB - 1], blockmask[:].broadcast_to([P, TPB - 1, P]),
                                            ALU.mult).then_inc(kv_copied, 1)
                    dve.wait_ge(kv_copied, b + 1)
                    for t in range(TPB - 1):
                        nc.vector.scalar_tensor_tensor(out=state[:, t + 1], in0=state[:, t], scalar=dchunk[:],
                                                       in1=kv[:, t], op0=ALU.mult, op1=ALU.add).then_inc(state_step, 1)
                        dve.wait_ge(state_step, b * (TPB - 1) + t + 1)

                    for h in range(HEADS):
                        dve.wait_ge(st_full, b * HEADS + h + 1)
                        dve.wait_ge(y_step, b * HEADS + h + 1)
                        nc.vector.tensor_tensor(sd[:, h % 2], st[:, h % 2],
                                                decay[:, h:h + 1].broadcast_to([P, TPB, P]),
                                                ALU.mult).then_inc(sd_ready, 1)
                        if h + 2 < HEADS:
                            mask_k(h + 2)
                    for half in range(2):
                        k = YT_JOB + half
                        dve.wait_ge(ab_full, base + k + 1)
                        nc.vector.tensor_copy(yf[:, half * CH:half * CH + CH], ab[:, k % 2]).then_inc(ab_done, 1)
                    dve.wait_ge(ab_done, base + YT_JOB + 2 + 2)
                    nc.vector.tensor_reduce(stat[:, 0:1], yf[:], AX.X, ALU.add).then_inc(stat_step, 1)
                    dve.wait_ge(ab_full, base + MEAN_JOB + 1)
                    nc.vector.tensor_scalar(cen[:], yf[:], ab[:, MEAN_JOB % 2, 0:1], None,
                                            ALU.subtract).then_inc(stat_step, 1)
                    dve.wait_ge(stat_step, b * STATS + 2)
                    dve.sem_inc(ab_done, 1)
                    dve.wait_ge(ab_full, base + VAR_JOB + 1)
                    nc.vector.tensor_scalar(stat[:, 2:3], ab[:, VAR_JOB % 2, 0:1], EPS, None,
                                            ALU.add).then_inc(stat_step, 1)
                    dve.wait_ge(stat_step, b * STATS + 3)
                    dve.sem_inc(ab_done, 1)
                    dve.wait_ge(rooted, b + 1)
                    nc.vector.reciprocal(stat[:, 4:5], stat[:, 3:4]).then_inc(stat_step, 1)
                    dve.wait_ge(stat_step, b * STATS + 4)
                    nc.vector.tensor_tensor(stat[:, 5:6], stat[:, 4:5], gn[:, 0:1], ALU.mult).then_inc(stat_step, 1)
                    dve.wait_ge(stat_step, b * STATS + 5)
                    for ch in range(2):
                        cols = slice(ch * CH, ch * CH + CH)
                        nc.vector.tensor_scalar(z[:, cols], cen[:, cols], stat[:, 5:6], gn[:, 1:2], ALU.mult,
                                                ALU.add).then_inc(z_ready, 1)
                        dve.wait_ge(z_ready, b * 2 + ch + 1)
                        nc.vector.tensor_tensor(zg[:, cols], z[:, cols], gate[:, cols], ALU.mult).then_inc(zg_ready, 1)
                    dve.sem_inc(stat_step, 2)
                    for ch in range(2):
                        k = OUT_JOB + ch
                        dve.wait_ge(ab_full, base + k + 1)
                        cols = ds(b * SEQ + ch * CH, CH)
                        nc.vector.tensor_tensor(res[:, cols], res[:, cols], ab[:, k % 2], ALU.add).then_inc(ab_done, 1)


def constants_retention(c):
    f = np.float32
    half = np.arange(0, HD, 2, dtype=f)
    inv = (1.0 / f(10000.0) ** (half / f(HD))).astype(f)
    t = np.arange(SEQ, dtype=f)
    ang = np.repeat((t[:, None] * inv[None, :]).astype(f), 2, axis=-1)
    vec = ((half + f(0.4 * HD)) / f(1.4 * HD)).astype(f)
    power = ((t - SEQ // 2) / f(512.0)).astype(f)
    scale = np.repeat((vec[None, :] ** power[:, None]).astype(f), 2, axis=-1)
    cos, sin = np.cos(ang), np.sin(ang) * np.tile(np.array([-1, 1], f), HD // 2)
    four = [cos * scale, sin * scale, cos / scale, sin / scale]
    c["ret_rope"] = np.stack([np.tile(a.T, (HEADS, 1)) for a in four], axis=1).astype(f)
    gamma = 1.0 - 2.0 ** (-5.0 - np.arange(HEADS, dtype=np.float64))
    d = np.arange(P)[None, :] - np.arange(P)[:, None]
    dec = np.where(d[:, None, :] >= 0, gamma[None, :, None] ** np.maximum(d, 0)[:, None, :], 0.0)
    c["ret_decay"] = (dec * HD ** -0.5).astype(f)
    rows = np.repeat(gamma, HD)[:, None]
    c["ret_dq"] = (rows ** (np.arange(P)[None, :] + 1) * HD ** -0.5).astype(f).reshape(P, 1, P)
    c["ret_dk"] = (rows ** (P - 1 - np.arange(P)[None, :])).astype(f).reshape(P, 1, P)
    c["ret_dchunk"] = (rows ** P).astype(f)
    head = np.arange(P) // HD
    c["headmask"] = (head[:, None] == np.arange(HEADS)[None, :]).astype(f)
    same = (head[:, None] == head[None, :]).astype(f)
    c["blockmask"] = same.reshape(P, 1, P)
    c["headmean"] = same * f(1.0 / (HD * SEQ))


def layout_retention(I, t):
    q, k, v = (I["L2_attn_w_qkv"][i * D:i * D + D].T for i in range(3))
    partner = np.arange(D) ^ 1
    t["a2_wqk"] = np.stack([q, q[:, partner], k, k[:, partner]], axis=1)
    t["a2_wv"], t["a2_wgate"], t["a2_wproj"] = v, I["L2_attn_w_gated"].T, I["L2_attn_w_proj"].T
    t["a2_gn"] = columns(I["L2_attn_gn_weight"], I["L2_attn_gn_bias"])


WH, WD, WINDOW, DEPTH = 8, 64, 64, 2
INNER = WH * WD
SPAN = WINDOW + P
FF = int(D * 4 * 2 / 3)


def shift_tokens(nc, name, src, dst):
    HALF = D // 2
    with ExitStack() as ctx:
        s = Scope(nc, ctx, name)
        moved = s.sem("moved")
        seqs = lambda t, lo, hi: t[lo:hi].rearrange("p (b n) -> p b n", b=BATCH)
        with nc.Block() as block:
            @block.vector
            def _(dve):
                nc.vector.tensor_copy(dst[0:HALF], src[0:HALF]).then_inc(moved, 1)

            @block.scalar
            def _(act):
                nc.scalar.activation(seqs(dst, HALF, D)[:, :, 1:], seqs(src, HALF, D)[:, :, :SEQ - 1],
                                     ACT.Copy).then_inc(moved, 1)

            @block.gpsimd
            def _(pool):
                nc.gpsimd.memset(seqs(dst, HALF, D)[:, :, 0:1], 0.0).then_inc(moved, 1)


def window_attention(nc, name, w, c, ht, src, dst, meanwhile):
    NB = TOK // P
    PAIRS = INNER // P
    SLOT_HEAD = [4 * (bank // 2) + 2 * col + bank % 2 for bank in range(4) for col in range(2)]
    HALVES = (1, 0)
    WS = float(8.0)
    VW = WD + 1
    with ExitStack() as ctx:
        s = Scope(nc, ctx, name)
        wqkv, wo = s.sb("wqkv", [P, 3, INNER]), s.sb("wo", [P, PAIRS, D])
        table = s.sb("table", [P, TPB, 4, WD])
        gains = s.sb("gains", [P, 1, 4, WD])
        mask = s.sb("mask", [P, TPB, SPAN], BF16)
        ident, identb = s.sb("ident", [P, P]), s.sb("identb", [P, P], BF16)
        load_phase(s, [
            (wqkv[:], w["wqkv"].rearrange("d (a n) -> d a n", a=3)), (wo[:], w["wo"].rearrange("(j p) d -> p j d", p=P)),
            (table[:], c["win_rope"]), (gains[:], w["gains"].broadcast_to([P, 4 * WD]).rearrange(
                "p (a f d) -> p a f d", a=1, f=4)), (mask[:], c["win_mask"]), (ident[:], c["ident"]),
            (identb[:], c["identb"])], meanwhile)
        hb = s.sb("hb", [P, 2, P])
        squares = s.sb("squares", [P, 2, 2 * WH, WD])
        norm2, clipped, rnorm = s.sb("norm2", [P, 2, 2 * WH]), s.sb("clipped", [P, 2, 2 * WH]), s.sb(
            "rnorm", [P, 2, 2 * WH])
        minus_half = s.sb("minus_half", [P, 2 * WH])
        rot_a, rot_b = s.sb("rot_a", [P, 2, 2, INNER]), s.sb("rot_b", [P, 2, 2, INNER])
        rot = s.sb("rot", [P, 2, 2, INNER])
        qk = s.sb("qk", [P, 2, 2, INNER])
        qt, kt = s.sb("qt", [P, 2, PAIRS, P]), s.sb("kt", [P, 2, PAIRS, SPAN])
        v, vprev = s.sb("v", [P, 2, WH, VW]), s.sb("vprev", [WINDOW, 2, WH, VW])
        top = s.sb("top", [P, 2, WH])
        less, ex = s.sb("less", [P, 2, WH, SPAN]), s.sb("ex", [P, 2, WH, SPAN])
        pt, ptprev = s.sb("pt", [P, WH, P]), s.sb("ptprev", [WINDOW, WH, P])
        inv = s.sb("inv", [P, 2, WH])
        o, ot = s.sb("o", [P, 2, INNER]), s.sb("ot", [P, 2, PAIRS, P])
        sets = s.ps("sets", [P, 2, 4, CH])

        ready = s.sem("ready")
        hb_ready, qk_full, v_full, squared, v_copied = (s.sem("hb_ready"), s.sem("qk_full"), s.sem("v_full"),
                                                        s.sem("squared"), s.sem("v_copied"))
        rotated, norm_step, norm_ready, rnorm_ready, qk_ready = (s.sem("rotated"), s.sem("norm_step"),
                                                               s.sem("norm_ready"), s.sem("rnorm_ready"),
                                                               s.sem("qk_ready"))
        t_full, qkt_copied, s_full, topped, less_ready, ex_ready = (
            s.sem("t_full"), s.sem("qkt_copied"), s.sem("s_full"), s.sem("topped"), s.sem("less_ready"),
            s.sem("ex_ready"))
        pt_full, pt_copied, o_full, inverted, o_ready, vprev_copied = (
            s.sem("pt_full"), s.sem("pt_copied"), s.sem("o_full"), s.sem("inverted"), s.sem("o_ready"),
            s.sem("vprev_copied"))
        ot_full, ot_copied, out_full, added = s.sem("ot_full"), s.sem("ot_copied"), s.sem("out_full"), s.sem("added")

        def of_block(i):
            return slice(i % TPB, i % TPB + 1) if isinstance(i, int) else ds(i % TPB, 1)

        def blocks(engine, first, body):
            first()
            with engine.Fori(0, (NB - 2) // 2) as n:
                body(n * 2, 0, 2)
                body(n * 2 + 1, 1, 2)
            body(NB - 2, 0, 1)
            body(NB - 1, 1, 0)

        with nc.Block() as block:
            @block.gpsimd
            def _(pool):
                nc.gpsimd.memset(v[:], 1.0).then_inc(ready, 1)
                nc.gpsimd.memset(vprev[:], 0.0).then_inc(ready, 1)
                nc.gpsimd.memset(kt[:], 0.0).then_inc(ready, 1)
                nc.gpsimd.memset(minus_half[:], -0.5).then_inc(ready, 1)

            @block.vector
            def _(dve):
                nc.vector.tensor_tensor(table[:], table[:], gains[:].broadcast_to([P, TPB, 4, WD]),
                                        ALU.mult).then_inc(ready, 1)

        with nc.Block() as block:
            @block.tensor
            def _(pe):
                def project_qk(i, sl):
                    pe.wait_ge(hb_ready, i + 1)
                    for j in range(2):
                        mm = nc.tensor.matmul(sets[:, sl, j], hb[:, sl], wqkv[:, j], start=True, stop=True)
                    mm.then_inc(qk_full, 1)

                def project_v(i, sl):
                    nc.tensor.matmul(sets[:, sl, 2], hb[:, sl], wqkv[:, 2], start=True, stop=True).then_inc(v_full, 1)

                def turn_qk(i, sl):
                    pe.wait_ge(qk_ready, i + 1)
                    for a in range(2):
                        for j in range(PAIRS):
                            mm = nc.tensor.transpose(sets[:, sl, a, j * P:j * P + P], qk[:, sl, a, j * P:j * P + P],
                                                     ident[:])
                    mm.then_inc(t_full, 1)

                def scores(i, sl):
                    pe.wait_ge(v_copied, i + 1)
                    pe.wait_ge(added, i + 1)
                    for half in HALVES:
                        for bank in (2 * half, 2 * half + 1):
                            nc.tensor.matmul(sets[:, sl, bank, 0:2 * SPAN].rearrange("p (a n) -> p a n", a=2),
                                             identb[:], mask[:, of_block(i)].broadcast_to([P, 2, SPAN]), start=True,
                                             stop=False, skip_group_check=True)
                        if half == HALVES[0]:
                            pe.wait_ge(qkt_copied, i * 3 + 3)
                        for u in (4 * half, 4 * half + 2, 4 * half + 1, 4 * half + 3):
                            h = SLOT_HEAD[u]
                            r = WD * (h % 2)
                            mm = nc.tensor.matmul(sets[:, sl, u // 2, u % 2 * SPAN:u % 2 * SPAN + SPAN],
                                                  qt[r:r + WD, sl, h // 2], kt[r:r + WD, sl, h // 2], start=False,
                                                  stop=True, skip_group_check=True)
                        mm.then_inc(s_full, 1)

                def turn_p(i, sl):
                    for n, half in enumerate(HALVES):
                        pe.wait_ge(ex_ready, i * 2 + n + 1)
                        for a, lo, hi in ((0, WINDOW, SPAN), (1, 0, P)):
                            for j in range(4):
                                mm = nc.tensor.transpose(sets[:, sl, 2 * half + a, j * P:j * P + P],
                                                         ex[:, sl, 4 * half + j, lo:hi], ident[:])
                        mm.then_inc(pt_full, 1)

                def values(i, sl):
                    pe.wait_ge(vprev_copied, i + 1)
                    for n, half in enumerate(HALVES):
                        pe.wait_ge(pt_copied, i * 4 + 2 * n + 2)
                        for u in range(4 * half, 4 * half + 4):
                            h = SLOT_HEAD[u]
                            out = sets[:, sl, 2 * half, h % 4 * VW:h % 4 * VW + VW]
                            nc.tensor.matmul(out, pt[:, u], v[:, sl, h], start=True, stop=False,
                                             skip_group_check=True)
                            mm = nc.tensor.matmul(out, ptprev[:, u], vprev[:, sl, h], start=False, stop=True,
                                                  skip_group_check=True)
                    mm.then_inc(o_full, 1)

                def turn_o(i, sl):
                    pe.wait_ge(o_ready, i + 1)
                    for j in range(PAIRS):
                        mm = nc.tensor.transpose(sets[:, sl, 2, j * P:j * P + P], o[:, sl, j * P:j * P + P], ident[:])
                    mm.then_inc(ot_full, 1)

                def output(i, sl):
                    pe.wait_ge(ot_copied, i + 1)
                    for j in range(PAIRS):
                        mm = nc.tensor.matmul(sets[:, sl, 3, 0:P], wo[:, j], ot[:, sl, j], start=j == 0,
                                              stop=j == PAIRS - 1)
                    mm.then_inc(out_full, 1)

                def first():
                    project_qk(0, 0)
                    project_v(0, 0)
                    turn_qk(0, 0)
                    project_qk(1, 1)
                    scores(0, 0)
                    project_v(1, 1)

                def body(i, sl, left):
                    turn_p(i, sl)
                    values(i, sl)
                    if left:
                        turn_qk(i + 1, 1 - sl)
                    turn_o(i, sl)
                    if left == 2:
                        project_qk(i + 2, sl)
                    if left:
                        scores(i + 1, 1 - sl)
                    output(i, sl)
                    if left == 2:
                        project_v(i + 2, sl)

                blocks(nc.tensor, first, body)

            @block.scalar
            def _(act):
                act.sem_inc(vprev_copied, 2)

                def square(i, sl):
                    act.wait_ge(qk_full, i + 1)
                    nc.scalar.activation(squares[:, sl].rearrange("p h d -> p (h d)"),
                                         sets[:, sl, 0:2].rearrange("p a n -> p (a n)"), ACT.Square).then_inc(squared, 1)

                def copy_v(i, sl):
                    act.wait_ge(v_full, i + 1)
                    nc.scalar.activation(v[:, sl, :, 0:WD], sets[:, sl, 2].rearrange("p (h d) -> p h d", h=WH),
                                         ACT.Copy).then_inc(v_copied, 1)

                def copy_qkt(i, sl):
                    act.wait_ge(t_full, i + 1)
                    nc.scalar.activation(qt[:, sl].rearrange("p j n -> p (j n)"), sets[:, sl, 0],
                                         ACT.Copy).then_inc(qkt_copied, 1)
                    keys = sets[:, sl, 1].rearrange("p (j n) -> p j n", j=PAIRS)
                    nc.scalar.activation(kt[:, sl, :, WINDOW:SPAN], keys, ACT.Copy).then_inc(qkt_copied, 1)
                    nc.scalar.activation(kt[:, 1 - sl, :, 0:WINDOW], keys[:, :, P - WINDOW:P],
                                         ACT.Copy).then_inc(qkt_copied, 1)

                def exponentials(i, sl, n):
                    slots = slice(4 * HALVES[n], 4 * HALVES[n] + 4)
                    act.wait_ge(less_ready, i * 2 + n + 1)
                    nc.scalar.activation(ex[:, sl, slots], less[:, sl, slots], ACT.Exp, scale=WS).then_inc(ex_ready, 1)

                def copy_pt(i, sl):
                    for n, half in enumerate(HALVES):
                        act.wait_ge(pt_full, i * 2 + n + 1)
                        for a, to in ((0, pt), (1, ptprev)):
                            nc.scalar.activation(to[:, 4 * half:4 * half + 4].rearrange("p u n -> p (u n)"),
                                                 sets[0:to.shape[0], sl, 2 * half + a], ACT.Copy).then_inc(pt_copied, 1)

                def copy_vprev(i, sl):
                    act.wait_ge(o_full, i + 1)
                    act.wait_ge(v_copied, i + 2)
                    nc.scalar.activation(vprev[:, sl], v[P - WINDOW:P, 1 - sl], ACT.Copy).then_inc(vprev_copied, 1)

                def copy_ot(i, sl):
                    act.wait_ge(ot_full, i + 1)
                    nc.scalar.activation(ot[:, sl].rearrange("p j n -> p (j n)"), sets[:, sl, 2],
                                         ACT.Copy).then_inc(ot_copied, 1)

                def first():
                    square(0, 0)
                    copy_v(0, 0)
                    copy_qkt(0, 0)
                    square(1, 1)
                    act.wait_ge(v_copied, 1)
                    nc.scalar.activation(vprev[:, 1], v[P - WINDOW:P, 0], ACT.Copy).then_inc(vprev_copied, 1)
                    exponentials(0, 0, 0)
                    copy_v(1, 1)
                    exponentials(0, 0, 1)

                def body(i, sl, left):
                    copy_pt(i, sl)
                    if left:
                        copy_qkt(i + 1, 1 - sl)
                    copy_ot(i, sl)
                    if left == 2:
                        square(i + 2, sl)
                        copy_vprev(i, sl)
                    if left:
                        exponentials(i + 1, 1 - sl, 0)
                    if left == 2:
                        copy_v(i + 2, sl)
                    if left:
                        exponentials(i + 1, 1 - sl, 1)

                blocks(nc.scalar, first, body)

            @block.gpsimd
            def _(pool):
                def inverse_norm(i, sl):
                    pool.wait_ge(norm_ready, i + 1)
                    nc.gpsimd.tensor_tensor(rnorm[:, sl], clipped[:, sl], minus_half[:], ALU.pow).then_inc(rnorm_ready, 1)

                def body(i, sl, left):
                    if left:
                        inverse_norm(i + 1, 1 - sl)

                blocks(nc.gpsimd, lambda: inverse_norm(0, 0), body)

            @block.vector
            def _(dve):
                dve.sem_inc(added, 2)

                def bring(i, sl):
                    nc.vector.tensor_scalar(hb[:, sl], ht[:, ds(i * P, P)], 1.0, None, ALU.mult).then_inc(hb_ready, 1)

                def factor(i, f, lo, hi):
                    t4 = table[:, of_block(i), f:f + 2, lo:hi].rearrange("p t f (a d) -> p (t f) a d", a=1)
                    return t4.broadcast_to([P, 2, WH, hi - lo])

                def norms(i, sl):
                    dve.wait_ge(squared, i + 1)
                    nc.vector.tensor_reduce(norm2[:, sl], squares[:, sl], AX.X, ALU.add).then_inc(norm_step, 1)
                    dve.wait_ge(norm_step, i + 1)
                    nc.vector.tensor_scalar(clipped[:, sl], norm2[:, sl], 1e-24, None, ALU.max).then_inc(norm_ready, 1)

                def rotate(i, sl):
                    proj = sets[:, sl, 0:2].rearrange("p a (h d) -> p a h d", d=WD)
                    half = WD // 2
                    nc.vector.tensor_tensor(rot_a[:, sl].rearrange("p a (h d) -> p a h d", d=WD), proj,
                                            factor(i, 0, 0, WD), ALU.mult).then_inc(rotated, 1)
                    part = rot_b[:, sl].rearrange("p a (h d) -> p a h d", d=WD)
                    nc.vector.tensor_tensor(part[:, :, :, 0:half], proj[:, :, :, half:WD], factor(i, 2, 0, half),
                                            ALU.mult).then_inc(rotated, 1)
                    nc.vector.tensor_tensor(part[:, :, :, half:WD], proj[:, :, :, 0:half], factor(i, 2, half, WD),
                                            ALU.mult).then_inc(rotated, 1)
                    dve.wait_ge(rotated, i * 4 + 3)
                    nc.vector.tensor_tensor(rot[:, sl], rot_a[:, sl], rot_b[:, sl], ALU.add).then_inc(rotated, 1)
                    dve.wait_ge(rotated, i * 4 + 4)
                    dve.wait_ge(rnorm_ready, i + 1)
                    nc.vector.tensor_tensor(qk[:, sl].rearrange("p a (h d) -> p (a h) d", d=WD),
                                            rot[:, sl].rearrange("p a (h d) -> p (a h) d", d=WD),
                                            rnorm[:, sl].rearrange("p (h a) -> p h a", a=1)
                                            .broadcast_to([P, 2 * WH, WD]), ALU.mult).then_inc(qk_ready, 1)

                def softmax_arguments(i, sl):
                    for n, half in enumerate(HALVES):
                        dve.wait_ge(s_full, i * 2 + n + 1)
                        slots = slice(4 * half, 4 * half + 4)
                        got = sets[:, sl, 2 * half:2 * half + 2, 0:2 * SPAN].rearrange("p b (c n) -> p b c n", c=2)
                        nc.vector.tensor_reduce(top[:, sl, slots].rearrange("p (b c) -> p b c", c=2), got, AX.X,
                                                ALU.max).then_inc(topped, 1)
                        dve.wait_ge(topped, i * 2 + n + 1)
                        nc.vector.tensor_tensor(less[:, sl, slots].rearrange("p (b c) n -> p b c n", c=2), got,
                                                top[:, sl, slots].rearrange("p (b c a) -> p b c a", c=2, a=1)
                                                .broadcast_to([P, 2, 2, SPAN]), ALU.subtract).then_inc(less_ready, 1)

                def normalise(i, sl):
                    dve.wait_ge(o_full, i + 1)
                    got = (sets[:, sl].rearrange("p (b x) n -> p b x n", x=2)[:, :, 0, 0:4 * VW]
                           .rearrange("p b (c n) -> p b c n", n=VW))
                    nc.vector.reciprocal(inv[:, sl].rearrange("p (b c a) -> p b c a", b=2, a=1),
                                         got[:, :, :, WD:VW]).then_inc(inverted, 1)
                    dve.wait_ge(inverted, i + 1)
                    nc.vector.tensor_tensor(o[:, sl].rearrange("p (b c n) -> p b c n", b=2, n=WD), got[:, :, :, 0:WD],
                                            inv[:, sl].rearrange("p (b c a) -> p b c a", b=2, a=1)
                                            .broadcast_to([P, 2, 4, WD]), ALU.mult).then_inc(o_ready, 1)

                def store(i, sl):
                    dve.wait_ge(out_full, i + 1)
                    cols = ds(i * P, P)
                    nc.vector.tensor_tensor(dst[:, cols], src[:, cols], sets[:, sl, 3, 0:P], ALU.add).then_inc(added, 1)

                def first():
                    bring(0, 0)
                    bring(1, 1)
                    norms(0, 0)
                    rotate(0, 0)
                    norms(1, 1)
                    softmax_arguments(0, 0)

                def body(i, sl, left):
                    if left:
                        rotate(i + 1, 1 - sl)
                    if left == 2:
                        bring(i + 2, sl)
                    normalise(i, sl)
                    if left == 2:
                        norms(i + 2, sl)
                    if left:
                        softmax_arguments(i + 1, 1 - sl)
                    store(i, sl)

                blocks(nc.vector, first, body)


def geglu(nc, name, w, hn, xf, meanwhile, total=None):
    parts = [(j * P, min(P, FF - j * P)) for j in range((FF + P - 1) // P)]
    J = len(parts)
    with ExitStack() as ctx:
        s = Scope(nc, ctx, name)
        w1, w2 = s.sb("w1", [P, 2 * FF]), s.sb("w2", [P, J, D])
        b1, b2 = s.sb("b1", [P, 2 * J]), s.sb("b2", [P, 1])
        load_phase(s, [(w1[:], w["w1"]), (w2[:], w["w2"].rearrange("(j p) d -> p j d", p=P)),
                       (b1[:], w["b1"]), (b2[:], w["b2"])], meanwhile)
        g_act, u = s.sb("g_act", [P, 2, CH]), s.sb("u", [P, 2, CH])
        a_ps, g_ps, y_ps = s.ps("a_ps", [P, 2, CH]), s.ps("g_ps", [P, 2, CH]), s.ps("y_ps", [P, 2, CH])
        full, act_done, u_ready, used, y_added, total_added = (
            s.sem("full"), s.sem("act_done"), s.sem("u_ready"), s.sem("used"), s.sem("y_added"),
            s.sem("total_added"))
        jobs = [(i, j, (i * J + j) % 2, lo, n) for i in range(2) for j, (lo, n) in enumerate(parts)]
        NJ = len(jobs)
        with nc.Block() as block:
            @block.tensor
            def _(pe):
                with nc.tensor.Fori(0, NCH // 2) as n:
                    def down(k):
                        i, j, sl, lo, m = jobs[k]
                        pe.wait_ge(u_ready, n * NJ + k + 3)
                        if j == 0:
                            pe.wait_ge(y_added, n * 2 + i + 1)
                        mm = nc.tensor.matmul(y_ps[:, i], w2[0:m, j], u[0:m, sl], start=j == 0, stop=j == J - 1)
                        mm.then_inc(used, 1)

                    for k, (i, j, sl, lo, m) in enumerate(jobs):
                        cols = ds(n * 2 * CH + i * CH, CH)
                        pe.wait_ge(u_ready, n * NJ + k + 1)
                        nc.tensor.matmul(a_ps[0:m, sl], w1[:, lo:lo + m], hn[:, cols], start=True, stop=True)
                        nc.tensor.matmul(g_ps[0:m, sl], w1[:, FF + lo:FF + lo + m], hn[:, cols], start=True,
                                         stop=True).then_inc(full, 1)
                        if k:
                            down(k - 1)
                    down(NJ - 1)

            @block.scalar
            def _(act):
                with nc.scalar.Fori(0, NCH // 2) as n:
                    for k, (i, j, sl, lo, m) in enumerate(jobs):
                        act.wait_ge(full, n * NJ + k + 1)
                        act.wait_ge(u_ready, n * NJ + k + 1)
                        nc.scalar.activation(g_act[0:m, sl], g_ps[0:m, sl], ACT.Gelu,
                                             bias=b1[0:m, J + j:J + j + 1]).then_inc(act_done, 1)

            @block.vector
            def _(dve):
                dve.sem_inc(u_ready, 2)
                dve.sem_inc(used, 2)
                dve.sem_inc(y_added, 2)
                with nc.vector.Fori(0, NCH // 2) as n:
                    for k, (i, j, sl, lo, m) in enumerate(jobs):
                        dve.wait_ge(act_done, n * NJ + k + 1)
                        dve.wait_ge(used, n * NJ + k + 1)
                        nc.vector.scalar_tensor_tensor(out=u[0:m, sl], in0=a_ps[0:m, sl], scalar=b1[0:m, j:j + 1],
                                                       in1=g_act[0:m, sl], op0=ALU.add,
                                                       op1=ALU.mult).then_inc(u_ready, 1)
                        if j == J - 1:
                            cols = ds(n * 2 * CH + i * CH, CH)
                            dve.wait_ge(used, n * NJ + k + 3)
                            nc.vector.scalar_tensor_tensor(out=xf[:, cols], in0=y_ps[:, i], scalar=b2[:],
                                                           in1=xf[:, cols], op0=ALU.add,
                                                           op1=ALU.add).then_inc(y_added, 1)
                            if total is not None:
                                dve.wait_ge(y_added, n * 2 + i + 3)
                                nc.vector.tensor_tensor(total[:, cols], total[:, cols], xf[:, cols],
                                                        ALU.add).then_inc(total_added, 1)


def local_transformer(nc, name, w, c, xn, res, norm_tables, ln):
    with ExitStack() as ctx:
        s = Scope(nc, ctx, name)
        xf, ht = s.sb("xf", [P, TOK]), s.sb("ht", [P, TOK])
        for l in range(DEPTH):
            wl = {k[1:]: v for k, v in w.items() if k[0] == str(l)}
            src = xf if l else xn

            def shift_and_norm():
                shift_tokens(nc, f"{name}t{l}", xf, ht)
                layernorm(nc, f"{name}n{l}", ht, ht, norm_tables, gain=ln[:, 2 * l:2 * l + 1],
                          shift=ln[:, 2 * l + 1:2 * l + 2])

            window_attention(nc, f"{name}w{l}", wl, c, ht, src, xf, lambda: shift_tokens(nc, f"{name}s{l}", src, ht))
            geglu(nc, f"{name}g{l}", wl, ht, xf, shift_and_norm, res if l == DEPTH - 1 else None)


def constants_local(c):
    f = np.float32
    half = np.arange(0, WD, 2, dtype=f)
    inv = (1.0 / f(10000.0) ** (half / f(WD))).astype(f)
    t = np.arange(SEQ, dtype=f)
    ang = (t[:, None] * inv[None, :]).astype(f)
    ang = np.concatenate([ang, ang], axis=-1)
    base = ((half + f(0.4 * WD)) / f(1.4 * WD)).astype(f)
    power = ((t - SEQ // 2) / f(WINDOW // 2)).astype(f)
    scale = (base[None, :].astype(np.float64) ** power[:, None]).astype(f)
    scale = np.concatenate([scale, scale], axis=-1)
    cos = np.cos(ang)
    sin = np.sin(ang) * np.concatenate([-np.ones(WD // 2, f), np.ones(WD // 2, f)])
    four = [cos * scale, cos / scale, sin * scale, sin / scale]
    c["win_rope"] = np.stack([a.reshape(TPB, P, WD).transpose(1, 0, 2) for a in four], axis=2).astype(f)
    q, k = np.arange(P)[:, None], np.arange(SPAN)[None, :] - WINDOW
    seen = (k <= q) & (k >= q - WINDOW)
    mask = np.where(seen, 0.0, -1e30)[:, None, :].repeat(TPB, axis=1)
    mask[:, 0, :WINDOW] = -1e30
    c["win_mask"] = mask.astype(np.dtype("bfloat16"))


def layout_local(I, t):
    partner = (np.arange(WD) + WD // 2) % WD
    J = (FF + P - 1) // P
    t["f0_ln"] = columns(*[I[k][l] for l in range(DEPTH) for k in ("L0_ffn_ln_g", "L0_ffn_ln_b")])
    for l in range(DEPTH):
        qs, ks = I["L0_ffn_q_scale"][l], I["L0_ffn_k_scale"][l]
        t[f"f0_{l}wqkv"], t[f"f0_{l}wo"] = I["L0_ffn_wqkv"][l], I["L0_ffn_wo"][l]
        t[f"f0_{l}gains"] = np.concatenate([qs, ks, qs[partner], ks[partner]]).reshape(1, 4 * WD)
        t[f"f0_{l}w1"] = I["L0_ffn_w1"][l]
        w2 = np.zeros((J * P, D), np.float32)
        w2[:FF] = I["L0_ffn_w2"][l]
        t[f"f0_{l}w2"] = w2
        b1 = np.zeros((2, J * P), np.float32)
        b1[:, :FF] = I["L0_ffn_b1"][l].reshape(2, FF)
        t[f"f0_{l}b1"] = b1.reshape(2 * J, P).T
        t[f"f0_{l}b2"] = I["L0_ffn_b2"][l].reshape(D, 1)


def build_program(nc, t, out):
    with ExitStack() as ctx:
        s = Scope(nc, ctx, "all")
        x = s.sb("x", [P, TOK])
        xn = s.sb("xn", [P, TOK])
        centre, collect = s.sb("centre", [P, P]), s.sb("collect", [P, NCH, NCH])
        spread, eps_col = s.sb("spread", [NCH, NCH, P]), s.sb("eps_col", [P, 1])
        norm_tables = centre, collect, spread, eps_col
        rev = s.sb("rev", [P, 1, EXPERTS])
        identb, tri, onesb = s.sb("identb", [P, P], BF16), s.sb("tri", [P, P], BF16), s.sb("onesb", [P, P], BF16)
        route_tables = rev, identb, tri, onesb
        gates = s.sb("gates", [P, 3, EXPERTS])
        ln = s.sb("ln", [P, 2 * DEPTH])
        load_phase(s, [(x[:], t["xT"]), (centre[:], t["centre"]), (collect[:], t["collect"]),
                       (spread[:], t["spread_rows"]), (eps_col[:], t["eps_col"]), (rev[:], t["rev"]),
                       (identb[:], t["identb"]), (tri[:], t["tri"]), (onesb[:], t["onesb"]),
                       (gates[:, 0], t["f1_gate"]), (gates[:, 1], t["f2_gate"]), (gates[:, 2], t["f3_wg"]),
                       (ln[:], t["f0_ln"])])

        def part(prefix):
            return {k[len(prefix):]: v for k, v in t.items() if k.startswith(prefix)}

        def norm(name):
            return lambda: layernorm(nc, name, x, xn, norm_tables)

        phases = [
            lambda: headwise_attention(nc, "a0", part("a0_"), t, xn, x, norm("ln0")),
            lambda: local_transformer(nc, "f0", part("f0_"), t, xn, x, norm_tables, ln),
            lambda: narrow_attention(nc, "a1", part("a1_"), t, xn, x, norm("ln1")),
            lambda: experts(nc, "f1", part("f1_"), t, xn, x, gates[:, 0], route_tables, biased=False),
            lambda: retention(nc, "a2", part("a2_"), t, xn, x, norm("ln2")),
            lambda: experts(nc, "f2", part("f2_"), t, xn, x, gates[:, 1], route_tables, biased=True),
            lambda: headwise_attention(nc, "a3", part("a3_"), t, xn, x, norm("ln3"), latent=True),
            lambda: switch_ffn(nc, "f3", part("f3_"), t, xn, x, gates[:, 2], route_tables),
        ]
        for phase in phases:
            phase()
        stored = s.sem("stored")
        with nc.Block() as block:
            @block.sync
            def _(sp):
                sp.dma_start(out, x[:]).then_inc(stored, 16)
                sp.wait_ge(stored, 16)


def constants():
    bf = np.dtype("bfloat16")
    f = np.float32
    c = {}
    c["centre"] = np.eye(P, dtype=f) - f(1.0 / P)
    c["collect"] = np.tile(np.eye(NCH, dtype=f) / f(P), (P, 1, 1))
    c["spread_rows"] = np.repeat(np.eye(NCH, dtype=f)[:, :, None], P, axis=2)
    c["eps_col"] = np.full((P, 1), EPS, f)
    c["ident"] = np.eye(P, dtype=f)
    c["identb"] = np.eye(P).astype(bf)
    c["ones1"] = np.ones((1, P), f)
    for key, parts in (("selq", Q_PART), ("selk", K_PART)):
        sel = np.zeros((P, QUADS, 2, 3, P), f)
        for q in range(QUADS):
            for g in range(2):
                for jj in range(2):
                    head = 4 * q + 2 * g + jj
                    for slot, l in enumerate(parts):
                        for d in range(HD):
                            sel[head * HD + d, q, g, l, 64 * jj + 8 * slot + d] = 1
        c[key] = sel.reshape(P, -1).astype(bf)
    kone = np.zeros((P, 1), f)
    for jj in range(2):
        kone[64 * jj + M_ROW:64 * jj + M_ROW + 3] = 1
    c["kone"] = kone
    sumbc = np.zeros((P, P), f)
    for j in range(4):
        sumbc[32 * j + HD, 32 * j:32 * j + 32] = 1
    c["sumbc"] = sumbc
    i, j = np.arange(P)[:, None], np.arange(P)[None, :]
    c["mask_qk"] = np.where(j > i, -1e30, 0).astype(bf)
    c["mask_kq"] = np.where(i > j, -1e30, 0).astype(bf)
    inv = (1.0 / f(10000.0) ** (np.arange(0, HD, 2, dtype=f) / f(HD))).astype(f)
    ang = (np.arange(SEQ, dtype=f)[:, None] * inv[None, :]).astype(f)
    cos, sin = np.cos(ang), np.sin(ang)
    by_block = lambda a: a.reshape(TPB, P, HD).transpose(1, 0, 2)
    c["cos8"] = by_block(np.concatenate([cos, cos], 1)).astype(f)
    c["sin8"] = by_block(np.concatenate([-sin, sin], 1)).astype(f)
    constants_experts(c)
    constants_local(c)
    constants_retention(c)
    return c


def quad_columns(wv, bias):
    k = wv.shape[0]
    out = np.zeros((k, HEADS, 32), np.float32)
    out[:, :, :HD] = wv.reshape(k, HEADS, HD)
    row = np.zeros((1, HEADS, 32), np.float32)
    if bias is not None:
        row[0, :, :HD] = bias.reshape(HEADS, HD)
    row[0, :, HD] = 1
    return out.reshape(k, -1), row.reshape(1, -1)


def quad_rows(wo, bias):
    out = np.zeros((HEADS, 32, D), np.float32)
    out[:, :HD] = wo.reshape(HEADS, HD, D)
    if bias is not None:
        out[0, HD] = bias
    return out.reshape(QUADS, P, D)


def columns(*vectors):
    out = np.zeros((P, len(vectors)), np.float32)
    for i, v in enumerate(vectors):
        out[:, i] = v
    return out


def layout(I):
    t = {"xT": I["L0_attn_x"].reshape(TOK, D).T}
    wqkv = I["L0_attn_W_qkv"].reshape(D, HEADS, 3, HD)
    bqkv = I["L0_attn_b_qkv"].reshape(HEADS, 3, HD)
    t["a0_wqkv"] = wqkv.transpose(0, 2, 1, 3).reshape(D, 3 * D)
    t["a0_bqkv"] = bqkv.transpose(1, 0, 2).reshape(1, 3 * D)
    t["a0_wo"], t["a0_bo"] = I["L0_attn_W_out"], I["L0_attn_b_out"].reshape(D, 1)

    t["a1_wq"], t["a1_wk"] = I["L1_attn_Wq"], I["L1_attn_Wk"]
    t["a1_wv"], t["a1_bv"] = quad_columns(I["L1_attn_Wv"], None)
    t["a1_wo"] = quad_rows(I["L1_attn_Wo"], None)

    wup, bup = I["L3_attn_Wup"].reshape(-1, HEADS, 2, HD), I["L3_attn_bup"].reshape(HEADS, 2, HD)
    t["a3_wqkv"] = I["L3_attn_Wq"]
    t["a3_bqkv"] = np.concatenate([I["L3_attn_bq"], bup[:, 0].reshape(-1), bup[:, 1].reshape(-1)]).reshape(1, 3 * D)
    t["a3_wdown"], t["a3_bdown"] = I["L3_attn_Wdown"], I["L3_attn_bdown"].reshape(-1, 1)
    t["a3_wup"] = wup.transpose(0, 2, 1, 3).reshape(-1, 2 * D)
    t["a3_wo"], t["a3_bo"] = I["L3_attn_Wout"], I["L3_attn_bout"].reshape(D, 1)
    layout_local(I, t)
    layout_experts(I, t)
    layout_retention(I, t)
    t["f3_wg"], t["f3_we"], t["f3_be"] = I["L3_ffn_Wg"], I["L3_ffn_We"], I["L3_ffn_be"].reshape(-1, 1)
    return t


def kernel(**inputs):
    import concourse.bacc as bacc
    from concourse.bass_utils import run_bass_kernel_spmd as run

    nc = bacc.Bacc("TRN2", target_bir_lowering=False, num_devices=1)
    arrays, views = {}, {}
    for key, a in {**constants(), **layout({k: np.asarray(v) for k, v in inputs.items()})}.items():
        a = np.ascontiguousarray(a)
        arrays[f"in_{key}"] = a
        views[key] = nc.dram_tensor(f"in_{key}", a.shape, mybir.dt.from_np(a.dtype), kind="ExternalInput").ap()
    out = nc.dram_tensor("out_x", (P, TOK), F32, kind="ExternalOutput").ap()
    build_program(nc, views, out)
    r = run(nc, [arrays], core_ids=[0])
    return r.results[0]["out_x"].T.reshape(BATCH, SEQ, D)
```
